# Optimizing a Trainium2 kernel written in Bass

```python
import numpy as np
import jax
import jax.numpy as jnp

def _softmax(x, axis=-1):
    return jax.nn.softmax(x, axis=axis)

def _gelu(x):
    return jax.nn.gelu(x, approximate=True)

def _silu(x):
    return jax.nn.silu(x)

def _sigmoid(x):
    return jax.nn.sigmoid(x)

def _layernorm(x, axis=-1, eps=1e-05):
    m = jnp.mean(x, axis=axis, keepdims=True)
    v = jnp.var(x, axis=axis, keepdims=True)
    return (x - m) / jnp.sqrt(v + eps)

def _scatter_add(tgt, idx, src, axis=0):
    return tgt.at[idx].add(src)

def _segment_sum(src, seg, n):
    return jax.ops.segment_sum(src, seg, n)
kernel_name = 'mk_adaln_d1_jaxref_r8_8630c1'

def setup_inputs(seed: int=0):
    np.random.seed(seed)
    _w = jnp.asarray

    def _L0_attn_setup():
        import jax, jax.numpy as jnp
        import numpy as np
        H = 256
        NH = 16
        HD = H // NH
        WINDOW = 128
        EPS = 1e-06
        ROPE_THETA = 10000.0

        def _rms_norm(x, w):
            var = jnp.mean(x * x, axis=-1, keepdims=True)
            return x * jax.lax.rsqrt(var + EPS) * w

        def _rope(x, offset=0):
            S = x.shape[-2]
            pos = jnp.arange(offset, offset + S, dtype=jnp.float32)
            inv_freq = 1.0 / ROPE_THETA ** (jnp.arange(0, HD, 2, dtype=jnp.float32) / HD)
            freqs = pos[:, None] * inv_freq[None, :]
            cos = jnp.cos(freqs)[None, None]
            sin = jnp.sin(freqs)[None, None]
            x1, x2 = jnp.split(x, 2, axis=-1)
            return jnp.concatenate([x1 * cos - x2 * sin, x2 * cos + x1 * sin], axis=-1)
        key = jax.random.key(seed)
        k1, k2, k3 = jax.random.split(key, 3)
        B, S = (2, 256)
        return {'hidden_states': jax.random.normal(k1, (B, S, H), dtype=jnp.float32), 'w_qkv': jax.random.normal(k2, (3 * H, H), dtype=jnp.float32) * (1.0 / np.sqrt(H)), 'q_norm_w': jnp.ones((H,), dtype=jnp.float32), 'k_norm_w': jnp.ones((H,), dtype=jnp.float32), 'w_o': jax.random.normal(k3, (H, H), dtype=jnp.float32) * (1.0 / np.sqrt(H))}
    _L0_attn_in = _L0_attn_setup()

    def _L0_ffn_setup():
        import jax, jax.numpy as jnp
        import numpy as np
        TOP_K = 2
        key = jax.random.key(seed)
        ks = jax.random.split(key, 5)
        B, T, D, E, H = (4, 256, 256, 8, 176)
        s = 1.0 / np.sqrt(D)
        sh = 1.0 / np.sqrt(H)
        return {'x': jax.random.normal(ks[0], (B, T, D), dtype=jnp.float32), 'Wg': jax.random.normal(ks[1], (E, D), dtype=jnp.float32) * s, 'W1': jax.random.normal(ks[2], (E, H, D), dtype=jnp.float32) * s, 'W2': jax.random.normal(ks[3], (E, H, D), dtype=jnp.float32) * s, 'W3': jax.random.normal(ks[4], (E, D, H), dtype=jnp.float32) * sh}
    _L0_ffn_in = _L0_ffn_setup()
    _L0_c = _w((lambda *s: np.random.randn(*s).astype(np.float32) * 0.05)(8, 256))
    _L0_wmod = _w((lambda *s: np.random.randn(*s).astype(np.float32) * 0.05)(256, 6 * 256) * 256 ** (-0.5))
    _d = {'L0_attn_hidden_states': _L0_attn_in['hidden_states'], 'L0_attn_w_qkv': _L0_attn_in['w_qkv'], 'L0_attn_q_norm_w': _L0_attn_in['q_norm_w'], 'L0_attn_k_norm_w': _L0_attn_in['k_norm_w'], 'L0_attn_w_o': _L0_attn_in['w_o'], 'L0_ffn_Wg': _L0_ffn_in['Wg'], 'L0_ffn_W1': _L0_ffn_in['W1'], 'L0_ffn_W2': _L0_ffn_in['W2'], 'L0_ffn_W3': _L0_ffn_in['W3'], 'L0_c': _L0_c, 'L0_wmod': _L0_wmod}
    _x0 = _d['L0_attn_hidden_states']
    _d['L0_attn_hidden_states'] = jax.random.normal(jax.random.fold_in(jax.random.key(seed), 1), (8, 512, 256), dtype=_x0.dtype)
    del _x0
    return _d

def reference(L0_attn_hidden_states, L0_attn_w_qkv, L0_attn_q_norm_w, L0_attn_k_norm_w, L0_attn_w_o, L0_ffn_Wg, L0_ffn_W1, L0_ffn_W2, L0_ffn_W3, L0_c, L0_wmod):

    def _L0_attn_ref(hidden_states, w_qkv, q_norm_w, k_norm_w, w_o):
        import jax, jax.numpy as jnp
        import numpy as np
        H = 256
        NH = 16
        HD = H // NH
        WINDOW = 128
        EPS = 1e-06
        ROPE_THETA = 10000.0

        def _rms_norm(x, w):
            var = jnp.mean(x * x, axis=-1, keepdims=True)
            return x * jax.lax.rsqrt(var + EPS) * w

        def _rope(x, offset=0):
            S = x.shape[-2]
            pos = jnp.arange(offset, offset + S, dtype=jnp.float32)
            inv_freq = 1.0 / ROPE_THETA ** (jnp.arange(0, HD, 2, dtype=jnp.float32) / HD)
            freqs = pos[:, None] * inv_freq[None, :]
            cos = jnp.cos(freqs)[None, None]
            sin = jnp.sin(freqs)[None, None]
            x1, x2 = jnp.split(x, 2, axis=-1)
            return jnp.concatenate([x1 * cos - x2 * sin, x2 * cos + x1 * sin], axis=-1)
        B, S, _ = hidden_states.shape
        qkv = hidden_states @ w_qkv.T
        q, k, v = jnp.split(qkv, 3, axis=-1)
        q = _rms_norm(q, q_norm_w)
        k = _rms_norm(k, k_norm_w)
        q = q.reshape(B, S, NH, HD).transpose(0, 2, 1, 3)
        k = k.reshape(B, S, NH, HD).transpose(0, 2, 1, 3)
        v = v.reshape(B, S, NH, HD).transpose(0, 2, 1, 3)
        q = _rope(q)
        k = _rope(k)
        q_idx = jnp.arange(S)[:, None]
        k_idx = jnp.arange(S)[None, :]
        mask = (q_idx >= k_idx) & (q_idx - k_idx <= WINDOW - 1)
        scale = 1.0 / np.sqrt(HD)
        scores = jnp.einsum('bhqd,bhkd->bhqk', q, k) * scale
        scores = jnp.where(mask[None, None], scores, -jnp.inf)
        probs = jax.nn.softmax(scores, axis=-1)
        out = jnp.einsum('bhqk,bhkd->bhqd', probs, v)
        out = out.transpose(0, 2, 1, 3).reshape(B, S, H)
        return out @ w_o.T

    def _L0_ffn_ref(x, Wg, W1, W2, W3):
        import jax, jax.numpy as jnp
        import numpy as np
        TOP_K = 2
        E = Wg.shape[0]
        scores = jnp.einsum('btd,ed->bte', x, Wg)
        topk_s, topk_i = jax.lax.top_k(scores, TOP_K)
        probs = jax.nn.softmax(topk_s, axis=-1)
        onehot = (topk_i[..., None] == jnp.arange(E)).astype(x.dtype)
        w = jnp.einsum('btk,btke->bte', probs, onehot)
        y = jnp.zeros_like(x)
        for e in range(E):
            h = jax.nn.silu(jnp.einsum('btd,hd->bth', x, W1[e])) * jnp.einsum('btd,hd->bth', x, W2[e])
            y = y + w[..., e:e + 1] * jnp.einsum('bth,dh->btd', h, W3[e])
        return y
    x = L0_attn_hidden_states
    mod = (_silu(L0_c) @ L0_wmod).reshape(L0_c.shape[0], 6, 1, -1)
    sa, ca, ga, sb, cb, gb = (mod[:, 0], mod[:, 1], mod[:, 2], mod[:, 3], mod[:, 4], mod[:, 5])
    ga = (2 * (ga >= 0) - 1) * jnp.maximum(jnp.abs(ga), 0.25)
    gb = (2 * (gb >= 0) - 1) * jnp.maximum(jnp.abs(gb), 0.25)
    h = _layernorm(x, axis=-1) * (1 + ca) + sa
    x = x + ga * _L0_attn_ref(h, L0_attn_w_qkv, L0_attn_q_norm_w, L0_attn_k_norm_w, L0_attn_w_o)
    h = _layernorm(x, axis=-1) * (1 + cb) + sb
    x = x + gb * _L0_ffn_ref(h, L0_ffn_Wg, L0_ffn_W1, L0_ffn_W2, L0_ffn_W3)
    return x

_drawn_inputs = setup_inputs


def setup_inputs(seed=0):
    import zlib

    import numpy as np

    out = dict(_drawn_inputs(seed))
    spreads = {'L0_attn_q_norm_w': (1.0, 0.6), 'L0_attn_k_norm_w': (1.0, 0.6)}
    factors = {}
    for name, (base, spread) in spreads.items():
        noise = np.random.default_rng([zlib.crc32(name.encode()), seed]).standard_normal(out[name].shape)
        drawn = base * np.exp(spread * noise) if base else spread * noise
        out[name] = jnp.asarray(drawn.astype(out[name].dtype))
    for name, factor in factors.items():
        out[name] = (out[name] * factor).astype(out[name].dtype)
    return out
```

```python
from contextlib import ExitStack

import numpy as np

import concourse.bass as bass
from concourse import mybir

F32 = mybir.dt.float32
F32R = mybir.dt.float32r
BF16 = mybir.dt.bfloat16
F16 = mybir.dt.float16
ACT = mybir.ActivationFunctionType
ALU = mybir.AluOpType
AX_X = mybir.AxisListType.X

P = 128
B, S, D = 8, 512, 256
T = S // P
KD = D // P
NH, HD = 16, 16
WINDOW = 128
E, HID = 8, 176
FH = E * HID
NC = FH // P
HALVES = 2
HH = NH // HALVES
PAIRS = HH // 2
G = 2
UNITS = G * T
V3 = 3 * HD + 1
RING = 3
HOOKS = NC + 1
PV_LAG = 2
ON_POOL = (0, 2, 4, 6)
ATT_STEPS = 21
WCOLS = 2 * FH * KD
W3COLS = NC * D
PIECE = (WCOLS + W3COLS) // HOOKS
LN_EPS, RMS_EPS = 1e-5, 1e-6
BIG = 1e30


def ring_jobs():
    jobs = [("ln", 0, k) for k in range(KD)]
    for t in range(T):
        jobs += [("qk", t), ("v", t)]
    for half in range(HALVES):
        for t in range(T):
            jobs += [("qT", half, t), ("kT", half, t)]
        jobs += [("max", half, t, u) for t in range(T) for u in range(2 * G)]
        jobs += [("mT", half)]
        for n in range(UNITS + PV_LAG):
            if n < UNITS:
                jobs += [("st", half, n, a) for a in range(2)]
            if n >= PV_LAG:
                jobs += [("pv", half, n - PV_LAG)]
    for t in range(T):
        jobs += [("oT", t)]
        if t >= 1:
            jobs += [("op", t - 1)]
    jobs += [("op", T - 1)]
    jobs += [("ln", 1, k) for k in range(KD)]
    jobs += [("lg",), ("lgT",), ("wT",)]
    return jobs


JOBS = ring_jobs()
JOB = {job: n for n, job in enumerate(JOBS)}


class Row:

    def __init__(self, base, shift=0):
        self.base, self.shift = base, shift

    def before(self):
        return Row(self.base, self.shift - 1)

    def index(self):
        return self.base + self.shift

    def exists(self):
        return not isinstance(self.base, int) or self.base + self.shift >= 0


class Event:

    def __init__(self, sem, per_row, step=1, ahead=0):
        self.sem, self.per_row, self.step, self.ahead = sem, per_row, step, ahead

    def grant(self, eng):
        eng.sem_inc(self.sem, self.per_row)

    def at(self, row, k):
        more = ((row.shift + self.ahead) * self.per_row + k + 1) * self.step
        return row.base * (self.per_row * self.step) + more


def last_on(ring, slot, count):
    return max(n for n in range(count) if n % ring == slot)


def build(nc, x, w_qkv_t, q_norm, k_norm, w_o_t, w_g_t, w_ffn, c_t, w_mod, rope, gates, out):
    ctx = ExitStack()
    with ctx:
        def sb(name, shape, dt=F32):
            return ctx.enter_context(nc.sbuf_tensor(name, shape, dt))

        def psum(name):
            return ctx.enter_context(nc.psum_tensor(name, [P, 512], F32))

        def sem(name):
            return ctx.enter_context(nc.semaphore(name))

        def event(name, per_row, step=1, ahead=0):
            return Event(sem(name), per_row, step, ahead)

        w_hi = sb("w_hi", [P, WCOLS + W3COLS], F32R)
        w12_lo = sb("w12_lo", [P, WCOLS], BF16)
        w3_lo = sb("w3_lo", [P, W3COLS], F32R)
        wqkv = sb("wqkv", [P, 2, KD, 3 * D], F32R)
        wo = sb("wo", [P, 2, KD, D], F32R)
        wg = sb("wg", [P, 2, KD, E], F32R)
        wg_raw = sb("wg_raw", [P, KD, E])
        ident = sb("ident", [P, P])
        band = sb("band", [P, 2 * P])
        expert_rows = sb("expert_rows", [2 * E, E, HID], F32R)
        earlier = sb("earlier", [P, E, E])
        minus_half = sb("minus_half", [P, T, 2])
        cos = sb("cos", [P, T, HD // 2])
        sin = sb("sin", [P, T, HD // 2])
        norm_w = sb("norm_w", [P, 2 * D])
        ct = sb("ct", [P, KD, B])
        ct_tmp = sb("ct_tmp", [P, KD, B])
        cmod = sb("cmod", [P, 4, KD, B])
        x_sb = sb("x_sb", [P, T, D])
        xn = sb("xn", [P, T, D])
        x1 = sb("x1", [P, T, D])
        ga = sb("ga", [P, D])
        gb = sb("gb", [P, D])
        stats = sb("stats", [P, T, 6])
        moments = sb("moments", [P, T, 2])
        variance = sb("variance", [P, T])
        rstd = sb("rstd", [P, T])
        h_f32 = sb("h_f32", [P, S])
        h1 = sb("h1", [P, 2, KD, S], F32R)
        h2 = sb("h2", [P, 2, KD, S], F32R)
        h2_bf = sb("h2_bf", [P, KD, S], BF16)
        square = sb("square", [P, 2, D])
        sumsq = sb("sumsq", [P, T, 2])
        meansq = sb("meansq", [P, T, 2])
        qk_rstd = sb("qk_rstd", [P, T, 2])
        weighted = sb("weighted", [P, 2, 2 * D])
        by_sin = sb("by_sin", [P, 2, 2 * D])
        rot = sb("rot", [P, T, 2 * D])
        q_parts = sb("q_parts", [P, 2, HH, 64], F32R)
        k_parts = sb("k_parts", [P, 2, HH, 64], F32R)
        q_t = sb("q_t", [P, PAIRS, S], F32R)
        k_t = sb("k_t", [P, PAIRS, S], F32R)
        v_parts = sb("v_parts", [P, T, NH, V3], BF16)
        v_rest = sb("v_rest", [P, 2, NH, HD])
        row_max = sb("row_max", [P, T, HH])
        neg_max_t = sb("neg_max_t", [HH, S], F32R)
        probs = sb("probs", [P, 2, 4, 2 * P])
        p_hi = sb("p_hi", [P, 3, 4, 2 * P], F16)
        p_lo = sb("p_lo", [P, 3, 4, 2 * P], F16)
        pv_sum = sb("pv_sum", [P, 2, 4, HD])
        pv_rden = sb("pv_rden", [P, 2, 4])
        attn = sb("attn", [P, T, NH, HD])
        attn_t = sb("attn_t", [P, 2, 2, KD, P], F32R)
        gated_proj = sb("gated_proj", [P, 2, D])
        logits_t = sb("logits_t", [E, S])
        logits = sb("logits", [P, T, E])
        top1 = sb("top1", [P, T])
        shifted = sb("shifted", [P, T, E])
        exps = sb("exps", [P, T, E])
        beats = sb("beats", [P, T, E, E])
        ties = sb("ties", [P, T, E, E])
        rank = sb("rank", [P, T, E])
        route_sum = sb("route_sum", [P, T])
        route = sb("route", [P, T, E])
        route_parts = sb("route_parts", [P, T, 2, E], F32R)
        route_t = sb("route_t", [2 * E, S], F32R)
        gated = sb("gated", [P, 3, S])
        g_hi = sb("g_hi", [P, 2, S], F32R)
        g_lo = sb("g_lo", [P, 2, S], F32R)
        y_gated = sb("y_gated", [P, 2, D])

        raw_qkv = rot.rearrange("p t c -> p (t c)")[:, 0:KD * 3 * D].rearrange("p (k c) -> p k c", k=KD)
        raw_o = attn.rearrange("p t h d -> p (t h d)")[:, 0:KD * D].rearrange("p (k c) -> p k c", k=KD)
        raw_ffn = gated.rearrange("p r c -> p (r c)")
        raw_mod = [gated.rearrange("p r c -> p (r c)"),
                   probs.rearrange("p r h c -> p (r h c)")[:, 0:6 * D]]

        flat = xn.rearrange("p t c -> p (t c)")
        gate_rows = [h_f32[0:B, :], flat[0:B, 0:2 * D], flat[0:B, 2 * D:4 * D]]

        ring = [psum(f"ring{n}") for n in range(RING)]
        ps_a, ps_b, ps_w = psum("ps_a"), psum("ps_b"), psum("ps_w")
        ps_y = [psum("ps_y0"), psum("ps_y1")]

        mod_loaded = sem("mod_loaded")
        consts_loaded = sem("consts_loaded")
        w_loaded = sem("w_loaded")
        constants = sem("constants")
        pool_step = sem("pool_step")
        silu_exp = sem("silu_exp")
        start_step = sem("start_step")
        silu_done = sem("silu_done")
        mod_full = sem("mod_full")
        mod_out = sem("mod_out")
        weights_split = sem("weights_split")
        gates_stored = sem("gates_stored")
        piece_loaded = [sem("piece_loaded0"), sem("piece_loaded1")]
        piece_hi = sem("piece_hi")
        piece_lo = sem("piece_lo")

        x_loaded = event("x_loaded", 2, 16)
        gb_loaded = event("gb_loaded", 1, 16)
        max_rows_set = event("max_rows_set", 4, 16)
        stored = event("stored", 1, 16)
        ring_full = event("ring_full", len(JOBS))
        stats_ready = event("stats_ready", 2)
        var_ready = event("var_ready", 3)
        rstd_ready = event("rstd_ready", 3)
        normed = event("normed", 2)
        modulated = event("modulated", 2 * KD)
        h_split = event("h_split", 2 * KD)
        squares = event("squares", T)
        qk_weighted = event("qk_weighted", T)
        sin_done = event("sin_done", T)
        rotated = event("rotated", T)
        v_hi = event("v_hi", T)
        v_sub = event("v_sub", T)
        v_mid = event("v_mid", T)
        v_done = event("v_done", T)
        qk_hi = event("qk_hi", HALVES * T)
        qk_lo = event("qk_lo", HALVES * T)
        q_t_out = event("q_t_out", HALVES * T)
        k_t_out = event("k_t_out", HALVES * T)
        maxed = event("maxed", HALVES * T * 2 * G)
        max_t_out = event("max_t_out", HALVES)
        exped = event("exped", HALVES * UNITS * 2)
        masked = event("masked", HALVES * UNITS)
        p_hi_out = event("p_hi_out", HALVES * UNITS)
        p_lo_pool = event("p_lo_pool", HALVES * len(ON_POOL))
        p_lo_dve = event("p_lo_dve", HALVES * (UNITS - len(ON_POOL)))
        pv_read = event("pv_read", HALVES * UNITS)
        attn_out = event("attn_out", HALVES * UNITS)
        attn_t_hi = event("attn_t_hi", T)
        attn_t_lo = event("attn_t_lo", T)
        proj_read = event("proj_read", T)
        resid = event("resid", T)
        logits_t_out = event("logits_t_out", 1)
        logits_out = event("logits_out", 1)
        shifted_out = event("shifted_out", 1)
        exps_out = event("exps_out", 1)
        route_out = event("route_out", 1)
        route_t_out = event("route_t_out", 1)
        ffn_full = event("ffn_full", 3 * NC)
        y_done = event("y_done", NC, ahead=1)
        tanh_out = event("tanh_out", NC)
        a_read = event("a_read", NC, ahead=1)
        b_read = event("b_read", NC, ahead=1)
        w_read = event("w_read", NC, ahead=1)
        g_hi_out = event("g_hi_out", NC)
        g_lo_out = event("g_lo_out", NC, ahead=1)
        y_read = event("y_read", 2, ahead=1)
        final = event("final", 2)
        att_step = event("att_step", ATT_STEPS)

        def p_lo_wait(eng, row, unit):
            half, n = divmod(unit, UNITS)
            if n in ON_POOL:
                eng.wait_ge(p_lo_pool.sem, p_lo_pool.at(row, half * len(ON_POOL) + ON_POOL.index(n)))
            else:
                on_dve = [m for m in range(UNITS) if m not in ON_POOL]
                eng.wait_ge(p_lo_dve.sem, p_lo_dve.at(row, half * len(on_dve) + on_dve.index(n)))

        def bank(job):
            return ring[JOB[job] % RING]

        def bank_free(eng, row, job):
            n = JOB[job]
            if n >= RING:
                n -= RING
            else:
                row, n = row.before(), last_on(RING, n, len(JOBS))
            if not row.exists():
                return
            kind, *at = JOBS[n]
            if kind == "ln":
                eng.wait_ge(modulated.sem, modulated.at(row, at[0] * KD + at[1]))
            if kind == "qk":
                eng.wait_ge(qk_weighted.sem, qk_weighted.at(row, at[0]))
            if kind == "v":
                eng.wait_ge(v_sub.sem, v_sub.at(row, at[0]))
            if kind == "qT":
                eng.wait_ge(q_t_out.sem, q_t_out.at(row, at[0] * T + at[1]))
            if kind == "kT":
                eng.wait_ge(k_t_out.sem, k_t_out.at(row, at[0] * T + at[1]))
            if kind == "max":
                eng.wait_ge(maxed.sem, maxed.at(row, (at[0] * T + at[1]) * 2 * G + at[2]))
            if kind == "mT":
                eng.wait_ge(max_t_out.sem, max_t_out.at(row, at[0]))
            if kind == "st":
                eng.wait_ge(exped.sem, exped.at(row, (at[0] * UNITS + at[1]) * 2 + at[2]))
            if kind == "pv":
                eng.wait_ge(pv_read.sem, pv_read.at(row, at[0] * UNITS + at[1]))
            if kind == "oT":
                eng.wait_ge(attn_t_lo.sem, attn_t_lo.at(row, at[0]))
            if kind == "op":
                eng.wait_ge(proj_read.sem, proj_read.at(row, at[0]))
            if kind == "lg":
                eng.wait_ge(logits_t_out.sem, logits_t_out.at(row, 0))
            if kind == "lgT":
                eng.wait_ge(logits_out.sem, logits_out.at(row, 0))
            if kind == "wT":
                eng.wait_ge(route_t_out.sem, route_t_out.at(row, 0))

        def queries(n):
            return 2 * P if n % T < T - 1 else P

        def heads(qk):
            return qk.rearrange("p (h d) -> p h d", d=HD // 2)

        def y_before(eng, f, m):
            if m >= 2:
                eng.wait_ge(y_done.sem, y_done.at(f, m - 2))
            else:
                eng.wait_ge(y_done.sem, y_done.at(f.before(), last_on(2, m, NC)))

        def low_probs(eng, row, unit, done):
            nq = queries(unit)
            eng.wait_ge(p_hi_out.sem, p_hi_out.at(row, unit))
            eng.tensor_tensor(p_lo[:, unit % 3, :, 0:nq], probs[:, unit % 2, :, 0:nq], p_hi[:, unit % 3, :, 0:nq],
                              ALU.subtract).then_inc(done.sem, 1)

        def one_row(row):
            b = row.index()
            return slice(b, b + 1) if isinstance(b, int) else bass.ds(b, 1)

        block = ctx.enter_context(nc.Block())

        @block.sync
        def _(sp):
            sp.dma_start(ct[:, :, :], c_t).then_inc(mod_loaded, 16)
            for k in range(KD):
                sp.dma_start(raw_mod[k], w_mod[k]).then_inc(mod_loaded, 16)
            sp.dma_start(x_sb[:, :, :], x[0]).then_inc(x_loaded.sem, 16)
            sp.dma_start(raw_qkv, w_qkv_t).then_inc(w_loaded, 16)
            sp.dma_start(raw_o, w_o_t).then_inc(w_loaded, 16)
            sp.dma_start(wg_raw[:, :, :], w_g_t).then_inc(w_loaded, 16)
            sp.dma_start(cos[:, :, :], rope[0]).then_inc(consts_loaded, 16)
            sp.dma_start(sin[:, :, :], rope[1]).then_inc(consts_loaded, 16)
            sp.dma_start(norm_w[:, 0:D], q_norm.broadcast_to((P, D))).then_inc(consts_loaded, 16)
            sp.dma_start(norm_w[:, D:2 * D], k_norm.broadcast_to((P, D))).then_inc(consts_loaded, 16)
            sp.wait_ge(mod_out, 2)
            sp.dma_start(gates[:, :], gate_rows[0]).then_inc(gates_stored, 16)
            sp.wait_ge(gates_stored, 16)
            sp.dma_start(ga[:, :], gates[0:1, 0:D].broadcast_to((P, D))).then_inc(x_loaded.sem, 16)

            def store(prev):
                sp.wait_ge(final.sem, final.at(prev, 1))
                sp.nop(nofuse=True)
                sp.dma_start(out[prev.index()], x1[:, :, :]).then_inc(stored.sem, 16)

            def attention(row):
                for half in range(HALVES):
                    sp.wait_ge(max_t_out.sem, max_t_out.at(row, half))
                    for a in range(2):
                        sp.dma_start(q_t[64 * a + 3 * HD:64 * a + 3 * HD + 1, :, :].bitcast(F32),
                                     neg_max_t[PAIRS * a:PAIRS * a + PAIRS, :].bitcast(F32)).then_inc(max_rows_set.sem, 16)
                if row.before().exists():
                    store(row.before())
                    sp.wait_ge(y_read.sem, y_read.at(row.before(), 1))
                    sp.nop(nofuse=True)
                sp.dma_start(gb[:, :], gates[one_row(row), D:2 * D].broadcast_to((P, D))).then_inc(gb_loaded.sem, 16)

            attention(Row(0))
            with sp.Fori(0, B - 1) as r:
                row = Row(r, 1)
                sp.wait_ge(resid.sem, resid.at(row.before(), T - 1))
                sp.nop(nofuse=True)
                sp.dma_start(x_sb[:, :, :], x[row.index()]).then_inc(x_loaded.sem, 16)
                sp.dma_start(ga[:, :], gates[one_row(row), 0:D].broadcast_to((P, D))).then_inc(x_loaded.sem, 16)
                attention(row)
            store(Row(B - 1))
            sp.wait_ge(stored.sem, stored.at(Row(B - 1), 0))

        @block.gpsimd
        def _(pool):
            steps = 0

            def step(instruction):
                nonlocal steps
                steps += 1
                instruction.then_inc(pool_step, 1)

            step(pool.memset(ident[:, :], 0.0))
            step(pool.memset(band[:, :], 0.0))
            step(pool.memset(earlier[:, :, :], 1.0))
            step(pool.memset(expert_rows[:, :, :].bitcast(F32), 0.0))
            step(pool.memset(minus_half[:, :, :], -0.5))
            pool.wait_ge(pool_step, steps)
            step(pool.affine_select(out=ident[:, :], in_=ident[:, :], compare_op=ALU.not_equal, fill=1.0,
                                    base=0, pattern=[[-1, P]], channel_multiplier=1))
            step(pool.affine_select(out=band[:, 0:P], in_=band[:, 0:P], compare_op=ALU.is_gt, fill=-BIG,
                                    base=0, pattern=[[1, P]], channel_multiplier=-1))
            step(pool.affine_select(out=band[:, P:2 * P], in_=band[:, P:2 * P], compare_op=ALU.is_ge, fill=-BIG,
                                    base=0, pattern=[[-1, P]], channel_multiplier=1))
            step(pool.affine_select(out=earlier[:, :, :], in_=earlier[:, :, :], compare_op=ALU.is_gt, fill=0.0,
                                    base=0, pattern=[[1, E], [-1, E]], channel_multiplier=0))
            for part in range(2):
                step(pool.affine_select(out=expert_rows[:, :, :], in_=expert_rows[:, :, :].bitcast(F32),
                                        compare_op=ALU.not_equal, fill=0.5, base=-E * part,
                                        pattern=[[-1, E], [0, HID]], channel_multiplier=1))
                pool.wait_ge(pool_step, steps)
            pool.sem_inc(constants, 1)

            def layer_norm(row, which):
                pool.wait_ge(stats_ready.sem, stats_ready.at(row, which))
                pool.nop(nofuse=True)
                pool.tensor_scalar(variance[:, :], moments[:, :, 1], LN_EPS, None, ALU.add).then_inc(var_ready.sem, 1)
                pool.wait_ge(var_ready.sem, var_ready.at(row, 2 * which))
                pool.tensor_tensor(rstd[:, :], variance[:, :], minus_half[:, :, 0], ALU.pow).then_inc(rstd_ready.sem, 1)

            def attention(row, hook):
                layer_norm(row, 0)
                for t in range(T):
                    pool.wait_ge(qk_weighted.sem, qk_weighted.at(row, t))
                    if t >= 2:
                        pool.wait_ge(rotated.sem, rotated.at(row, t - 2))
                    pool.tensor_tensor(
                        heads(by_sin[:, t % 2, :]), heads(weighted[:, t % 2, :]),
                        sin[:, t, :].unsqueeze(1).broadcast_to((P, 4 * NH, HD // 2)), ALU.mult).then_inc(sin_done.sem, 1)
                    pool.wait_ge(v_mid.sem, v_mid.at(row, t))
                    pool.tensor_tensor(v_parts[:, t, :, 2 * HD:3 * HD], v_rest[:, t % 2, :, :],
                                       v_parts[:, t, :, HD:2 * HD], ALU.subtract).then_inc(v_done.sem, 1)
                    if t % 2:
                        hook(t // 2)
                pool.wait_ge(squares.sem, squares.at(row, T - 1))
                pool.nop(nofuse=True)
                pool.tensor_scalar(meansq[:, :, :], sumsq[:, :, :], 1.0 / D, RMS_EPS, ALU.mult, ALU.add)\
                    .then_inc(var_ready.sem, 1)
                pool.wait_ge(var_ready.sem, var_ready.at(row, 1))
                pool.tensor_tensor(qk_rstd[:, :, :], meansq[:, :, :], minus_half[:, :, :], ALU.pow)\
                    .then_inc(rstd_ready.sem, 1)
                for half in range(HALVES):
                    hook(2 + 5 * half)
                    hook(3 + 5 * half)
                    hook(4 + 5 * half)
                    for n in range(UNITS + 1):
                        if n < UNITS:
                            unit, nq = half * UNITS + n, queries(n)
                            pool.wait_ge(exped.sem, exped.at(row, 2 * unit + 1))
                            pool.nop(nofuse=True)
                            own = probs[:, unit % 2, :, 0:P]
                            ins = pool.affine_select(out=own, in_=own, compare_op=ALU.is_ge, fill=0.0, base=0,
                                                     pattern=[[0, 4], [1, P]], channel_multiplier=-1)
                            if nq > P:
                                late = probs[:, unit % 2, :, P:2 * P]
                                ins = pool.affine_select(out=late, in_=late, compare_op=ALU.is_gt, fill=0.0, base=0,
                                                         pattern=[[0, 4], [-1, P]], channel_multiplier=1)
                            ins.then_inc(masked.sem, 1)
                        if n >= 1 and n - 1 in ON_POOL:
                            low_probs(pool, row, half * UNITS + n - 1, p_lo_pool)
                        if n == 2:
                            hook(5 + 5 * half)
                        if n == 5:
                            hook(6 + 5 * half)
                layer_norm(row, 1)

            def split_piece(n):
                pool.wait_ge(piece_hi, n + 1)
                a, z = n * PIECE, (n + 1) * PIECE
                low = w12_lo[:, a:z] if z <= WCOLS else w3_lo[:, a - WCOLS:z - WCOLS]
                pool.tensor_tensor(low, raw_ffn[:, n % 2 * PIECE:(n % 2 + 1) * PIECE], w_hi[:, a:z].bitcast(F32),
                                   ALU.subtract).then_inc(piece_lo, 1)

            def experts(f, c):
                if c >= 1:
                    m = c - 1
                    pool.wait_ge(g_hi_out.sem, g_hi_out.at(f, m))
                    y_before(pool, f, m)
                    pool.tensor_tensor(g_lo[:, m % 2, :], gated[:, m % 3, :], g_hi[:, m % 2, :].bitcast(F32),
                                       ALU.subtract).then_inc(g_lo_out.sem, 1)

            attention(Row(0), split_piece)
            g_lo_out.grant(pool)
            with pool.Fori(0, B - 1) as r:
                attention(Row(r, 1), lambda c: experts(Row(r, 0), c))
            for c in range(HOOKS):
                experts(Row(B - 1), c)


        @block.scalar
        def _(act):
            act.wait_ge(mod_loaded, 16 * (1 + KD))
            act.activation(ct_tmp[:, :, :], ct[:, :, :], ACT.Exp, scale=-1.0).then_inc(silu_exp, 1)

            def load_piece(n):
                act.dma_start(raw_ffn[:, n % 2 * PIECE:(n % 2 + 1) * PIECE], w_ffn[:, n * PIECE:(n + 1) * PIECE])\
                    .then_inc(piece_loaded[n % 2], 16)

            act.wait_ge(mod_full, 1)
            for n in range(2):
                load_piece(n)

            def modulate(row, which):
                for k in range(KD):
                    act.wait_ge(ring_full.sem, ring_full.at(row, JOB[("ln", which, k)]))
                    if k >= 1:
                        act.wait_ge(h_split.sem, h_split.at(row, which * KD + k - 1))
                    b = one_row(row)
                    act.activation(h_f32[:, :], bank(("ln", which, k))[:, :], ACT.Identity,
                                   scale=cmod[:, 2 * which, k, b], bias=cmod[:, 2 * which + 1, k, b])\
                        .then_inc(modulated.sem, 1)

            def v_middle(row, t):
                act.wait_ge(v_sub.sem, v_sub.at(row, t))
                act.activation(v_parts[:, t, :, HD:2 * HD], v_rest[:, t % 2, :, :], ACT.Copy).then_inc(v_mid.sem, 1)

            def attention(row, hook):
                modulate(row, 0)
                for t in range(T):
                    act.wait_ge(ring_full.sem, ring_full.at(row, JOB[("qk", t)]))
                    for s in range(2):
                        ins = act.activation(square[:, s, :], bank(("qk", t))[:, s * D:(s + 1) * D], ACT.Square,
                                             accum_out=sumsq[:, t, s:s + 1])
                    ins.then_inc(squares.sem, 1)
                    act.wait_ge(ring_full.sem, ring_full.at(row, JOB[("v", t)]))
                    act.activation(v_parts[:, t, :, 0:HD],
                                   bank(("v", t))[:, 0:D].rearrange("p (h d) -> p h d", d=HD), ACT.Copy)\
                        .then_inc(v_hi.sem, 1)
                    v_middle(row, t)
                    if t % 2:
                        hook(t // 2)
                act.wait_ge(rstd_ready.sem, rstd_ready.at(row, 1))
                for half in range(HALVES):
                    for t in range(T + 1):
                        if t < T:
                            high_qk(row, half, t)
                        if t >= 1:
                            transposed_out(row, half, t - 1)
                    hook(2 + 5 * half)
                    hook(3 + 5 * half)
                    act.wait_ge(ring_full.sem, ring_full.at(row, JOB[("mT", half)]))
                    act.activation(neg_max_t[:, :], bank(("mT", half))[0:HH, :], ACT.Copy, scale=-1.0)\
                        .then_inc(max_t_out.sem, 1)
                    hook(4 + 5 * half)
                    for n in range(UNITS + 1):
                        if n < UNITS:
                            exp_unit(row, half, n)
                        if n >= 1:
                            high_probs(row, half * UNITS + n - 1)
                        if n == 2:
                            hook(5 + 5 * half)
                        if n == 5:
                            hook(6 + 5 * half)
                for t in range(T):
                    act.wait_ge(ring_full.sem, ring_full.at(row, JOB[("oT", t)]))
                    act.activation(attn_t[:, t % 2, 0, :, :],
                                   bank(("oT", t))[:, 0:D].rearrange("p (k c) -> p k c", k=KD), ACT.Copy)\
                        .then_inc(attn_t_hi.sem, 1)
                modulate(row, 1)
                act.wait_ge(ring_full.sem, ring_full.at(row, JOB[("lg",)]))
                act.activation(logits_t[:, :], bank(("lg",))[0:E, :], ACT.Copy).then_inc(logits_t_out.sem, 1)
                act.wait_ge(shifted_out.sem, shifted_out.at(row, 0))
                act.activation(exps[:, :, :], shifted[:, :, :], ACT.Exp).then_inc(exps_out.sem, 1)
                act.wait_ge(ring_full.sem, ring_full.at(row, JOB[("wT",)]))
                act.activation(route_t[:, :], bank(("wT",))[0:2 * E, :], ACT.Copy).then_inc(route_t_out.sem, 1)

            def high_qk(row, half, t):
                slot, c = (half * T + t) % 2, half * HH * HD
                act.wait_ge(rotated.sem, rotated.at(row, t))
                if half * T + t >= 2:
                    act.wait_ge(ring_full.sem, ring_full.at(row, JOB[("kT", *divmod(half * T + t - 2, T))]))
                for s, dst in ((0, q_parts[:, slot, :, 0:2 * HD].rearrange("p h (r d) -> p h r d", r=2)),
                               (1, k_parts[:, slot, :, :].rearrange("p h (r d) -> p h r d", d=HD)[:, :, 0:3:2, :])):
                    src = rot[:, t, s * D + c:s * D + c + HH * HD].rearrange("p (h d) -> p h d", d=HD)
                    ins = act.activation(dst, src.unsqueeze(2).broadcast_to((P, HH, 2, HD)), ACT.Copy,
                                         scale=qk_rstd[:, t, s:s + 1])
                ins.then_inc(qk_hi.sem, 1)

            def transposed_out(row, half, t):
                for job, dst, done in (("qT", q_t, q_t_out), ("kT", k_t, k_t_out)):
                    act.wait_ge(ring_full.sem, ring_full.at(row, JOB[(job, half, t)]))
                    act.activation(dst[:, :, t * P:(t + 1) * P],
                                   bank((job, half, t))[:, :].rearrange("p (a c) -> p a c", a=PAIRS), ACT.Copy)\
                        .then_inc(done.sem, 1)

            def exp_unit(row, half, n):
                unit, nq = half * UNITS + n, queries(n)
                for a in range(2):
                    act.wait_ge(ring_full.sem, ring_full.at(row, JOB[("st", half, n, a)]))
                    if a == 0:
                        if unit >= 2:
                            p_lo_wait(act, row, unit - 2)
                        elif row.before().exists():
                            p_lo_wait(act, row.before(), HALVES * UNITS - 2 + unit)
                    act.activation(probs[:, unit % 2, 2 * a:2 * a + 2, 0:nq],
                                   bank(("st", half, n, a))[:, :].rearrange("p (r c) -> p r c", r=2)[:, :, 0:nq],
                                   ACT.Exp).then_inc(exped.sem, 1)

            def high_probs(row, unit):
                nq = queries(unit)
                act.wait_ge(masked.sem, masked.at(row, unit))
                if unit >= 2:
                    act.wait_ge(ring_full.sem, ring_full.at(row, JOB[("pv", *divmod(unit - 2, UNITS))]))
                act.activation(p_hi[:, unit % 3, :, 0:nq], probs[:, unit % 2, :, 0:nq], ACT.Copy)\
                    .then_inc(p_hi_out.sem, 1)

            def split_piece(n):
                act.wait_ge(piece_loaded[n % 2], 16 * (n // 2 + 1))
                act.activation(w_hi[:, n * PIECE:(n + 1) * PIECE], raw_ffn[:, n % 2 * PIECE:(n % 2 + 1) * PIECE],
                               ACT.Copy).then_inc(piece_hi, 1)
                if 1 <= n < HOOKS - 1:
                    act.wait_ge(piece_lo, n)
                    load_piece(n + 1)

            def experts(f, c):
                if c < NC:
                    act.wait_ge(ffn_full.sem, ffn_full.at(f, 3 * c))
                    if c >= 3:
                        act.wait_ge(g_lo_out.sem, g_lo_out.at(f, c - 3))
                    else:
                        act.wait_ge(g_lo_out.sem, g_lo_out.at(f.before(), last_on(3, c, NC)))
                    act.activation(gated[:, c % 3, :], ps_a[:, :], ACT.Tanh, scale=0.5).then_inc(tanh_out.sem, 1)
                if c >= 1:
                    m = c - 1
                    act.wait_ge(w_read.sem, w_read.at(f, m))
                    y_before(act, f, m)
                    act.activation(g_hi[:, m % 2, :], gated[:, m % 3, :], ACT.Copy).then_inc(g_hi_out.sem, 1)

            attention(Row(0), split_piece)
            with act.Fori(0, B - 1) as r:
                attention(Row(r, 1), lambda c: experts(Row(r, 0), c))
            for c in range(HOOKS):
                experts(Row(B - 1), c)

        @block.vector
        def _(dve):
            steps = 0

            def start(instruction):
                nonlocal steps
                steps += 1
                instruction.then_inc(start_step, 1)
                dve.wait_ge(start_step, steps)

            dve.wait_ge(silu_exp, 1)
            start(dve.tensor_scalar(ct_tmp[:, :, :], ct_tmp[:, :, :], 1.0, None, ALU.add))
            start(dve.reciprocal(ct_tmp[:, :, :], ct_tmp[:, :, :]))
            dve.tensor_tensor(ct[:, :, :], ct[:, :, :], ct_tmp[:, :, :], ALU.mult).then_inc(silu_done, 1)
            for parts in (q_parts, k_parts):
                dve.memset(parts[:, :, :, 3 * HD:64].bitcast(F32), 0.0)
            dve.memset(v_parts[:, :, :, 3 * HD:V3], 1.0)
            dve.wait_ge(consts_loaded, 64)
            start(dve.tensor_scalar(norm_w[:, 0:D], norm_w[:, 0:D], HD ** -0.5, None, ALU.mult))
            start(dve.memset(k_parts[:, :, :, 3 * HD:3 * HD + 1].bitcast(F32), 1.0))
            dve.wait_ge(w_loaded, 48)
            for raw, w in ((raw_qkv, wqkv), (raw_o, wo), (wg_raw, wg)):
                start(dve.tensor_copy(w[:, 0, :, :], raw[:, :, :]))
                ins = dve.tensor_tensor(w[:, 1, :, :], raw[:, :, :], w[:, 0, :, :].bitcast(F32), ALU.subtract)
            ins.then_inc(weights_split, 1)
            dve.wait_ge(mod_full, 1)
            start(dve.tensor_copy(cmod[:, :, :, :], ring[0][:, 0:4 * KD * B].rearrange("p (m k b) -> p m k b", m=4, k=KD)))
            for m in (0, 2):
                ins = dve.tensor_scalar(cmod[:, m, :, :], cmod[:, m, :, :], 1.0, None, ALU.add)
            ins.then_inc(mod_out, 1)
            g = ring[1][0:B, :]
            dve.tensor_scalar(gate_rows[1], g, 0.0, None, ALU.is_ge)
            dve.tensor_scalar(gate_rows[2], g, 0.25, None, ALU.max)
            start(dve.tensor_scalar(gate_rows[0], g, -0.25, None, ALU.min))
            start(dve.tensor_tensor(gate_rows[2], gate_rows[2], gate_rows[0], ALU.subtract))
            start(dve.tensor_tensor(gate_rows[1], gate_rows[1], gate_rows[2], ALU.mult))
            dve.tensor_tensor(gate_rows[0], gate_rows[0], gate_rows[1], ALU.add).then_inc(mod_out, 1)
            dve.wait_ge(constants, 1)

            def attention(row, hook, finish):
                done = 0

                def step(instruction):
                    nonlocal done
                    instruction.then_inc(att_step.sem, 1)
                    dve.wait_ge(att_step.sem, att_step.at(row, done))
                    done += 1

                def layer_norm(which, src):
                    for t in range(T):
                        ins = dve.bn_stats(stats[:, t, :], src[:, t, :])
                    step(ins)
                    dve.nop(nofuse=True)
                    for t in range(T):
                        ins = dve.bn_aggr(moments[:, t, :], stats[:, t, :])
                    ins.then_inc(stats_ready.sem, 1)
                    dve.wait_ge(stats_ready.sem, stats_ready.at(row, which))
                    dve.wait_ge(rstd_ready.sem, rstd_ready.at(row, 2 * which))
                    for t in range(T):
                        ins = dve.tensor_scalar(xn[:, t, :], src[:, t, :], moments[:, t, 0:1], rstd[:, t:t + 1],
                                                ALU.subtract, ALU.mult)
                    ins.then_inc(normed.sem, 1)
                    h = (h1, h2)[which]
                    for k in range(KD):
                        dve.wait_ge(modulated.sem, modulated.at(row, which * KD + k))
                        if which == 1:
                            dve.tensor_copy(h2_bf[:, k, :], h_f32[:, :])
                        step(dve.tensor_copy(h[:, 0, k, :], h_f32[:, :]))
                        dve.tensor_tensor(h[:, 1, k, :], h_f32[:, :], h[:, 0, k, :].bitcast(F32), ALU.subtract)\
                            .then_inc(h_split.sem, 1)

                dve.wait_ge(x_loaded.sem, x_loaded.at(row, 1))
                layer_norm(0, x_sb)

                for t in range(T):
                    w2, turned = weighted[:, t % 2, :], rot[:, t, :]
                    dve.wait_ge(squares.sem, squares.at(row, t))
                    if t >= 2:
                        dve.wait_ge(sin_done.sem, sin_done.at(row, t - 2))
                    dve.tensor_tensor(w2, bank(("qk", t))[:, :], norm_w[:, :], ALU.mult).then_inc(qk_weighted.sem, 1)
                    dve.wait_ge(v_hi.sem, v_hi.at(row, t))
                    if t >= 2:
                        dve.wait_ge(v_done.sem, v_done.at(row, t - 2))
                    dve.tensor_tensor(v_rest[:, t % 2, :, :], bank(("v", t))[:, 0:D].rearrange("p (h d) -> p h d", d=HD),
                                      v_parts[:, t, :, 0:HD], ALU.subtract).then_inc(v_sub.sem, 1)
                    dve.wait_ge(qk_weighted.sem, qk_weighted.at(row, t))
                    step(dve.tensor_tensor(heads(turned), heads(w2),
                                           cos[:, t, :].unsqueeze(1).broadcast_to((P, 4 * NH, HD // 2)), ALU.mult))
                    dve.wait_ge(sin_done.sem, sin_done.at(row, t))
                    a, z = (turned.rearrange("p (h s d) -> p h s d", s=2, d=HD // 2)[:, :, s, :] for s in range(2))
                    sa, sz = (by_sin[:, t % 2, :].rearrange("p (h s d) -> p h s d", s=2, d=HD // 2)[:, :, s, :] for s in range(2))
                    dve.tensor_tensor(a, a, sz, ALU.subtract)
                    dve.tensor_tensor(z, z, sa, ALU.add).then_inc(rotated.sem, 1)
                    if t % 2:
                        hook(t // 2)
                dve.wait_ge(rstd_ready.sem, rstd_ready.at(row, 1))
                for half in range(HALVES):
                    for t in range(T):
                        low_qk(row, half, t)
                    hook(2 + 5 * half)
                    for t in range(T):
                        for u in range(2 * G):
                            maxima(row, half, t, u)
                        if t == 1:
                            hook(3 + 5 * half)
                    hook(4 + 5 * half)
                    for n in range(UNITS + 3):
                        if 1 <= n <= UNITS and n - 1 not in ON_POOL:
                            low_probs(dve, row, half * UNITS + n - 1, p_lo_dve)
                        if n >= 3:
                            attend(half, n - 3, step)
                        if n == 2:
                            hook(5 + 5 * half)
                        if n == 5:
                            hook(6 + 5 * half)
                finish()
                for t in range(T + 1):
                    if t < T:
                        dve.wait_ge(attn_t_hi.sem, attn_t_hi.at(row, t))
                        dve.tensor_tensor(attn_t[:, t % 2, 1, :, :],
                                          bank(("oT", t))[:, 0:D].rearrange("p (k c) -> p k c", k=KD),
                                          attn_t[:, t % 2, 0, :, :].bitcast(F32), ALU.subtract).then_inc(attn_t_lo.sem, 1)
                    if t >= 1:
                        dve.wait_ge(ring_full.sem, ring_full.at(row, JOB[("op", t - 1)]))
                        dve.tensor_tensor(gated_proj[:, t % 2, :], bank(("op", t - 1))[:, 0:D], ga[:, :], ALU.mult)\
                            .then_inc(proj_read.sem, 1)
                        dve.wait_ge(proj_read.sem, proj_read.at(row, t - 1))
                        if t == 1 and row.before().exists():
                            dve.wait_ge(stored.sem, stored.at(row.before(), 0))
                        dve.tensor_tensor(x1[:, t - 1, :], gated_proj[:, t % 2, :], x_sb[:, t - 1, :], ALU.add)\
                            .then_inc(resid.sem, 1)
                dve.wait_ge(resid.sem, resid.at(row, T - 1))
                layer_norm(1, x1)
                route_row(row, step)
                assert done == ATT_STEPS, done

            def low_qk(row, half, t):
                slot, c = (half * T + t) % 2, half * HH * HD
                dve.wait_ge(qk_hi.sem, qk_hi.at(row, half * T + t))
                for s, parts, at in ((0, q_parts, 2), (1, k_parts, 1)):
                    src = rot[:, t, s * D + c:s * D + c + HH * HD].rearrange("p (h d) -> p h d", d=HD)
                    ins = dve.scalar_tensor_tensor(
                        out=parts[:, slot, :, at * HD:(at + 1) * HD], in0=src, scalar=qk_rstd[:, t, s:s + 1],
                        in1=parts[:, slot, :, 0:HD].bitcast(F32), op0=ALU.mult, op1=ALU.subtract)
                ins.then_inc(qk_lo.sem, 1)

            def maxima(row, half, t, u):
                g, a = divmod(u, 2)
                nk = 2 * P if t else P
                dve.wait_ge(ring_full.sem, ring_full.at(row, JOB[("max", half, t, u)]))
                dve.nop(nofuse=True)
                for r in range(2):
                    m = PAIRS * a + 2 * g + r
                    scores = bank(("max", half, t, u))[:, 2 * P * r:2 * P * r + nk]
                    ins = dve.tensor_tensor_reduce(scores, scores, band[:, 2 * P - nk:2 * P], 1.0, -3e38, ALU.add, ALU.max,
                                                   row_max[:, t, m:m + 1])
                ins.then_inc(maxed.sem, 1)

            def attend(half, n, step):
                nonlocal_row = row_now[0]
                unit, (g, t) = half * UNITS + n, divmod(n, T)
                dve.wait_ge(ring_full.sem, ring_full.at(nonlocal_row, JOB[("pv", half, n)]))
                sums = bank(("pv", half, n))[:, 0:4 * V3].rearrange("p (h c) -> p h c", c=V3)
                dve.reciprocal(pv_rden[:, n % 2, :], sums[:, :, V3 - 1])
                dve.tensor_reduce(pv_sum[:, n % 2, :, :], sums[:, :, 0:3 * HD].rearrange("p h (s d) -> p h d s", s=3),
                                  AX_X, ALU.add).then_inc(pv_read.sem, 1)
                dve.wait_ge(pv_read.sem, pv_read.at(nonlocal_row, unit))
                h = half * HH + 4 * g
                dve.tensor_tensor(attn[:, t, h:h + 4, :], pv_sum[:, n % 2, :, :],
                                  pv_rden[:, n % 2, :].unsqueeze(2).broadcast_to((P, 4, HD)), ALU.mult).then_inc(attn_out.sem, 1)

            def route_row(row, step):
                dve.wait_ge(ring_full.sem, ring_full.at(row, JOB[("lgT",)]))
                dve.tensor_copy(logits[:, :, :], bank(("lgT",))[:, 0:T * E].rearrange("p (t e) -> p t e", e=E))\
                    .then_inc(logits_out.sem, 1)
                dve.wait_ge(logits_out.sem, logits_out.at(row, 0))
                step(dve.tensor_reduce(top1[:, :], logits[:, :, :], AX_X, ALU.max))
                dve.tensor_tensor(shifted[:, :, :], logits[:, :, :], top1[:, :].unsqueeze(2).broadcast_to((P, T, E)),
                                  ALU.subtract).then_inc(shifted_out.sem, 1)
                other = logits[:, :, :].unsqueeze(2).broadcast_to((P, T, E, E))
                own = logits[:, :, :].unsqueeze(3).broadcast_to((P, T, E, E))
                dve.tensor_tensor(beats[:, :, :, :], other, own, ALU.is_gt)
                step(dve.tensor_tensor(ties[:, :, :, :], other, own, ALU.is_equal))
                step(dve.tensor_tensor(ties[:, :, :, :], ties[:, :, :, :],
                                       earlier[:, :, :].unsqueeze(1).broadcast_to((P, T, E, E)), ALU.mult))
                step(dve.tensor_tensor(beats[:, :, :, :], beats[:, :, :, :], ties[:, :, :, :], ALU.add))
                step(dve.tensor_reduce(rank[:, :, :], beats[:, :, :, :], AX_X, ALU.add))
                step(dve.tensor_scalar(rank[:, :, :], rank[:, :, :], 1.5, None, ALU.is_lt))
                dve.wait_ge(exps_out.sem, exps_out.at(row, 0))
                step(dve.tensor_tensor(route[:, :, :], exps[:, :, :], rank[:, :, :], ALU.mult))
                step(dve.tensor_reduce(route_sum[:, :], route[:, :, :], AX_X, ALU.add))
                step(dve.reciprocal(route_sum[:, :], route_sum[:, :]))
                step(dve.tensor_tensor(route[:, :, :], route[:, :, :],
                                       route_sum[:, :].unsqueeze(2).broadcast_to((P, T, E)), ALU.mult))
                step(dve.tensor_copy(route_parts[:, :, 0, :], route[:, :, :]))
                dve.tensor_tensor(route_parts[:, :, 1, :], route[:, :, :], route_parts[:, :, 0, :].bitcast(F32),
                                  ALU.subtract).then_inc(route_out.sem, 1)

            def experts(f, c):
                if c == NC:
                    return
                g = gated[:, c % 3, :]
                dve.wait_ge(tanh_out.sem, tanh_out.at(f, c))
                dve.scalar_tensor_tensor(out=g, in0=g, scalar=1.0, in1=ps_a[:, :], op0=ALU.add, op1=ALU.mult)\
                    .then_inc(a_read.sem, 1)
                dve.wait_ge(a_read.sem, a_read.at(f, c))
                dve.wait_ge(ffn_full.sem, ffn_full.at(f, 3 * c + 1))
                dve.tensor_tensor(g, g, ps_b[:, :], ALU.mult).then_inc(b_read.sem, 1)
                dve.wait_ge(b_read.sem, b_read.at(f, c))
                dve.wait_ge(ffn_full.sem, ffn_full.at(f, 3 * c + 2))
                dve.tensor_tensor(g, g, ps_w[:, :], ALU.mult).then_inc(w_read.sem, 1)

            def finish(f):
                dve.wait_ge(y_done.sem, y_done.at(f, NC - 1))
                dve.wait_ge(gb_loaded.sem, gb_loaded.at(f, 0))
                for b in range(2):
                    if b:
                        dve.wait_ge(final.sem, final.at(f, 0))
                    dve.tensor_tensor(y_gated[:, :, :], ps_y[b][:, :].rearrange("p (t c) -> p t c", t=2),
                                      gb[:, :].unsqueeze(1).broadcast_to((P, 2, D)), ALU.mult).then_inc(y_read.sem, 1)
                    dve.wait_ge(y_read.sem, y_read.at(f, b))
                    dve.tensor_tensor(x1[:, 2 * b:2 * b + 2, :], x1[:, 2 * b:2 * b + 2, :], y_gated[:, :, :], ALU.add)\
                        .then_inc(final.sem, 1)

            row_now = [Row(0)]
            attention(Row(0), lambda c: None, lambda: None)
            for read in (a_read, b_read, w_read, y_read):
                read.grant(dve)
            with dve.Fori(0, B - 1) as r:
                row_now[0] = Row(r, 1)
                attention(Row(r, 1), lambda c: experts(Row(r, 0), c), lambda: finish(Row(r, 0)))
            for c in range(HOOKS):
                experts(Row(B - 1), c)
            finish(Row(B - 1))

        @block.tensor
        def _(pe):
            pe.wait_ge(silu_done, 1)
            for m, chunk in enumerate((1, 0, 4, 3)):
                for k in range(KD):
                    at = (m * KD + k) * B
                    for j in range(KD):
                        c = chunk * D + k * P
                        pe.matmul(ring[0][:, at:at + B], raw_mod[j][:, c:c + P], ct[:, j, :],
                                  start=(j == 0), stop=(j == KD - 1))
            for m, chunk in enumerate((2, 5)):
                for j in range(KD):
                    ins = pe.matmul(ring[1][0:B, m * D:(m + 1) * D], ct[:, j, :],
                                    raw_mod[j][:, chunk * D:(chunk + 1) * D], start=(j == 0), stop=(j == KD - 1))
            ins.then_inc(mod_full, 1)
            pe.wait_ge(constants, 1)
            pe.wait_ge(weights_split, 1)
            pe.wait_ge(mod_out, 2)

            SPLIT = ((0, 0), (0, 1), (1, 0))

            def products(dst, stationary, moving, signal=None):
                for k in range(KD):
                    for n, (s, m) in enumerate(SPLIT):
                        ins = pe.matmul(dst, stationary(s, k), moving(m, k), start=(k == 0 and n == 0),
                                        stop=(k == KD - 1 and n == len(SPLIT) - 1))
                return ins

            def layer_norm_transposes(row, which):
                pe.wait_ge(normed.sem, normed.at(row, which))
                for k in range(KD):
                    bank_free(pe, row, ("ln", which, k))
                    for t in range(T):
                        ins = pe.transpose(bank(("ln", which, k))[:, t * P:(t + 1) * P], xn[:, t, k * P:(k + 1) * P],
                                           ident[:, :])
                    ins.then_inc(ring_full.sem, 1)

            def attention(row, hook):
                layer_norm_transposes(row, 0)
                pe.wait_ge(h_split.sem, h_split.at(row, KD - 1))
                for t in range(T):
                    tokens = slice(t * P, (t + 1) * P)
                    for job, a, z in ((("qk", t), 0, 2 * D), (("v", t), 2 * D, 3 * D)):
                        bank_free(pe, row, job)
                        products(bank(job)[:, 0:z - a], lambda s, k: h1[:, s, k, tokens],
                                 lambda m, k: wqkv[:, m, k, a:z]).then_inc(ring_full.sem, 1)
                    if t % 2:
                        hook(t // 2)
                for half in range(HALVES):
                    for t in range(T):
                        transpose_qk(row, half, t)
                    hook(2 + 5 * half)
                    for t in range(T):
                        pe.wait_ge(k_t_out.sem, k_t_out.at(row, half * T + t))
                        for u in range(2 * G):
                            query_scores(row, half, t, u)
                        if t == 1:
                            hook(3 + 5 * half)
                    bank_free(pe, row, ("mT", half))
                    pe.wait_ge(maxed.sem, maxed.at(row, (half * T + T) * 2 * G - 1))
                    for t in range(T):
                        ins = pe.transpose(bank(("mT", half))[0:HH, t * P:(t + 1) * P], row_max[:, t, :], ident[:, :])
                    ins.then_inc(ring_full.sem, 1)
                    hook(4 + 5 * half)
                    pe.wait_ge(max_rows_set.sem, max_rows_set.at(row, 2 * half + 1))
                    for n in range(UNITS + PV_LAG):
                        if n < UNITS:
                            for a in range(2):
                                key_scores(row, half, n, a)
                        if n >= PV_LAG:
                            probs_times_v(row, half, n - PV_LAG)
                        if n == 2:
                            hook(5 + 5 * half)
                        if n == 5:
                            hook(6 + 5 * half)
                for t in range(T + 1):
                    if t < T:
                        job = ("oT", t)
                        pe.wait_ge(attn_out.sem, attn_out.at(row, HALVES * UNITS - T + t))
                        bank_free(pe, row, job)
                        for k in range(KD):
                            ins = pe.transpose(bank(job)[:, k * P:(k + 1) * P],
                                               attn[:, t, k * HH:(k + 1) * HH, :].rearrange("p h d -> p (h d)"), ident[:, :])
                        ins.then_inc(ring_full.sem, 1)
                    if t >= 1:
                        job, slot = ("op", t - 1), (t - 1) % 2
                        pe.wait_ge(attn_t_lo.sem, attn_t_lo.at(row, t - 1))
                        bank_free(pe, row, job)
                        products(bank(job)[:, 0:D], lambda s, k: attn_t[:, slot, s, k, :],
                                 lambda m, k: wo[:, m, k, :]).then_inc(ring_full.sem, 1)
                layer_norm_transposes(row, 1)
                pe.wait_ge(h_split.sem, h_split.at(row, 2 * KD - 1))
                bank_free(pe, row, ("lg",))
                products(bank(("lg",))[0:E, :], lambda s, k: wg[:, s, k, :], lambda m, k: h2[:, m, k, :])\
                    .then_inc(ring_full.sem, 1)
                bank_free(pe, row, ("lgT",))
                pe.wait_ge(logits_t_out.sem, logits_t_out.at(row, 0))
                pe.nop(nofuse=True)
                for t in range(T):
                    ins = pe.transpose(bank(("lgT",))[:, t * E:(t + 1) * E], logits_t[:, t * P:(t + 1) * P],
                                       ident[0:E, 0:E])
                ins.then_inc(ring_full.sem, 1)
                pe.wait_ge(route_out.sem, route_out.at(row, 0))
                bank_free(pe, row, ("wT",))
                for t in range(T):
                    ins = pe.transpose(bank(("wT",))[0:2 * E, t * P:(t + 1) * P],
                                       route_parts[:, t, :, :].rearrange("p s e -> p (s e)").bitcast(F32), ident[:, :])
                ins.then_inc(ring_full.sem, 1)

            def transpose_qk(row, half, t):
                slot = (half * T + t) % 2
                pe.wait_ge(qk_lo.sem, qk_lo.at(row, half * T + t))
                for job, parts in (("qT", q_parts), ("kT", k_parts)):
                    bank_free(pe, row, (job, half, t))
                    for p in range(PAIRS):
                        ins = pe.transpose(bank((job, half, t))[:, p * P:(p + 1) * P],
                                           parts[:, slot, 2 * p:2 * p + 2, :].rearrange("p h c -> p (h c)").bitcast(F32),
                                           ident[:, :])
                    ins.then_inc(ring_full.sem, 1)

            def query_scores(row, half, t, u):
                g, a = divmod(u, 2)
                job, rows = ("max", half, t, u), slice(64 * a, 64 * a + 64)
                first = max(t - 1, 0)
                nk = (t + 1 - first) * P
                bank_free(pe, row, job)
                for r in range(2):
                    ins = pe.matmul(bank(job)[:, 2 * P * r:2 * P * r + nk], q_t[rows, 2 * g + r, t * P:(t + 1) * P],
                                    k_t[rows, 2 * g + r, first * P:(t + 1) * P], start=True, stop=True)
                ins.then_inc(ring_full.sem, 1)

            def key_scores(row, half, n, a):
                (g, j), nq, rows = divmod(n, T), queries(n), slice(64 * a, 64 * a + 64)
                job = ("st", half, n, a)
                bank_free(pe, row, job)
                for r in range(2):
                    ins = pe.matmul(bank(job)[:, 2 * P * r:2 * P * r + nq], k_t[rows, 2 * g + r, j * P:(j + 1) * P],
                                    q_t[rows, 2 * g + r, j * P:j * P + nq], start=True, stop=True)
                ins.then_inc(ring_full.sem, 1)

            def probs_times_v(row, half, n):
                unit, (g, t) = half * UNITS + n, divmod(n, T)
                job = ("pv", half, n)
                if half * T + t == 0 and g == 0:
                    pe.wait_ge(v_done.sem, v_done.at(row, T - 1))
                p_lo_wait(pe, row, unit)
                bank_free(pe, row, job)
                for h in range(4):
                    r, a = divmod(h, 2)
                    todo = [(p, u, at) for u, at in ([(unit - 1, P)] if t else []) + [(unit, 0)] for p in (p_hi, p_lo)]
                    for i, (p, u, at) in enumerate(todo):
                        tile = t - (at > 0)
                        ins = pe.matmul(bank(job)[:, h * V3:(h + 1) * V3], p[:, u % 3, 2 * a + r, at:at + P],
                                        v_parts[:, tile, half * HH + 4 * g + h, :],
                                        start=(i == 0), stop=(i == len(todo) - 1))
                ins.then_inc(ring_full.sem, 1)

            def hidden(f, c):
                for n, (dst, free) in enumerate(((ps_a, a_read), (ps_b, b_read))):
                    if c:
                        pe.wait_ge(free.sem, free.at(f, c - 1))
                    else:
                        pe.wait_ge(free.sem, free.at(f.before(), NC - 1))
                    for k in range(KD):
                        at = k * 2 * FH + n * FH + c * P
                        first, last = k == 0, k == KD - 1
                        pe.matmul(dst[:, :], w_hi[:, at:at + P], h2[:, 0, k, :], start=first, stop=False)
                        pe.matmul(dst[:, :], w_hi[:, at:at + P], h2[:, 1, k, :], start=False, stop=False)
                        ins = pe.matmul(dst[:, :], w12_lo[:, at:at + P], h2_bf[:, k, :], start=False, stop=last)
                    ins.then_inc(ffn_full.sem, 1)
                if c:
                    pe.wait_ge(w_read.sem, w_read.at(f, c - 1))
                else:
                    pe.wait_ge(w_read.sem, w_read.at(f.before(), NC - 1))
                    pe.wait_ge(route_t_out.sem, route_t_out.at(f, 0))
                pe.matmul(ps_w[:, :], expert_rows.rearrange("p e r -> p (e r)")[:, c * P:(c + 1) * P], route_t[:, :],
                          start=True, stop=True).then_inc(ffn_full.sem, 1)

            def add_to_y(f, c):
                pe.wait_ge(g_lo_out.sem, g_lo_out.at(f, c))
                if c == 0:
                    pe.wait_ge(y_read.sem, y_read.at(f.before(), 1))
                w3_hi = w_hi[:, WCOLS + c * D:WCOLS + (c + 1) * D]
                for t in range(T):
                    tokens = slice(t * P, (t + 1) * P)
                    for n, (g, w) in enumerate(((g_hi, w3_hi), (g_hi, w3_lo[:, c * D:(c + 1) * D]), (g_lo, w3_hi))):
                        ins = pe.matmul(ps_y[t // 2][:, t % 2 * D:(t % 2 + 1) * D], g[:, c % 2, tokens], w,
                                        start=(c == 0 and n == 0 and t % 2 == 0), stop=(c == NC - 1 and n == 2),
                                        skip_group_check=True)
                ins.then_inc(y_done.sem, 1)

            def experts(f, c):
                if c < NC:
                    hidden(f, c)
                if c >= 1:
                    add_to_y(f, c - 1)

            attention(Row(0), lambda c: None)
            y_done.grant(pe)
            pe.wait_ge(piece_hi, HOOKS)
            pe.wait_ge(piece_lo, HOOKS)
            with pe.Fori(0, B - 1) as r:
                attention(Row(r, 1), lambda c: experts(Row(r, 0), c))
            for c in range(HOOKS):
                experts(Row(B - 1), c)


def kernel(L0_attn_hidden_states, L0_attn_w_qkv, L0_attn_q_norm_w, L0_attn_k_norm_w, L0_attn_w_o,
           L0_ffn_Wg, L0_ffn_W1, L0_ffn_W2, L0_ffn_W3, L0_c, L0_wmod):
    import concourse.bacc as bacc
    from concourse.bass_utils import run_bass_kernel_spmd

    def by_contraction(w):
        return np.ascontiguousarray(np.transpose(np.asarray(w).reshape(w.shape[0], -1, P), (2, 1, 0)))

    w12 = by_contraction(np.concatenate([np.asarray(L0_ffn_W1).reshape(FH, D), np.asarray(L0_ffn_W2).reshape(FH, D)]))
    w3 = by_contraction(np.transpose(np.asarray(L0_ffn_W3), (1, 0, 2)).reshape(D, FH))
    angles = np.arange(S, dtype=np.float32)[:, None] * (
        1.0 / 10000.0 ** (np.arange(0, HD, 2, dtype=np.float32) / np.float32(HD))).astype(np.float32)[None, :]
    rope = np.stack([np.cos(angles), np.sin(angles)]).astype(np.float32)
    arrays = {
        "x": np.ascontiguousarray(np.asarray(L0_attn_hidden_states).reshape(B, T, P, D).transpose(0, 2, 1, 3)),
        "w_qkv_t": by_contraction(L0_attn_w_qkv),
        "q_norm": np.asarray(L0_attn_q_norm_w).reshape(1, D),
        "k_norm": np.asarray(L0_attn_k_norm_w).reshape(1, D),
        "w_o_t": by_contraction(L0_attn_w_o),
        "w_g_t": by_contraction(L0_ffn_Wg),
        "w_ffn": np.concatenate([w12.reshape(P, WCOLS), w3.reshape(P, W3COLS)], axis=1),
        "c_t": by_contraction(L0_c),
        "w_mod": np.ascontiguousarray(np.asarray(L0_wmod).reshape(KD, P, 6 * D)),
        "rope": np.ascontiguousarray(rope.reshape(2, T, P, HD // 2).transpose(0, 2, 1, 3)),
    }
    nc = bacc.Bacc("TRN2", target_bir_lowering=False, num_devices=1,
                   dynamic_dma_scratch_size=1024)
    args = {n: nc.dram_tensor("in_" + n, a.shape, mybir.dt.from_np(a.dtype), kind="ExternalInput").ap()
            for n, a in arrays.items()}
    gates = nc.dram_tensor("gates", (B, 2 * D), F32).ap()
    out = nc.dram_tensor("out", (B, P, T, D), F32, kind="ExternalOutput").ap()
    build(nc, **args, gates=gates, out=out)
    r = run_bass_kernel_spmd(nc, [{"in_" + n: a for n, a in arrays.items()}], core_ids=[0])
    got = r.results[0]["out"]
    return got.transpose(0, 2, 1, 3).reshape(B, S, D)
```

```python
from contextlib import ExitStack

import numpy as np

import concourse.bass as bass
from concourse import mybir

F32 = mybir.dt.float32
F32R = mybir.dt.float32r
BF16 = mybir.dt.bfloat16
F16 = mybir.dt.float16
ACT = mybir.ActivationFunctionType
ALU = mybir.AluOpType
AX_X = mybir.AxisListType.X

P = 128
B, S, D = 8, 512, 256
T = S // P
KD = D // P
NH, HD = 16, 16
WINDOW = 128
E, HID = 8, 176
FH = E * HID
NC = FH // P
HALVES = 2
HH = NH // HALVES
PAIRS = HH // 2
G = 2
UNITS = G * T
V3 = 3 * HD + 1
RING = 3
PIECES = NC + 1
PLACES = 2 * NC + 4
PV_LAG = 2
ON_POOL = (0, 2, 4, 6)
EARLY_STEPS = 1 + KD + T
LATE_STEPS = 1 + KD + 11
WCOLS = 2 * FH * KD
W3COLS = NC * D
PIECE = (WCOLS + W3COLS) // PIECES
LN_EPS, RMS_EPS = 1e-5, 1e-6
BIG = 1e30


NU = HALVES * UNITS
TURN_AT = {0: 2, 2: 3}
MAX_AT = {1: 1, 3: 2, 5: 3}
MAX_ROWS_AT = 6
STATS_AT, NORM_AT = 8, 11
OUT_AT = NU
END = NU + T + 3


def places_at(point):
    kind, *at = point
    first = {"tile": lambda t, n: 2 * t + n, "gap": lambda: 2 * T, "unit": lambda u: 2 * T + 1 + u}[kind](*at)
    return [first] if first < PLACES else []


def ring_jobs():
    def queries(half, t):
        return [("max", half, t, u) for u in range(2 * G)]

    def turned(half, t):
        return [("qT", half, t), ("kT", half, t)]

    jobs = []
    for t in range(T):
        jobs += turned(0, t)
        if t >= 1:
            jobs += queries(0, t - 1)
    jobs += queries(0, T - 1) + turned(1, 0) + [("mT", 0)] + turned(1, 1) + queries(1, 0)
    for u in range(END):
        if u < NU:
            jobs += [("st", u, a) for a in range(2)]
        if PV_LAG <= u < NU + PV_LAG:
            jobs += [("pv", u - PV_LAG)]
        if u in TURN_AT:
            jobs += turned(1, TURN_AT[u])
        if u in MAX_AT:
            jobs += queries(1, MAX_AT[u])
        if u == MAX_ROWS_AT:
            jobs += [("mT", 1)]
        if 0 <= u - OUT_AT - 2 < T:
            jobs += [("op", u - OUT_AT - 2)]
        if 0 <= u - OUT_AT < T:
            jobs += [("oT", u - OUT_AT)]
        if u == NU:
            jobs += [("early ln", k) for k in range(KD)]
        if 0 <= u - NU - 3 < T:
            jobs += [("qk", u - NU - 3), ("v", u - NU - 3)]
    jobs += [("ln", k) for k in range(KD)]
    jobs += [("lg",), ("lgT",)]
    return jobs


JOBS = ring_jobs()
SLOT = {job: n for n, job in enumerate(JOBS)}
EARLY = ("early ln", "qk", "v")
EARLY_JOB = {job: n for n, job in enumerate(j for j in JOBS if j[0] in EARLY)}
JOB = {job: n for n, job in enumerate(j for j in JOBS if j[0] not in EARLY)}


class Row:

    def __init__(self, base, shift=0):
        self.base, self.shift = base, shift

    def before(self):
        return Row(self.base, self.shift - 1)

    def after(self):
        return Row(self.base, self.shift + 1)

    def index(self):
        return self.base + self.shift

    def exists(self):
        return not isinstance(self.base, int) or 0 <= self.base + self.shift < B


class Event:

    def __init__(self, sem, per_row, step=1, ahead=0):
        self.sem, self.per_row, self.step, self.ahead = sem, per_row, step, ahead

    def grant(self, eng):
        eng.sem_inc(self.sem, self.per_row)

    def at(self, row, k):
        more = ((row.shift + self.ahead) * self.per_row + k + 1) * self.step
        return row.base * (self.per_row * self.step) + more


def last_on(ring, slot, count):
    return max(n for n in range(count) if n % ring == slot)


def build(nc, x, w_qkv_t, q_norm, k_norm, w_o_t, w_g_t, w_ffn, c_t, w_mod, rope, gates, out):
    ctx = ExitStack()
    with ctx:
        def sb(name, shape, dt=F32):
            return ctx.enter_context(nc.sbuf_tensor(name, shape, dt))

        def before(name, shape):
            with nc.sbuf_tensor(name, shape, F32) as buffer:
                return buffer

        def psum(name):
            return ctx.enter_context(nc.psum_tensor(name, [P, 512], F32))

        def sem(name):
            return ctx.enter_context(nc.semaphore(name))

        def event(name, per_row, step=1, ahead=0):
            return Event(sem(name), per_row, step, ahead)

        w_hi = sb("w_hi", [P, WCOLS + W3COLS], F32R)
        w12_lo = sb("w12_lo", [P, WCOLS], BF16)
        w3_lo = sb("w3_lo", [P, W3COLS], F32R)
        wqkv = sb("wqkv", [P, 2, KD, 3 * D], F32R)
        wo = sb("wo", [P, 2, KD, D], F32R)
        wg = sb("wg", [P, 2, KD, E], F32R)
        wg_raw = sb("wg_raw", [P, KD, E])
        ident = sb("ident", [P, P])
        band = sb("band", [P, 2 * P])
        few_rows = sb("few_rows", [P, FH], F32R)
        expert_rows = few_rows[0:2 * E, :].rearrange("p (e r) -> p e r", e=E)
        neg_max_t = few_rows[64:64 + HH, 0:S]
        earlier = sb("earlier", [P, E, E])
        minus_half = sb("minus_half", [P, T, 2])
        cos = sb("cos", [P, T, HD // 2])
        sin = sb("sin", [P, T, HD // 2])
        norm_w = sb("norm_w", [P, 2 * D])
        ct = sb("ct", [P, KD, B])
        ct_tmp = sb("ct_tmp", [P, KD, B])
        cmod = sb("cmod", [P, 4, KD, B])
        x_early = sb("x_early", [P, T, D])
        x_sb = sb("x_sb", [P, T, D])
        xn = sb("xn", [P, T, D])
        x1 = sb("x1", [P, T, D])
        ga = sb("ga", [P, D])
        gb = sb("gb", [P, D])
        stats = sb("stats", [P, T, 6])
        moments = sb("moments", [P, T, 2])
        variance = sb("variance", [P, T])
        rstd = sb("rstd", [P, T])
        h_f32 = sb("h_f32", [P, S])
        h1 = sb("h1", [P, 2, KD, S], F32R)
        raw_mod0 = before("raw_mod0", [P, 6 * D])
        h2 = sb("h2", [P, 2, KD, S], F32R)
        h2_bf = sb("h2_bf", [P, KD, S], BF16)
        square = sb("square", [P, 2, D])
        logits_t = square.rearrange("p s c -> p (s c)")[0:E, :]
        sumsq = sb("sumsq", [P, T, 2])
        meansq = sb("meansq", [P, T, 2])
        qk_rstd = sb("qk_rstd", [P, T, 2])
        weighted = sb("weighted", [P, 2, 2 * D])
        by_sin = sb("by_sin", [P, 2, 2 * D])
        rot = before("rot", [P, 2 * HALVES, T, P])
        q_t_2 = sb("q_t_2", [P, PAIRS, S], F32R)
        q_parts = sb("q_parts", [P, 2, HH, 64], F32R)
        k_parts = sb("k_parts", [P, 2, HH, 64], F32R)
        q_t = [sb("q_t", [P, PAIRS, S], F32R)[:, :, :], q_t_2[:, :, :]]
        k_t = [sb("k_t", [P, PAIRS, S], F32R)[:, :, :], h1.rearrange("p s k c -> p (s k) c")]
        v_parts = sb("v_parts", [P, T, NH, V3], BF16)
        v_rest = sb("v_rest", [P, 2, NH, HD])
        row_max = sb("row_max", [P, HALVES, T, HH])
        probs = sb("probs", [P, 2, 4, 2 * P])
        p_hi = sb("p_hi", [P, 3, 4, 2 * P], F16)
        p_lo = sb("p_lo", [P, 3, 4, 2 * P], F16)
        pv_sum = sb("pv_sum", [P, 2, 4, HD])
        pv_rden = sb("pv_rden", [P, 2, 4])
        attn = sb("attn", [P, T, NH, HD])
        attn_t = sb("attn_t", [P, 2, 2, KD, P], F32R)
        gated_proj = sb("gated_proj", [P, 2, D])
        logits = sb("logits", [P, T, E])
        top1 = sb("top1", [P, T])
        shifted = sb("shifted", [P, T, E])
        exps = sb("exps", [P, T, E])
        beats = sb("beats", [P, T, E, E])
        ties = sb("ties", [P, T, E, E])
        rank = sb("rank", [P, T, E])
        route_sum = sb("route_sum", [P, T])
        route = sb("route", [P, T, E])
        route_parts = sb("route_parts", [P, T, 2, E], F32R)
        route_t = sb("route_t", [2 * E, S], F32R)
        gated = sb("gated", [P, 2, S])
        raw_ffn = before("raw_ffn", [P, 2, PIECE])
        g_hi = sb("g_hi", [P, 2, S], F32R)
        g_lo = sb("g_lo", [P, 2, S], F32R)
        y_gated = sb("y_gated", [P, 2, D])

        raw_qkv = rot.rearrange("p b t c -> p (b t c)")[:, 0:KD * 3 * D].rearrange("p (k c) -> p k c", k=KD)
        raw_o = attn.rearrange("p t h d -> p (t h d)")[:, 0:KD * D].rearrange("p (k c) -> p k c", k=KD)
        raw_mod = [raw_mod0[:, :], probs.rearrange("p r h c -> p (r h c)")[:, 0:6 * D]]

        flat = xn.rearrange("p t c -> p (t c)")
        gate_rows = [y_gated.rearrange("p t c -> p (t c)")[0:B, :], flat[0:B, 0:2 * D], flat[0:B, 2 * D:4 * D]]

        ring = [psum(f"ring{n}") for n in range(RING)]
        ps_a, ps_b, ps_w = psum("ps_a"), psum("ps_b"), psum("ps_w")
        ps_y = [psum("ps_y0"), psum("ps_y1")]

        mod_loaded = sem("mod_loaded")
        consts_loaded = sem("consts_loaded")
        w_loaded = sem("w_loaded")
        constants = sem("constants")
        pool_step = sem("pool_step")
        silu_exp = sem("silu_exp")
        start_step = sem("start_step")
        silu_done = sem("silu_done")
        mod_full = sem("mod_full")
        mod_out = sem("mod_out")
        weights_split = sem("weights_split")
        gates_stored = sem("gates_stored")
        piece_loaded = [sem("piece_loaded0"), sem("piece_loaded1")]
        piece_hi = sem("piece_hi")
        piece_lo = sem("piece_lo")

        x_early_loaded = event("x_early_loaded", 1, 16)
        x_loaded = event("x_loaded", 2, 16)
        gb_loaded = event("gb_loaded", 1, 16)
        max_rows_set = event("max_rows_set", 4, 16)
        stored = event("stored", 1, 16)
        ring_full = event("ring_full", len(JOB))
        early_full = event("early_full", len(EARLY_JOB))
        stats_ready = [event(f"stats_ready{n}", 1) for n in range(2)]
        var_ready = [event(f"var_ready{n}", 1) for n in range(2)]
        rstd_ready = [event(f"rstd_ready{n}", 1) for n in range(2)]
        normed = [event(f"normed{n}", 1) for n in range(2)]
        modulated = [event(f"modulated{n}", KD) for n in range(2)]
        h_split = [event(f"h_split{n}", KD) for n in range(2)]
        qk_var_ready = event("qk_var_ready", 2)
        qk_rstd_ready = event("qk_rstd_ready", 2)
        squares = event("squares", T)
        qk_weighted = event("qk_weighted", T)
        sin_done = event("sin_done", T)
        rotated = event("rotated", T)
        v_hi = event("v_hi", T)
        v_sub = event("v_sub", T)
        v_mid = event("v_mid", T)
        v_done = event("v_done", T)
        qk_hi = event("qk_hi", HALVES * T)
        qk_lo = event("qk_lo", HALVES * T)
        q_t_out = event("q_t_out", HALVES * T)
        k_t_out = event("k_t_out", HALVES * T)
        maxed = event("maxed", HALVES * T * 2 * G)
        max_t_out = event("max_t_out", HALVES)
        exped = event("exped", HALVES * UNITS * 2)
        masked = event("masked", HALVES * UNITS)
        p_hi_out = event("p_hi_out", HALVES * UNITS)
        p_lo_pool = event("p_lo_pool", HALVES * len(ON_POOL))
        p_lo_dve = event("p_lo_dve", HALVES * (UNITS - len(ON_POOL)))
        pv_read = event("pv_read", HALVES * UNITS)
        attn_out = event("attn_out", HALVES * UNITS)
        attn_t_hi = event("attn_t_hi", T)
        attn_t_lo = event("attn_t_lo", T)
        proj_read = event("proj_read", T)
        resid = event("resid", T)
        logits_t_out = event("logits_t_out", 1)
        logits_out = event("logits_out", 1)
        shifted_out = event("shifted_out", 1)
        exps_out = event("exps_out", 1)
        route_out = event("route_out", 1)
        route_t_out = event("route_t_out", 1)
        route_turned = event("route_turned", 1)
        ffn_full = event("ffn_full", 3 * NC)
        y_done = event("y_done", NC, ahead=1)
        tanh_out = event("tanh_out", NC)
        a_read = event("a_read", NC, ahead=1)
        b_read = event("b_read", NC, ahead=1)
        w_read = event("w_read", NC, ahead=1)
        g_hi_out = event("g_hi_out", NC)
        g_lo_out = event("g_lo_out", NC, ahead=1)
        y_read = event("y_read", 2, ahead=1)
        final = event("final", 2)
        early_step = event("early_step", EARLY_STEPS)
        late_step = event("late_step", LATE_STEPS)

        def p_lo_wait(eng, row, unit):
            half, n = divmod(unit, UNITS)
            if n in ON_POOL:
                eng.wait_ge(p_lo_pool.sem, p_lo_pool.at(row, half * len(ON_POOL) + ON_POOL.index(n)))
            else:
                on_dve = [m for m in range(UNITS) if m not in ON_POOL]
                eng.wait_ge(p_lo_dve.sem, p_lo_dve.at(row, half * len(on_dve) + on_dve.index(n)))

        def bank(job):
            return ring[SLOT[job] % RING]

        def bank_free(eng, row, job):
            n = SLOT[job]
            while True:
                n -= RING
                if n < 0:
                    row, n = row.before(), last_on(RING, SLOT[job] % RING, len(JOBS))
                if not row.exists() and not row.after().exists():
                    return
                kind, *at = JOBS[n]
                if (row.after() if kind in EARLY else row).exists():
                    break
            next_row = row.after()
            if kind == "early ln":
                eng.wait_ge(modulated[0].sem, modulated[0].at(next_row, at[0]))
            if kind == "ln":
                eng.wait_ge(modulated[1].sem, modulated[1].at(row, at[0]))
            if kind == "qk":
                eng.wait_ge(qk_weighted.sem, qk_weighted.at(next_row, at[0]))
            if kind == "v":
                eng.wait_ge(v_sub.sem, v_sub.at(next_row, at[0]))
            if kind == "qT":
                eng.wait_ge(q_t_out.sem, q_t_out.at(row, at[0] * T + at[1]))
            if kind == "kT":
                eng.wait_ge(k_t_out.sem, k_t_out.at(row, at[0] * T + at[1]))
            if kind == "max":
                eng.wait_ge(maxed.sem, maxed.at(row, (at[0] * T + at[1]) * 2 * G + at[2]))
            if kind == "mT":
                eng.wait_ge(max_t_out.sem, max_t_out.at(row, at[0]))
            if kind == "st":
                eng.wait_ge(exped.sem, exped.at(row, at[0] * 2 + at[1]))
            if kind == "pv":
                eng.wait_ge(pv_read.sem, pv_read.at(row, at[0]))
            if kind == "oT":
                eng.wait_ge(attn_t_lo.sem, attn_t_lo.at(row, at[0]))
            if kind == "op":
                eng.wait_ge(proj_read.sem, proj_read.at(row, at[0]))
            if kind == "lg":
                eng.wait_ge(logits_t_out.sem, logits_t_out.at(row, 0))
            if kind == "lgT":
                eng.wait_ge(logits_out.sem, logits_out.at(row, 0))

        def queries(n):
            return 2 * P if n % T < T - 1 else P

        def heads(qk):
            return qk.rearrange("p (h d) -> p h d", d=HD // 2)

        def y_before(eng, f, m):
            if m >= 2:
                eng.wait_ge(y_done.sem, y_done.at(f, m - 2))
            else:
                eng.wait_ge(y_done.sem, y_done.at(f.before(), last_on(2, m, NC)))

        def low_probs(eng, row, unit, done):
            nq = queries(unit)
            eng.wait_ge(p_hi_out.sem, p_hi_out.at(row, unit))
            eng.tensor_tensor(p_lo[:, unit % 3, :, 0:nq], probs[:, unit % 2, :, 0:nq], p_hi[:, unit % 3, :, 0:nq],
                              ALU.subtract).then_inc(done.sem, 1)

        def one_row(row):
            b = row.index()
            return slice(b, b + 1) if isinstance(b, int) else bass.ds(b, 1)

        def run(place, point):
            for n in places_at(point):
                place(n)

        block = ctx.enter_context(nc.Block())

        @block.sync
        def _(sp):
            sp.dma_start(ct[:, :, :], c_t).then_inc(mod_loaded, 16)
            for k in range(KD):
                sp.dma_start(raw_mod[k], w_mod[k]).then_inc(mod_loaded, 16)
            sp.dma_start(x_early[:, :, :], x[0]).then_inc(x_early_loaded.sem, 16)
            sp.dma_start(raw_qkv, w_qkv_t).then_inc(w_loaded, 16)
            sp.dma_start(raw_o, w_o_t).then_inc(w_loaded, 16)
            sp.dma_start(wg_raw[:, :, :], w_g_t).then_inc(w_loaded, 16)
            sp.dma_start(cos[:, :, :], rope[0]).then_inc(consts_loaded, 16)
            sp.dma_start(sin[:, :, :], rope[1]).then_inc(consts_loaded, 16)
            sp.dma_start(norm_w[:, 0:D], q_norm.broadcast_to((P, D))).then_inc(consts_loaded, 16)
            sp.dma_start(norm_w[:, D:2 * D], k_norm.broadcast_to((P, D))).then_inc(consts_loaded, 16)
            sp.wait_ge(mod_out, 2)
            sp.dma_start(gates[:, :], gate_rows[0]).then_inc(gates_stored, 16)
            sp.wait_ge(gates_stored, 16)

            def store(prev):
                sp.wait_ge(final.sem, final.at(prev, 1))
                sp.nop(nofuse=True)
                sp.dma_start(out[prev.index()], x1[:, :, :]).then_inc(stored.sem, 16)

            def attention(row):
                if row.after().exists():
                    sp.wait_ge(normed[0].sem, normed[0].at(row, 0))
                    sp.nop(nofuse=True)
                    sp.dma_start(x_early[:, :, :], x[row.after().index()]).then_inc(x_early_loaded.sem, 16)
                if row.before().exists():
                    sp.wait_ge(resid.sem, resid.at(row.before(), T - 1))
                    sp.nop(nofuse=True)
                sp.dma_start(x_sb[:, :, :], x[row.index()]).then_inc(x_loaded.sem, 16)
                sp.dma_start(ga[:, :], gates[one_row(row), 0:D].broadcast_to((P, D))).then_inc(x_loaded.sem, 16)
                for half in range(HALVES):
                    sp.wait_ge(max_t_out.sem, max_t_out.at(row, half))
                    for a in range(2):
                        sp.dma_start(q_t[half][64 * a + 3 * HD:64 * a + 3 * HD + 1, :, :].bitcast(F32),
                                     neg_max_t[PAIRS * a:PAIRS * a + PAIRS, :].bitcast(F32))\
                            .then_inc(max_rows_set.sem, 16)
                if row.before().exists():
                    store(row.before())
                    sp.wait_ge(y_read.sem, y_read.at(row.before(), 1))
                    sp.nop(nofuse=True)
                sp.dma_start(gb[:, :], gates[one_row(row), D:2 * D].broadcast_to((P, D))).then_inc(gb_loaded.sem, 16)

            attention(Row(0))
            with sp.Fori(0, B - 2) as r:
                attention(Row(r, 1))
            attention(Row(B - 1))
            store(Row(B - 1))
            sp.wait_ge(stored.sem, stored.at(Row(B - 1), 0))

        @block.gpsimd
        def _(pool):
            steps = 0

            def step(instruction):
                nonlocal steps
                steps += 1
                instruction.then_inc(pool_step, 1)

            step(pool.memset(ident[:, :], 0.0))
            step(pool.memset(band[:, :], 0.0))
            step(pool.memset(earlier[:, :, :], 1.0))
            step(pool.memset(expert_rows[:, :, :].bitcast(F32), 0.0))
            step(pool.memset(minus_half[:, :, :], -0.5))
            pool.wait_ge(pool_step, steps)
            step(pool.affine_select(out=ident[:, :], in_=ident[:, :], compare_op=ALU.not_equal, fill=1.0,
                                    base=0, pattern=[[-1, P]], channel_multiplier=1))
            step(pool.affine_select(out=band[:, 0:P], in_=band[:, 0:P], compare_op=ALU.is_gt, fill=-BIG,
                                    base=0, pattern=[[1, P]], channel_multiplier=-1))
            step(pool.affine_select(out=band[:, P:2 * P], in_=band[:, P:2 * P], compare_op=ALU.is_ge, fill=-BIG,
                                    base=0, pattern=[[-1, P]], channel_multiplier=1))
            step(pool.affine_select(out=earlier[:, :, :], in_=earlier[:, :, :], compare_op=ALU.is_gt, fill=0.0,
                                    base=0, pattern=[[1, E], [-1, E]], channel_multiplier=0))
            for part in range(2):
                step(pool.affine_select(out=expert_rows[:, :, :], in_=expert_rows[:, :, :].bitcast(F32),
                                        compare_op=ALU.not_equal, fill=0.5, base=-E * part,
                                        pattern=[[-1, E], [0, HID]], channel_multiplier=1))
                pool.wait_ge(pool_step, steps)
            pool.sem_inc(constants, 1)

            def layer_norm(row, which):
                pool.wait_ge(stats_ready[which].sem, stats_ready[which].at(row, 0))
                pool.nop(nofuse=True)
                pool.tensor_scalar(variance[:, :], moments[:, :, 1], LN_EPS, None, ALU.add).then_inc(var_ready[which].sem, 1)
                pool.wait_ge(var_ready[which].sem, var_ready[which].at(row, 0))
                pool.tensor_tensor(rstd[:, :], variance[:, :], minus_half[:, :, 0], ALU.pow)\
                    .then_inc(rstd_ready[which].sem, 1)

            def early_tile(row, t):
                pool.wait_ge(qk_weighted.sem, qk_weighted.at(row, t))
                if t >= 2:
                    pool.wait_ge(rotated.sem, rotated.at(row, t - 2))
                pool.tensor_tensor(
                    heads(by_sin[:, t % 2, :]), heads(weighted[:, t % 2, :]),
                    sin[:, t, :].unsqueeze(1).broadcast_to((P, 4 * NH, HD // 2)), ALU.mult).then_inc(sin_done.sem, 1)
                pool.wait_ge(v_mid.sem, v_mid.at(row, t))
                pool.tensor_tensor(v_parts[:, t, :, 2 * HD:3 * HD], v_rest[:, t % 2, :, :],
                                   v_parts[:, t, :, HD:2 * HD], ALU.subtract).then_inc(v_done.sem, 1)
                if t % 2:
                    two = slice(t - 1, t + 1)
                    pool.wait_ge(squares.sem, squares.at(row, t))
                    pool.nop(nofuse=True)
                    pool.tensor_scalar(meansq[:, two, :], sumsq[:, two, :], 1.0 / D, RMS_EPS, ALU.mult, ALU.add)\
                        .then_inc(qk_var_ready.sem, 1)
                    pool.wait_ge(qk_var_ready.sem, qk_var_ready.at(row, t // 2))
                    pool.tensor_tensor(qk_rstd[:, two, :], meansq[:, two, :], minus_half[:, two, :], ALU.pow)\
                        .then_inc(qk_rstd_ready.sem, 1)

            def mask_unit(row, unit):
                nq = queries(unit)
                pool.wait_ge(exped.sem, exped.at(row, 2 * unit + 1))
                pool.nop(nofuse=True)
                own = probs[:, unit % 2, :, 0:P]
                ins = pool.affine_select(out=own, in_=own, compare_op=ALU.is_ge, fill=0.0, base=0,
                                         pattern=[[0, 4], [1, P]], channel_multiplier=-1)
                if nq > P:
                    late = probs[:, unit % 2, :, P:2 * P]
                    ins = pool.affine_select(out=late, in_=late, compare_op=ALU.is_gt, fill=0.0, base=0,
                                             pattern=[[0, 4], [-1, P]], channel_multiplier=1)
                ins.then_inc(masked.sem, 1)

            def attention(row, place):
                next_row = row.after()
                for t in range(T):
                    for n in range(2):
                        run(place, ("tile", t, n))
                run(place, ("gap",))
                for u in range(END):
                    if u < NU:
                        mask_unit(row, u)
                    if 1 <= u <= NU and (u - 1) % UNITS in ON_POOL:
                        low_probs(pool, row, u - 1, p_lo_pool)
                    if u == STATS_AT and next_row.exists():
                        layer_norm(next_row, 0)
                    run(place, ("unit", u))
                    t = u - NU - 3
                    if 0 <= t < T and next_row.exists():
                        early_tile(next_row, t)
                    if u == OUT_AT + T + 1:
                        layer_norm(row, 1)

            def split_piece(place):
                n, odd = divmod(place, 2)
                if odd or n >= PIECES:
                    return
                pool.wait_ge(piece_hi, n + 1)
                a, z = n * PIECE, (n + 1) * PIECE
                low = w12_lo[:, a:z] if z <= WCOLS else w3_lo[:, a - WCOLS:z - WCOLS]
                pool.tensor_tensor(low, raw_ffn[:, n % 2, :], w_hi[:, a:z].bitcast(F32),
                                   ALU.subtract).then_inc(piece_lo, 1)

            def experts(f, place):
                c, odd = divmod(place - 3, 2)
                if 0 <= c < NC and not odd:
                    pool.wait_ge(g_hi_out.sem, g_hi_out.at(f, c))
                    y_before(pool, f, c)
                    pool.tensor_tensor(g_lo[:, c % 2, :], gated[:, c % 2, :], g_hi[:, c % 2, :].bitcast(F32),
                                       ALU.subtract).then_inc(g_lo_out.sem, 1)

            layer_norm(Row(0), 0)
            for t in range(T):
                early_tile(Row(0), t)
            attention(Row(0), split_piece)
            g_lo_out.grant(pool)
            with pool.Fori(0, B - 2) as r:
                attention(Row(r, 1), lambda place: experts(Row(r, 0), place))
            attention(Row(B - 1), lambda place: experts(Row(B - 2), place))
            for place in range(PLACES):
                experts(Row(B - 1), place)

        @block.scalar
        def _(act):
            act.wait_ge(mod_loaded, 16 * (1 + KD))
            act.activation(ct_tmp[:, :, :], ct[:, :, :], ACT.Exp, scale=-1.0).then_inc(silu_exp, 1)

            def load_piece(n):
                act.dma_start(raw_ffn[:, n % 2, :], w_ffn[:, n * PIECE:(n + 1) * PIECE])\
                    .then_inc(piece_loaded[n % 2], 16)

            act.wait_ge(mod_full, 1)
            for n in range(2):
                load_piece(n)

            def modulate(row, which):
                for k in range(KD):
                    job = ("ln", k) if which else ("early ln", k)
                    if which:
                        act.wait_ge(ring_full.sem, ring_full.at(row, JOB[job]))
                    else:
                        act.wait_ge(early_full.sem, early_full.at(row, EARLY_JOB[job]))
                    if k >= 1:
                        act.wait_ge(h_split[which].sem, h_split[which].at(row, k - 1))
                    b = one_row(row)
                    act.activation(h_f32[:, :], bank(job)[:, :], ACT.Identity,
                                   scale=cmod[:, 2 * which, k, b], bias=cmod[:, 2 * which + 1, k, b])\
                        .then_inc(modulated[which].sem, 1)

            def early_tile(row, t):
                act.wait_ge(early_full.sem, early_full.at(row, EARLY_JOB[("qk", t)]))
                if t >= 1:
                    act.wait_ge(squares.sem, squares.at(row, t - 1))
                for s in range(2):
                    ins = act.activation(square[:, s, :], bank(("qk", t))[:, s * D:(s + 1) * D], ACT.Square,
                                         accum_out=sumsq[:, t, s:s + 1])
                ins.then_inc(squares.sem, 1)
                act.wait_ge(early_full.sem, early_full.at(row, EARLY_JOB[("v", t)]))
                act.activation(v_parts[:, t, :, 0:HD],
                               bank(("v", t))[:, 0:D].rearrange("p (h d) -> p h d", d=HD), ACT.Copy)\
                    .then_inc(v_hi.sem, 1)

            def v_middle(row, t):
                act.wait_ge(v_sub.sem, v_sub.at(row, t))
                act.activation(v_parts[:, t, :, HD:2 * HD], v_rest[:, t % 2, :, :], ACT.Copy).then_inc(v_mid.sem, 1)

            def max_out(row, half):
                act.wait_ge(ring_full.sem, ring_full.at(row, JOB[("mT", half)]))
                act.activation(neg_max_t, bank(("mT", half))[0:HH, :], ACT.Copy, scale=-1.0).then_inc(max_t_out.sem, 1)

            def attention(row, place, start_experts):
                next_row = row.after()
                high_qk(row, 0, 0)
                high_qk(row, 0, 1)
                for t in range(T):
                    transposed_out(row, 0, t)
                    if t == 0:
                        start_experts()
                    run(place, ("tile", t, 0))
                    high_qk(row, *divmod(t + 2, T))
                    run(place, ("tile", t, 1))
                transposed_out(row, 1, 0)
                max_out(row, 0)
                high_qk(row, 1, 2)
                transposed_out(row, 1, 1)
                high_qk(row, 1, 3)
                run(place, ("gap",))
                for u in range(END):
                    if u < NU:
                        exp_unit(row, u)
                    if 1 <= u <= NU:
                        high_probs(row, u - 1)
                    if u in TURN_AT:
                        transposed_out(row, 1, TURN_AT[u])
                    if u == MAX_ROWS_AT:
                        max_out(row, 1)
                    run(place, ("unit", u))
                    if 0 <= u - OUT_AT < T:
                        t = u - OUT_AT
                        act.wait_ge(ring_full.sem, ring_full.at(row, JOB[("oT", t)]))
                        act.activation(attn_t[:, t % 2, 0, :, :],
                                       bank(("oT", t))[:, 0:D].rearrange("p (k c) -> p k c", k=KD), ACT.Copy)\
                            .then_inc(attn_t_hi.sem, 1)
                    if next_row.exists():
                        if u == NU:
                            modulate(next_row, 0)
                        if 0 <= u - NU - 3 < T:
                            early_tile(next_row, u - NU - 3)
                        if 0 <= u - NU - 4 < T:
                            v_middle(next_row, u - NU - 4)
                if next_row.exists():
                    v_middle(next_row, T - 1)
                modulate(row, 1)
                act.wait_ge(ring_full.sem, ring_full.at(row, JOB[("lg",)]))
                act.activation(logits_t, bank(("lg",))[0:E, :], ACT.Copy).then_inc(logits_t_out.sem, 1)
                act.wait_ge(shifted_out.sem, shifted_out.at(row, 0))
                act.activation(exps[:, :, :], shifted[:, :, :], ACT.Exp).then_inc(exps_out.sem, 1)

            def start_experts(f):
                act.wait_ge(route_turned.sem, route_turned.at(f, 0))
                act.activation(route_t[:, :], ps_w[0:2 * E, :], ACT.Copy).then_inc(route_t_out.sem, 1)

            def high_qk(row, half, t):
                slot = (half * T + t) % 2
                if half == 0 and t % 2 == 0:
                    act.wait_ge(qk_rstd_ready.sem, qk_rstd_ready.at(row, t // 2))
                act.wait_ge(rotated.sem, rotated.at(row, t))
                if half * T + t >= 2:
                    act.wait_ge(ring_full.sem, ring_full.at(row, JOB[("kT", *divmod(half * T + t - 2, T))]))
                for s, dst in ((0, q_parts[:, slot, :, 0:2 * HD].rearrange("p h (r d) -> p h r d", r=2)),
                               (1, k_parts[:, slot, :, :].rearrange("p h (r d) -> p h r d", d=HD)[:, :, 0:3:2, :])):
                    src = rot[:, 2 * s + half, t, :].rearrange("p (h d) -> p h d", d=HD)
                    ins = act.activation(dst, src.unsqueeze(2).broadcast_to((P, HH, 2, HD)), ACT.Copy,
                                         scale=qk_rstd[:, t, s:s + 1])
                ins.then_inc(qk_hi.sem, 1)

            def transposed_out(row, half, t):
                at = slice(t * P, (t + 1) * P)
                for job, dst, done in (("qT", q_t[half][:, :, at], q_t_out), ("kT", k_t[half][:, :, at], k_t_out)):
                    act.wait_ge(ring_full.sem, ring_full.at(row, JOB[(job, half, t)]))
                    act.activation(dst, bank((job, half, t))[:, :].rearrange("p (a c) -> p a c", a=PAIRS), ACT.Copy)\
                        .then_inc(done.sem, 1)

            def exp_unit(row, unit):
                nq = queries(unit)
                for a in range(2):
                    act.wait_ge(ring_full.sem, ring_full.at(row, JOB[("st", unit, a)]))
                    if a == 0:
                        if unit >= 2:
                            p_lo_wait(act, row, unit - 2)
                        elif row.before().exists():
                            p_lo_wait(act, row.before(), NU - 2 + unit)
                    act.activation(probs[:, unit % 2, 2 * a:2 * a + 2, 0:nq],
                                   bank(("st", unit, a))[:, :].rearrange("p (r c) -> p r c", r=2)[:, :, 0:nq],
                                   ACT.Exp).then_inc(exped.sem, 1)

            def high_probs(row, unit):
                nq = queries(unit)
                act.wait_ge(masked.sem, masked.at(row, unit))
                if unit >= 2:
                    act.wait_ge(ring_full.sem, ring_full.at(row, JOB[("pv", unit - 2)]))
                act.activation(p_hi[:, unit % 3, :, 0:nq], probs[:, unit % 2, :, 0:nq], ACT.Copy)\
                    .then_inc(p_hi_out.sem, 1)

            def split_piece(place):
                n, odd = divmod(place, 2)
                if odd or n >= PIECES:
                    return
                act.wait_ge(piece_loaded[n % 2], 16 * (n // 2 + 1))
                act.activation(w_hi[:, n * PIECE:(n + 1) * PIECE], raw_ffn[:, n % 2, :],
                               ACT.Copy).then_inc(piece_hi, 1)
                if 1 <= n < PIECES - 1:
                    act.wait_ge(piece_lo, n)
                    load_piece(n + 1)

            def experts(f, place):
                c, odd = divmod(place, 2)
                if odd:
                    return
                if 1 <= c <= NC:
                    m = c - 1
                    act.wait_ge(w_read.sem, w_read.at(f, m))
                    y_before(act, f, m)
                    act.activation(g_hi[:, m % 2, :], gated[:, m % 2, :], ACT.Copy).then_inc(g_hi_out.sem, 1)
                if c < NC:
                    act.wait_ge(ffn_full.sem, ffn_full.at(f, 3 * c))
                    if c >= 2:
                        act.wait_ge(g_lo_out.sem, g_lo_out.at(f, c - 2))
                    else:
                        act.wait_ge(g_lo_out.sem, g_lo_out.at(f.before(), last_on(2, c, NC)))
                    act.activation(gated[:, c % 2, :], ps_a[:, :], ACT.Tanh, scale=0.5).then_inc(tanh_out.sem, 1)

            modulate(Row(0), 0)
            for t in range(T):
                early_tile(Row(0), t)
                v_middle(Row(0), t)
            attention(Row(0), split_piece, lambda: None)
            with act.Fori(0, B - 2) as r:
                f = Row(r, 0)
                attention(Row(r, 1), lambda place: experts(f, place), lambda: start_experts(f))
            f = Row(B - 2)
            attention(Row(B - 1), lambda place: experts(f, place), lambda: start_experts(f))
            start_experts(Row(B - 1))
            for place in range(PLACES):
                experts(Row(B - 1), place)

        @block.vector
        def _(dve):
            steps = 0

            def start(instruction):
                nonlocal steps
                steps += 1
                instruction.then_inc(start_step, 1)
                dve.wait_ge(start_step, steps)

            dve.wait_ge(silu_exp, 1)
            start(dve.tensor_scalar(ct_tmp[:, :, :], ct_tmp[:, :, :], 1.0, None, ALU.add))
            start(dve.reciprocal(ct_tmp[:, :, :], ct_tmp[:, :, :]))
            dve.tensor_tensor(ct[:, :, :], ct[:, :, :], ct_tmp[:, :, :], ALU.mult).then_inc(silu_done, 1)
            for parts in (q_parts, k_parts):
                dve.memset(parts[:, :, :, 3 * HD:64].bitcast(F32), 0.0)
            dve.memset(v_parts[:, :, :, 3 * HD:V3], 1.0)
            dve.wait_ge(consts_loaded, 64)
            start(dve.tensor_scalar(norm_w[:, 0:D], norm_w[:, 0:D], HD ** -0.5, None, ALU.mult))
            start(dve.memset(k_parts[:, :, :, 3 * HD:3 * HD + 1].bitcast(F32), 1.0))
            dve.wait_ge(w_loaded, 48)
            for raw, w in ((raw_qkv, wqkv), (raw_o, wo), (wg_raw, wg)):
                start(dve.tensor_copy(w[:, 0, :, :], raw[:, :, :]))
                ins = dve.tensor_tensor(w[:, 1, :, :], raw[:, :, :], w[:, 0, :, :].bitcast(F32), ALU.subtract)
            ins.then_inc(weights_split, 1)
            dve.wait_ge(mod_full, 1)
            start(dve.tensor_copy(cmod[:, :, :, :], ring[0][:, 0:4 * KD * B].rearrange("p (m k b) -> p m k b", m=4, k=KD)))
            for m in (0, 2):
                ins = dve.tensor_scalar(cmod[:, m, :, :], cmod[:, m, :, :], 1.0, None, ALU.add)
            ins.then_inc(mod_out, 1)
            g = ring[1][0:B, :]
            dve.tensor_scalar(gate_rows[1], g, 0.0, None, ALU.is_ge)
            dve.tensor_scalar(gate_rows[2], g, 0.25, None, ALU.max)
            start(dve.tensor_scalar(gate_rows[0], g, -0.25, None, ALU.min))
            start(dve.tensor_tensor(gate_rows[2], gate_rows[2], gate_rows[0], ALU.subtract))
            start(dve.tensor_tensor(gate_rows[1], gate_rows[1], gate_rows[2], ALU.mult))
            dve.tensor_tensor(gate_rows[0], gate_rows[0], gate_rows[1], ALU.add).then_inc(mod_out, 1)
            dve.wait_ge(constants, 1)

            def counted(event, row, count):
                done = 0

                def step(instruction):
                    nonlocal done
                    assert done < count
                    instruction.then_inc(event.sem, 1)
                    dve.wait_ge(event.sem, event.at(row, done))
                    done += 1
                return step

            def ln_stats(row, which, src, step):
                for t in range(T):
                    ins = dve.bn_stats(stats[:, t, :], src[:, t, :])
                step(ins)
                dve.nop(nofuse=True)
                for t in range(T):
                    ins = dve.bn_aggr(moments[:, t, :], stats[:, t, :])
                ins.then_inc(stats_ready[which].sem, 1)

            def ln_normalise(row, which, src):
                dve.wait_ge(stats_ready[which].sem, stats_ready[which].at(row, 0))
                dve.wait_ge(rstd_ready[which].sem, rstd_ready[which].at(row, 0))
                for t in range(T):
                    ins = dve.tensor_scalar(xn[:, t, :], src[:, t, :], moments[:, t, 0:1], rstd[:, t:t + 1],
                                            ALU.subtract, ALU.mult)
                ins.then_inc(normed[which].sem, 1)

            def ln_split(row, which, step):
                h = (h1, h2)[which]
                for k in range(KD):
                    dve.wait_ge(modulated[which].sem, modulated[which].at(row, k))
                    if which == 1:
                        dve.tensor_copy(h2_bf[:, k, :], h_f32[:, :])
                    step(dve.tensor_copy(h[:, 0, k, :], h_f32[:, :]))
                    dve.tensor_tensor(h[:, 1, k, :], h_f32[:, :], h[:, 0, k, :].bitcast(F32), ALU.subtract)\
                        .then_inc(h_split[which].sem, 1)

            def early_tile(row, t, step):
                w2 = weighted[:, t % 2, :]
                dve.wait_ge(squares.sem, squares.at(row, t))
                if t >= 2:
                    dve.wait_ge(sin_done.sem, sin_done.at(row, t - 2))
                dve.tensor_tensor(w2, bank(("qk", t))[:, :], norm_w[:, :], ALU.mult).then_inc(qk_weighted.sem, 1)
                dve.wait_ge(v_hi.sem, v_hi.at(row, t))
                if t >= 2:
                    dve.wait_ge(v_done.sem, v_done.at(row, t - 2))
                dve.tensor_tensor(v_rest[:, t % 2, :, :], bank(("v", t))[:, 0:D].rearrange("p (h d) -> p h d", d=HD),
                                  v_parts[:, t, :, 0:HD], ALU.subtract).then_inc(v_sub.sem, 1)
                dve.wait_ge(qk_weighted.sem, qk_weighted.at(row, t))
                step(dve.tensor_tensor(rot[:, :, t, :].rearrange("p b (h d) -> p b h d", d=HD // 2),
                                       w2.rearrange("p (b h d) -> p b h d", d=HD // 2, b=4),
                                       cos[:, t, :].unsqueeze(1).unsqueeze(1).broadcast_to((P, 4, NH, HD // 2)), ALU.mult))

            def early_turn(row, t):
                dve.wait_ge(sin_done.sem, sin_done.at(row, t))
                a, z = (rot[:, :, t, :].rearrange("p b (h s d) -> p b h s d", s=2, d=HD // 2)[:, :, :, s, :]
                        for s in range(2))
                sa, sz = (by_sin[:, t % 2, :].rearrange("p (b h s d) -> p b h s d", b=4, s=2, d=HD // 2)[:, :, :, s, :]
                          for s in range(2))
                dve.tensor_tensor(a, a, sz, ALU.subtract)
                dve.tensor_tensor(z, z, sa, ALU.add).then_inc(rotated.sem, 1)

            def residual(row, t):
                if t == 0:
                    dve.wait_ge(x_loaded.sem, x_loaded.at(row, 1))
                dve.wait_ge(ring_full.sem, ring_full.at(row, JOB[("op", t)]))
                dve.tensor_tensor(gated_proj[:, t % 2, :], bank(("op", t))[:, 0:D], ga[:, :], ALU.mult)\
                    .then_inc(proj_read.sem, 1)
                dve.wait_ge(proj_read.sem, proj_read.at(row, t))
                if t == 0 and row.before().exists():
                    dve.wait_ge(stored.sem, stored.at(row.before(), 0))
                dve.tensor_tensor(x1[:, t, :], gated_proj[:, t % 2, :], x_sb[:, t, :], ALU.add)\
                    .then_inc(resid.sem, 1)

            def attention(row, place, finish):
                next_row = row.after()
                early, late = counted(early_step, next_row, EARLY_STEPS), counted(late_step, row, LATE_STEPS)
                low_qk(row, 0, 0)
                low_qk(row, 0, 1)
                for t in range(T):
                    run(place, ("tile", t, 0))
                    if t >= 1:
                        maxima(row, 0, t - 1)
                    low_qk(row, *divmod(t + 2, T))
                    run(place, ("tile", t, 1))
                maxima(row, 0, T - 1)
                low_qk(row, 1, 2)
                maxima(row, 1, 0)
                low_qk(row, 1, 3)
                run(place, ("gap",))
                for u in range(END):
                    if 1 <= u <= NU and (u - 1) % UNITS not in ON_POOL:
                        low_probs(dve, row, u - 1, p_lo_dve)
                    if PV_LAG <= u < NU + PV_LAG:
                        attend(row, u - PV_LAG)
                    if u in MAX_AT:
                        maxima(row, 1, MAX_AT[u])
                    if next_row.exists():
                        if u == STATS_AT:
                            dve.wait_ge(x_early_loaded.sem, x_early_loaded.at(next_row, 0))
                            ln_stats(next_row, 0, x_early, early)
                        if u == NORM_AT:
                            ln_normalise(next_row, 0, x_early)
                    run(place, ("unit", u))
                    if u == OUT_AT + 1:
                        finish()
                    if 0 <= u - OUT_AT - 2 < T:
                        residual(row, u - OUT_AT - 2)
                    if 0 <= u - OUT_AT < T:
                        t = u - OUT_AT
                        dve.wait_ge(attn_t_hi.sem, attn_t_hi.at(row, t))
                        dve.tensor_tensor(attn_t[:, t % 2, 1, :, :],
                                          bank(("oT", t))[:, 0:D].rearrange("p (k c) -> p k c", k=KD),
                                          attn_t[:, t % 2, 0, :, :].bitcast(F32), ALU.subtract).then_inc(attn_t_lo.sem, 1)
                    if u == NU and next_row.exists():
                        ln_split(next_row, 0, early)
                    if u - OUT_AT - 2 == T - 1:
                        dve.wait_ge(resid.sem, resid.at(row, T - 1))
                        ln_stats(row, 1, x1, late)
                    if next_row.exists() and 0 <= u - NU - 3 < T:
                        early_tile(next_row, u - NU - 3, early)
                        early_turn(next_row, u - NU - 3)
                ln_normalise(row, 1, x1)
                ln_split(row, 1, late)
                route_row(row, late)

            def low_qk(row, half, t):
                slot = (half * T + t) % 2
                dve.wait_ge(qk_hi.sem, qk_hi.at(row, half * T + t))
                for s, parts, at in ((0, q_parts, 2), (1, k_parts, 1)):
                    src = rot[:, 2 * s + half, t, :].rearrange("p (h d) -> p h d", d=HD)
                    ins = dve.scalar_tensor_tensor(
                        out=parts[:, slot, :, at * HD:(at + 1) * HD], in0=src, scalar=qk_rstd[:, t, s:s + 1],
                        in1=parts[:, slot, :, 0:HD].bitcast(F32), op0=ALU.mult, op1=ALU.subtract)
                ins.then_inc(qk_lo.sem, 1)

            def maxima(row, half, t):
                nk = 2 * P if t else P
                for u in range(2 * G):
                    g, a = divmod(u, 2)
                    dve.wait_ge(ring_full.sem, ring_full.at(row, JOB[("max", half, t, u)]))
                    dve.nop(nofuse=True)
                    for r in range(2):
                        m = PAIRS * a + 2 * g + r
                        scores = bank(("max", half, t, u))[:, 2 * P * r:2 * P * r + nk]
                        ins = dve.tensor_tensor_reduce(scores, scores, band[:, 2 * P - nk:2 * P], 1.0, -3e38, ALU.add,
                                                       ALU.max, row_max[:, half, t, m:m + 1])
                    ins.then_inc(maxed.sem, 1)

            def attend(row, unit):
                t, slot = unit % T, unit % 2
                dve.wait_ge(ring_full.sem, ring_full.at(row, JOB[("pv", unit)]))
                sums = bank(("pv", unit))[:, 0:4 * V3].rearrange("p (h c) -> p h c", c=V3)
                dve.reciprocal(pv_rden[:, slot, :], sums[:, :, V3 - 1])
                dve.tensor_reduce(pv_sum[:, slot, :, :], sums[:, :, 0:3 * HD].rearrange("p h (s d) -> p h d s", s=3),
                                  AX_X, ALU.add).then_inc(pv_read.sem, 1)
                dve.wait_ge(pv_read.sem, pv_read.at(row, unit))
                h = unit // T * 4
                dve.tensor_tensor(attn[:, t, h:h + 4, :], pv_sum[:, slot, :, :],
                                  pv_rden[:, slot, :].unsqueeze(2).broadcast_to((P, 4, HD)), ALU.mult).then_inc(attn_out.sem, 1)

            def route_row(row, step):
                dve.wait_ge(ring_full.sem, ring_full.at(row, JOB[("lgT",)]))
                dve.tensor_copy(logits[:, :, :], bank(("lgT",))[:, 0:T * E].rearrange("p (t e) -> p t e", e=E))\
                    .then_inc(logits_out.sem, 1)
                dve.wait_ge(logits_out.sem, logits_out.at(row, 0))
                step(dve.tensor_reduce(top1[:, :], logits[:, :, :], AX_X, ALU.max))
                dve.tensor_tensor(shifted[:, :, :], logits[:, :, :], top1[:, :].unsqueeze(2).broadcast_to((P, T, E)),
                                  ALU.subtract).then_inc(shifted_out.sem, 1)
                other = logits[:, :, :].unsqueeze(2).broadcast_to((P, T, E, E))
                own = logits[:, :, :].unsqueeze(3).broadcast_to((P, T, E, E))
                dve.tensor_tensor(beats[:, :, :, :], other, own, ALU.is_gt)
                step(dve.tensor_tensor(ties[:, :, :, :], other, own, ALU.is_equal))
                step(dve.tensor_tensor(ties[:, :, :, :], ties[:, :, :, :],
                                       earlier[:, :, :].unsqueeze(1).broadcast_to((P, T, E, E)), ALU.mult))
                step(dve.tensor_tensor(beats[:, :, :, :], beats[:, :, :, :], ties[:, :, :, :], ALU.add))
                step(dve.tensor_reduce(rank[:, :, :], beats[:, :, :, :], AX_X, ALU.add))
                step(dve.tensor_scalar(rank[:, :, :], rank[:, :, :], 1.5, None, ALU.is_lt))
                dve.wait_ge(exps_out.sem, exps_out.at(row, 0))
                step(dve.tensor_tensor(route[:, :, :], exps[:, :, :], rank[:, :, :], ALU.mult))
                step(dve.tensor_reduce(route_sum[:, :], route[:, :, :], AX_X, ALU.add))
                step(dve.reciprocal(route_sum[:, :], route_sum[:, :]))
                step(dve.tensor_tensor(route[:, :, :], route[:, :, :],
                                       route_sum[:, :].unsqueeze(2).broadcast_to((P, T, E)), ALU.mult))
                step(dve.tensor_copy(route_parts[:, :, 0, :], route[:, :, :]))
                dve.tensor_tensor(route_parts[:, :, 1, :], route[:, :, :], route_parts[:, :, 0, :].bitcast(F32),
                                  ALU.subtract).then_inc(route_out.sem, 1)

            def experts(f, place):
                c, odd = divmod(place, 2)
                if not odd or c >= NC:
                    return
                g = gated[:, c % 2, :]
                dve.wait_ge(tanh_out.sem, tanh_out.at(f, c))
                dve.scalar_tensor_tensor(out=g, in0=g, scalar=1.0, in1=ps_a[:, :], op0=ALU.add, op1=ALU.mult)\
                    .then_inc(a_read.sem, 1)
                dve.wait_ge(a_read.sem, a_read.at(f, c))
                dve.wait_ge(ffn_full.sem, ffn_full.at(f, 3 * c + 1))
                dve.tensor_tensor(g, g, ps_b[:, :], ALU.mult).then_inc(b_read.sem, 1)
                dve.wait_ge(b_read.sem, b_read.at(f, c))
                dve.wait_ge(ffn_full.sem, ffn_full.at(f, 3 * c + 2))
                dve.tensor_tensor(g, g, ps_w[:, :], ALU.mult).then_inc(w_read.sem, 1)

            def finish(f):
                dve.wait_ge(y_done.sem, y_done.at(f, NC - 1))
                dve.wait_ge(gb_loaded.sem, gb_loaded.at(f, 0))
                for b in range(2):
                    if b:
                        dve.wait_ge(final.sem, final.at(f, 0))
                    dve.tensor_tensor(y_gated[:, :, :], ps_y[b][:, :].rearrange("p (t c) -> p t c", t=2),
                                      gb[:, :].unsqueeze(1).broadcast_to((P, 2, D)), ALU.mult).then_inc(y_read.sem, 1)
                    dve.wait_ge(y_read.sem, y_read.at(f, b))
                    dve.tensor_tensor(x1[:, 2 * b:2 * b + 2, :], x1[:, 2 * b:2 * b + 2, :], y_gated[:, :, :], ALU.add)\
                        .then_inc(final.sem, 1)

            early = counted(early_step, Row(0), EARLY_STEPS)
            dve.wait_ge(x_early_loaded.sem, x_early_loaded.at(Row(0), 0))
            ln_stats(Row(0), 0, x_early, early)
            ln_normalise(Row(0), 0, x_early)
            ln_split(Row(0), 0, early)
            for t in range(T):
                early_tile(Row(0), t, early)
                early_turn(Row(0), t)
            attention(Row(0), lambda place: None, lambda: None)
            for read in (a_read, b_read, w_read, y_read):
                read.grant(dve)
            with dve.Fori(0, B - 2) as r:
                f = Row(r, 0)
                attention(Row(r, 1), lambda place: experts(f, place), lambda: finish(f))
            f = Row(B - 2)
            attention(Row(B - 1), lambda place: experts(f, place), lambda: finish(f))
            for place in range(PLACES):
                experts(Row(B - 1), place)
            finish(Row(B - 1))

        @block.tensor
        def _(pe):
            pe.wait_ge(silu_done, 1)
            for m, chunk in enumerate((1, 0, 4, 3)):
                for k in range(KD):
                    at = (m * KD + k) * B
                    for j in range(KD):
                        c = chunk * D + k * P
                        pe.matmul(ring[0][:, at:at + B], raw_mod[j][:, c:c + P], ct[:, j, :],
                                  start=(j == 0), stop=(j == KD - 1))
            for m, chunk in enumerate((2, 5)):
                for j in range(KD):
                    ins = pe.matmul(ring[1][0:B, m * D:(m + 1) * D], ct[:, j, :],
                                    raw_mod[j][:, chunk * D:(chunk + 1) * D], start=(j == 0), stop=(j == KD - 1))
            ins.then_inc(mod_full, 1)
            pe.wait_ge(constants, 1)
            pe.wait_ge(weights_split, 1)
            pe.wait_ge(mod_out, 2)

            SPLIT = ((0, 0), (0, 1), (1, 0))

            def products(dst, stationary, moving, signal=None):
                for k in range(KD):
                    for n, (s, m) in enumerate(SPLIT):
                        ins = pe.matmul(dst, stationary(s, k), moving(m, k), start=(k == 0 and n == 0),
                                        stop=(k == KD - 1 and n == len(SPLIT) - 1))
                return ins

            def layer_norm_transposes(row, which):
                pe.wait_ge(normed[which].sem, normed[which].at(row, 0))
                now = row if which else row.before()
                for k in range(KD):
                    job = ("ln", k) if which else ("early ln", k)
                    bank_free(pe, now, job)
                    for t in range(T):
                        ins = pe.transpose(bank(job)[:, t * P:(t + 1) * P], xn[:, t, k * P:(k + 1) * P], ident[:, :])
                    ins.then_inc((ring_full if which else early_full).sem, 1)

            def project(row, t):
                if t == 0:
                    pe.wait_ge(h_split[0].sem, h_split[0].at(row, KD - 1))
                tokens = slice(t * P, (t + 1) * P)
                for job, a, z in ((("qk", t), 0, 2 * D), (("v", t), 2 * D, 3 * D)):
                    bank_free(pe, row.before(), job)
                    products(bank(job)[:, 0:z - a], lambda s, k: h1[:, s, k, tokens],
                             lambda m, k: wqkv[:, m, k, a:z]).then_inc(early_full.sem, 1)

            def turn_maxima(row, half):
                bank_free(pe, row, ("mT", half))
                pe.wait_ge(maxed.sem, maxed.at(row, (half * T + T) * 2 * G - 1))
                for t in range(T):
                    ins = pe.transpose(bank(("mT", half))[0:HH, t * P:(t + 1) * P], row_max[:, half, t, :], ident[:, :])
                ins.then_inc(ring_full.sem, 1)

            def attention(row, place, start_experts):
                next_row = row.after()
                for t in range(T):
                    transpose_qk(row, 0, t)
                    if t == 0:
                        start_experts()
                    run(place, ("tile", t, 0))
                    if t >= 1:
                        query_scores(row, 0, t - 1)
                    run(place, ("tile", t, 1))
                query_scores(row, 0, T - 1)
                transpose_qk(row, 1, 0)
                turn_maxima(row, 0)
                transpose_qk(row, 1, 1)
                query_scores(row, 1, 0)
                run(place, ("gap",))
                for u in range(END):
                    if u < NU:
                        if u % UNITS == 0:
                            pe.wait_ge(max_rows_set.sem, max_rows_set.at(row, 2 * (u // UNITS) + 1))
                        for a in range(2):
                            key_scores(row, u, a)
                    if PV_LAG <= u < NU + PV_LAG:
                        probs_times_v(row, u - PV_LAG)
                    if u in TURN_AT:
                        transpose_qk(row, 1, TURN_AT[u])
                    if u in MAX_AT:
                        query_scores(row, 1, MAX_AT[u])
                    if u == MAX_ROWS_AT:
                        turn_maxima(row, 1)
                    run(place, ("unit", u))
                    if 0 <= u - OUT_AT - 2 < T:
                        job, slot = ("op", u - OUT_AT - 2), u % 2
                        pe.wait_ge(attn_t_lo.sem, attn_t_lo.at(row, u - OUT_AT - 2))
                        bank_free(pe, row, job)
                        products(bank(job)[:, 0:D], lambda s, k: attn_t[:, slot, s, k, :],
                                 lambda m, k: wo[:, m, k, :]).then_inc(ring_full.sem, 1)
                    if 0 <= u - OUT_AT < T:
                        t = u - OUT_AT
                        job = ("oT", t)
                        pe.wait_ge(attn_out.sem, attn_out.at(row, NU - T + t))
                        bank_free(pe, row, job)
                        for k in range(KD):
                            ins = pe.transpose(bank(job)[:, k * P:(k + 1) * P],
                                               attn[:, t, k * HH:(k + 1) * HH, :].rearrange("p h d -> p (h d)"), ident[:, :])
                        ins.then_inc(ring_full.sem, 1)
                    if next_row.exists():
                        if u == NU:
                            layer_norm_transposes(next_row, 0)
                        if 0 <= u - NU - 3 < T:
                            project(next_row, u - NU - 3)
                layer_norm_transposes(row, 1)
                pe.wait_ge(h_split[1].sem, h_split[1].at(row, KD - 1))
                bank_free(pe, row, ("lg",))
                products(bank(("lg",))[0:E, :], lambda s, k: wg[:, s, k, :], lambda m, k: h2[:, m, k, :])\
                    .then_inc(ring_full.sem, 1)
                bank_free(pe, row, ("lgT",))
                pe.wait_ge(logits_t_out.sem, logits_t_out.at(row, 0))
                pe.nop(nofuse=True)
                for t in range(T):
                    ins = pe.transpose(bank(("lgT",))[:, t * E:(t + 1) * E], logits_t[:, t * P:(t + 1) * P],
                                       ident[0:E, 0:E])
                ins.then_inc(ring_full.sem, 1)

            def start_experts(f):
                pe.wait_ge(route_out.sem, route_out.at(f, 0))
                pe.wait_ge(w_read.sem, w_read.at(f.before(), NC - 1))
                for t in range(T):
                    ins = pe.transpose(ps_w[0:2 * E, t * P:(t + 1) * P],
                                       route_parts[:, t, :, :].rearrange("p s e -> p (s e)").bitcast(F32), ident[:, :])
                ins.then_inc(route_turned.sem, 1)

            def transpose_qk(row, half, t):
                slot = (half * T + t) % 2
                pe.wait_ge(qk_lo.sem, qk_lo.at(row, half * T + t))
                for job, parts in (("qT", q_parts), ("kT", k_parts)):
                    bank_free(pe, row, (job, half, t))
                    for p in range(PAIRS):
                        ins = pe.transpose(bank((job, half, t))[:, p * P:(p + 1) * P],
                                           parts[:, slot, 2 * p:2 * p + 2, :].rearrange("p h c -> p (h c)").bitcast(F32),
                                           ident[:, :])
                    ins.then_inc(ring_full.sem, 1)

            def query_scores(row, half, t):
                pe.wait_ge(k_t_out.sem, k_t_out.at(row, half * T + t))
                first = max(t - 1, 0)
                nk = (t + 1 - first) * P
                for u in range(2 * G):
                    g, a = divmod(u, 2)
                    job, rows = ("max", half, t, u), slice(64 * a, 64 * a + 64)
                    bank_free(pe, row, job)
                    for r in range(2):
                        ins = pe.matmul(bank(job)[:, 2 * P * r:2 * P * r + nk], q_t[half][rows, 2 * g + r, t * P:(t + 1) * P],
                                        k_t[half][rows, 2 * g + r, first * P:(t + 1) * P], start=True, stop=True)
                    ins.then_inc(ring_full.sem, 1)

            def key_scores(row, unit, a):
                half, n = divmod(unit, UNITS)
                (g, j), nq, rows = divmod(n, T), queries(n), slice(64 * a, 64 * a + 64)
                job = ("st", unit, a)
                bank_free(pe, row, job)
                for r in range(2):
                    ins = pe.matmul(bank(job)[:, 2 * P * r:2 * P * r + nq], k_t[half][rows, 2 * g + r, j * P:(j + 1) * P],
                                    q_t[half][rows, 2 * g + r, j * P:j * P + nq], start=True, stop=True)
                ins.then_inc(ring_full.sem, 1)

            def probs_times_v(row, unit):
                job, t = ("pv", unit), unit % T
                if unit == 0:
                    pe.wait_ge(v_done.sem, v_done.at(row, T - 1))
                p_lo_wait(pe, row, unit)
                bank_free(pe, row, job)
                for h in range(4):
                    r, a = divmod(h, 2)
                    todo = [(p, u, at) for u, at in ([(unit - 1, P)] if t else []) + [(unit, 0)] for p in (p_hi, p_lo)]
                    for i, (p, u, at) in enumerate(todo):
                        tile = t - (at > 0)
                        ins = pe.matmul(bank(job)[:, h * V3:(h + 1) * V3], p[:, u % 3, 2 * a + r, at:at + P],
                                        v_parts[:, tile, unit // T * 4 + h, :],
                                        start=(i == 0), stop=(i == len(todo) - 1))
                ins.then_inc(ring_full.sem, 1)

            def hidden(f, c):
                for n, (dst, free) in enumerate(((ps_a, a_read), (ps_b, b_read))):
                    if c:
                        pe.wait_ge(free.sem, free.at(f, c - 1))
                    else:
                        pe.wait_ge(free.sem, free.at(f.before(), NC - 1))
                    for k in range(KD):
                        at = k * 2 * FH + n * FH + c * P
                        first, last = k == 0, k == KD - 1
                        pe.matmul(dst[:, :], w_hi[:, at:at + P], h2[:, 0, k, :], start=first, stop=False)
                        pe.matmul(dst[:, :], w_hi[:, at:at + P], h2[:, 1, k, :], start=False, stop=False)
                        ins = pe.matmul(dst[:, :], w12_lo[:, at:at + P], h2_bf[:, k, :], start=False, stop=last)
                    ins.then_inc(ffn_full.sem, 1)
                if c:
                    pe.wait_ge(w_read.sem, w_read.at(f, c - 1))
                else:
                    pe.wait_ge(w_read.sem, w_read.at(f.before(), NC - 1))
                    pe.wait_ge(route_t_out.sem, route_t_out.at(f, 0))
                pe.matmul(ps_w[:, :], few_rows[0:2 * E, :][:, c * P:(c + 1) * P], route_t[:, :],
                          start=True, stop=True).then_inc(ffn_full.sem, 1)

            def add_to_y(f, c):
                pe.wait_ge(g_lo_out.sem, g_lo_out.at(f, c))
                if c == 0:
                    pe.wait_ge(y_read.sem, y_read.at(f.before(), 1))
                w3_hi = w_hi[:, WCOLS + c * D:WCOLS + (c + 1) * D]
                for t in range(T):
                    tokens = slice(t * P, (t + 1) * P)
                    for n, (g, w) in enumerate(((g_hi, w3_hi), (g_hi, w3_lo[:, c * D:(c + 1) * D]), (g_lo, w3_hi))):
                        ins = pe.matmul(ps_y[t // 2][:, t % 2 * D:(t % 2 + 1) * D], g[:, c % 2, tokens], w,
                                        start=(c == 0 and n == 0 and t % 2 == 0), stop=(c == NC - 1 and n == 2),
                                        skip_group_check=True)
                ins.then_inc(y_done.sem, 1)

            def experts(f, place):
                if place % 2 == 0 and place // 2 < NC:
                    hidden(f, place // 2)
                if place % 2 and place >= 5:
                    add_to_y(f, (place - 5) // 2)

            layer_norm_transposes(Row(0), 0)
            for t in range(T):
                project(Row(0), t)
            attention(Row(0), lambda place: None, lambda: None)
            y_done.grant(pe)
            pe.wait_ge(piece_hi, PIECES)
            pe.wait_ge(piece_lo, PIECES)
            with pe.Fori(0, B - 2) as r:
                f = Row(r, 0)
                attention(Row(r, 1), lambda place: experts(f, place), lambda: start_experts(f))
            f = Row(B - 2)
            attention(Row(B - 1), lambda place: experts(f, place), lambda: start_experts(f))
            start_experts(Row(B - 1))
            for place in range(PLACES):
                experts(Row(B - 1), place)


def kernel(L0_attn_hidden_states, L0_attn_w_qkv, L0_attn_q_norm_w, L0_attn_k_norm_w, L0_attn_w_o,
           L0_ffn_Wg, L0_ffn_W1, L0_ffn_W2, L0_ffn_W3, L0_c, L0_wmod):
    import concourse.bacc as bacc
    from concourse.bass_utils import run_bass_kernel_spmd

    def by_contraction(w):
        return np.ascontiguousarray(np.transpose(np.asarray(w).reshape(w.shape[0], -1, P), (2, 1, 0)))

    w12 = by_contraction(np.concatenate([np.asarray(L0_ffn_W1).reshape(FH, D), np.asarray(L0_ffn_W2).reshape(FH, D)]))
    w3 = by_contraction(np.transpose(np.asarray(L0_ffn_W3), (1, 0, 2)).reshape(D, FH))
    angles = np.arange(S, dtype=np.float32)[:, None] * (
        1.0 / 10000.0 ** (np.arange(0, HD, 2, dtype=np.float32) / np.float32(HD))).astype(np.float32)[None, :]
    rope = np.stack([np.cos(angles), np.sin(angles)]).astype(np.float32)
    arrays = {
        "x": np.ascontiguousarray(np.asarray(L0_attn_hidden_states).reshape(B, T, P, D).transpose(0, 2, 1, 3)),
        "w_qkv_t": by_contraction(L0_attn_w_qkv),
        "q_norm": np.asarray(L0_attn_q_norm_w).reshape(1, D),
        "k_norm": np.asarray(L0_attn_k_norm_w).reshape(1, D),
        "w_o_t": by_contraction(L0_attn_w_o),
        "w_g_t": by_contraction(L0_ffn_Wg),
        "w_ffn": np.concatenate([w12.reshape(P, WCOLS), w3.reshape(P, W3COLS)], axis=1),
        "c_t": by_contraction(L0_c),
        "w_mod": np.ascontiguousarray(np.asarray(L0_wmod).reshape(KD, P, 6 * D)),
        "rope": np.ascontiguousarray(rope.reshape(2, T, P, HD // 2).transpose(0, 2, 1, 3)),
    }
    nc = bacc.Bacc("TRN2", target_bir_lowering=False, num_devices=1,
                   dynamic_dma_scratch_size=1024)
    args = {n: nc.dram_tensor("in_" + n, a.shape, mybir.dt.from_np(a.dtype), kind="ExternalInput").ap()
            for n, a in arrays.items()}
    gates = nc.dram_tensor("gates", (B, 2 * D), F32).ap()
    out = nc.dram_tensor("out", (B, P, T, D), F32, kind="ExternalOutput").ap()
    build(nc, **args, gates=gates, out=out)
    r = run_bass_kernel_spmd(nc, [{"in_" + n: a for n, a in arrays.items()}], core_ids=[0])
    got = r.results[0]["out"]
    return got.transpose(0, 2, 1, 3).reshape(B, S, D)
```

```python
from contextlib import ExitStack

import numpy as np

import concourse.bass as bass
from concourse import mybir

F32 = mybir.dt.float32
F32R = mybir.dt.float32r
BF16 = mybir.dt.bfloat16
F16 = mybir.dt.float16
ACT = mybir.ActivationFunctionType
ALU = mybir.AluOpType
AX_X = mybir.AxisListType.X

P = 128
B, S, D = 8, 512, 256
T = S // P
KD = D // P
NH, HD = 16, 16
WINDOW = 128
E, HID = 8, 176
FH = E * HID
NC = FH // P
HALVES = 2
HH = NH // HALVES
PAIRS = HH // 2
G = 2
UNITS = G * T
V3 = 3 * HD + 1
RING = 4
PIECES = NC + 1
PLACES = 2 * NC + 4
PV_LAG = 2
ON_POOL = (0, 1, 3, 4, 7)
EARLY_STEPS = 1 + T
LATE_STEPS = 1
ROUTE_STEPS = 11
WCOLS = 2 * FH * KD
W3COLS = NC * D
PIECE = (WCOLS + W3COLS) // PIECES
LN_EPS, RMS_EPS = 1e-5, 1e-6
BIG = 1e30

NU = HALVES * UNITS
TURN_AT = {0: 2, 2: 3}
MAX_AT = {1: 1, 3: 2, 5: 3}
MAX_ROWS_AT = 6
STATS_AT, NORM_AT = 7, 11
OUT_AT = NU
END = NU + T + 3


POINTS = [("tile", 1, 1), ("tile", 1, 1), ("tile", 2, 1), ("tile", 3, 0), ("tile", 3, 1), ("gap",)]
POINTS += [("unit", u) for u in (1, 3, 5, 6, 7, 8, 10, 13, 14, 16, 18, 18, 19, 20, 22, 22)]
POINTS += [("end", 0), ("end", 1), ("end", 1), ("end", 1)]
assert len(POINTS) == PLACES and ("end", 1) not in POINTS[:2 * NC - 1]


def places_at(point):
    return [n for n, at in enumerate(POINTS) if at == point]


def ring_jobs():
    def queries(half, t):
        return [("max", half, t, u) for u in range(2 * G)]

    def turned(half, t):
        return [("qT", half, t), ("kT", half, t)]

    jobs = []
    for t in range(T):
        jobs += turned(0, t)
        if t >= 1:
            jobs += queries(0, t - 1)
    jobs += queries(0, T - 1) + turned(1, 0) + [("mT", 0)] + turned(1, 1) + queries(1, 0)
    for u in range(END):
        if u < NU:
            jobs += [("st", u, a) for a in range(2)]
        if PV_LAG <= u < NU + PV_LAG:
            jobs += [("pv", u - PV_LAG)]
        if u in MAX_AT:
            jobs += queries(1, MAX_AT[u])
        if u in TURN_AT:
            jobs += turned(1, TURN_AT[u])
        if u == MAX_ROWS_AT:
            jobs += [("mT", 1)]
        if 0 <= u - OUT_AT - 2 < T:
            jobs += [("op", u - OUT_AT - 2)]
        if 0 <= u - OUT_AT < T:
            jobs += [("oT", u - OUT_AT)]
        if u == NU:
            jobs += [("early ln", k) for k in range(KD)]
        if 0 <= u - NU - 3 < T:
            jobs += [("qk", u - NU - 3), ("v", u - NU - 3)]
    jobs += [("ln", k) for k in range(KD)]
    return jobs


JOBS = ring_jobs()
SLOT = {job: n for n, job in enumerate(JOBS)}
EARLY = ("early ln", "qk", "v")
EARLY_JOB = {job: n for n, job in enumerate(j for j in JOBS if j[0] in EARLY)}
JOB = {job: n for n, job in enumerate(j for j in JOBS if j[0] not in EARLY)}


class Row:

    def __init__(self, base, shift=0):
        self.base, self.shift = base, shift

    def before(self):
        return Row(self.base, self.shift - 1)

    def after(self):
        return Row(self.base, self.shift + 1)

    def index(self):
        return self.base + self.shift

    def exists(self):
        return not isinstance(self.base, int) or 0 <= self.base + self.shift < B


class Event:

    def __init__(self, sem, per_row, step=1, ahead=0):
        self.sem, self.per_row, self.step, self.ahead = sem, per_row, step, ahead

    def grant(self, eng):
        eng.sem_inc(self.sem, self.per_row * self.step)

    def at(self, row, k):
        more = ((row.shift + self.ahead) * self.per_row + k + 1) * self.step
        return row.base * (self.per_row * self.step) + more


def last_on(ring, slot, count):
    return max(n for n in range(count) if n % ring == slot)


def build(nc, x, w_qkv_t, q_norm, k_norm, w_o_t, w_g_t, w_ffn, c_t, w_mod, rope, gates, out):
    ctx = ExitStack()
    with ctx:
        def sb(name, shape, dt=F32):
            return ctx.enter_context(nc.sbuf_tensor(name, shape, dt))

        def before(name, shape):
            with nc.sbuf_tensor(name, shape, F32) as buffer:
                return buffer

        def psum(name):
            return ctx.enter_context(nc.psum_tensor(name, [P, 512], F32))

        def sem(name):
            return ctx.enter_context(nc.semaphore(name))

        def event(name, per_row, step=1, ahead=0):
            return Event(sem(name), per_row, step, ahead)

        w_hi = sb("w_hi", [P, WCOLS + W3COLS], F32R)
        w12_lo = sb("w12_lo", [P, WCOLS], BF16)
        w3_lo = sb("w3_lo", [P, W3COLS], F32R)
        wqkv = sb("wqkv", [P, 2, KD, 3 * D], F32R)
        wo = sb("wo", [P, 2, KD, D], F32R)
        wg = sb("wg", [P, 2, KD, E], F32R)
        wg_raw = sb("wg_raw", [P, KD, E])
        ident = sb("ident", [P, P])
        band = sb("band", [P, 2 * P])
        band_t = sb("band_t", [P, 2, 2 * P], BF16)
        ident_bf = sb("ident_bf", [P, P], BF16)
        few_rows = sb("few_rows", [P, FH], F32R)
        expert_rows = few_rows[0:2 * E, :].rearrange("p (e r) -> p e r", e=E)
        neg_max_t = few_rows[64:64 + HH, 0:S]
        earlier = sb("earlier", [P, E, E])
        minus_half = sb("minus_half", [P, T, 2])
        cos = sb("cos", [P, T, HD // 2])
        sin = sb("sin", [P, T, HD // 2])
        norm_w = sb("norm_w", [P, 2 * D])
        ct = sb("ct", [P, KD, B])
        ct_tmp = sb("ct_tmp", [P, KD, B])
        cmod = sb("cmod", [P, 4, KD, B])
        x_early = sb("x_early", [P, T, D])
        x_sb = sb("x_sb", [P, T, D])
        xn = sb("xn", [P, T, D])
        x1 = sb("x1", [P, T, D])
        ga = sb("ga", [P, D])
        gb = sb("gb", [P, D])
        stats = sb("stats", [P, T, 6])
        moments = sb("moments", [P, T, 2])
        variance = sb("variance", [P, T])
        rstd = sb("rstd", [P, T])
        h_f32 = sb("h_f32", [P, S])
        h1 = sb("h1", [P, 2, KD, S], F32R)
        raw_mod0 = before("raw_mod0", [P, 6 * D])
        h2 = sb("h2", [P, 2, KD, S], F32R)
        h2_bf = sb("h2_bf", [P, KD, S], BF16)
        square = sb("square", [P, 2, D])
        logits_t = square.rearrange("p s c -> p (s c)")[0:E, :]
        sumsq = sb("sumsq", [P, T, 2])
        meansq = sb("meansq", [P, T, 2])
        qk_rstd = sb("qk_rstd", [P, T, 2])
        weighted = sb("weighted", [P, 2, 2 * D])
        by_sin = sb("by_sin", [P, 2, 2 * D])
        rot = before("rot", [P, 2 * HALVES, T, P])
        q_t_2 = sb("q_t_2", [P, PAIRS, S], F32R)
        q_parts = sb("q_parts", [P, 2, HH, 64], F32R)
        k_parts = sb("k_parts", [P, 2, HH, 64], F32R)
        q_t = [sb("q_t", [P, PAIRS, S], F32R)[:, :, :], q_t_2[:, :, :]]
        k_t = [sb("k_t", [P, PAIRS, S], F32R)[:, :, :], h1.rearrange("p s k c -> p (s k) c")]
        v_parts = sb("v_parts", [P, T, NH, V3], BF16)
        v_rest = sb("v_rest", [P, 2, NH, HD])
        row_max = sb("row_max", [P, HALVES, T, HH])
        probs = sb("probs", [P, 2, 4, 2 * P])
        p_hi = sb("p_hi", [P, 3, 4, 2 * P], F16)
        p_lo = sb("p_lo", [P, 3, 4, 2 * P], F16)
        pv_sum = sb("pv_sum", [P, 2, 4, HD])
        pv_rden = sb("pv_rden", [P, 2, 4])
        attn = sb("attn", [P, T, NH, HD])
        attn_t = sb("attn_t", [P, 2, 2, KD, P], F32R)
        gated_proj = sb("gated_proj", [P, 2, D])
        logits = sb("logits", [P, T, E])
        top1 = sb("top1", [P, T])
        shifted = sb("shifted", [P, T, E])
        exps = sb("exps", [P, T, E])
        beats = sb("beats", [P, T, E, E])
        ties = sb("ties", [P, T, E, E])
        rank = sb("rank", [P, T, E])
        route_sum = sb("route_sum", [P, T])
        route = sb("route", [P, T, E])
        route_parts = sb("route_parts", [P, T, 2, E], F32R)
        route_t = sb("route_t", [2 * E, S], F32R)
        gated = sb("gated", [P, 2, S])
        raw_ffn = before("raw_ffn", [P, 2, PIECE])
        w_spread = sb("w_spread", [P, 2, S])
        g_hi = sb("g_hi", [P, 2, S], F32R)
        g_lo = sb("g_lo", [P, 2, S], F32R)

        raw_qkv = rot.rearrange("p b t c -> p (b t c)")[:, 0:KD * 3 * D].rearrange("p (k c) -> p k c", k=KD)
        raw_o = attn.rearrange("p t h d -> p (t h d)")[:, 0:KD * D].rearrange("p (k c) -> p k c", k=KD)
        raw_mod = [raw_mod0[:, :], probs.rearrange("p r h c -> p (r h c)")[:, 0:6 * D]]

        flat = x1.rearrange("p t c -> p (t c)")
        gate_rows = [gated_proj.rearrange("p t c -> p (t c)")[0:B, :], flat[0:B, 0:2 * D], flat[0:B, 2 * D:4 * D]]

        ring = [psum(f"ring{n}") for n in range(RING)]
        ps_a, ps_b = psum("ps_a"), psum("ps_b")
        ps_y = [psum("ps_y0"), psum("ps_y1")]

        gated_y = [by_sin[:, b, :].rearrange("p (t c) -> p t c", t=2) for b in range(2)]
        pairs = [(ps_a, ps_b)] * 2
        spare_pairs = [(ps_a, ps_b), (ring[0], ring[1])]

        c_loaded = sem("c_loaded")
        mod_loaded = sem("mod_loaded")
        consts_loaded = sem("consts_loaded")
        w_loaded = sem("w_loaded")
        ident_ready = sem("ident_ready")
        constants = sem("constants")
        pool_step = sem("pool_step")
        silu_exp = sem("silu_exp")
        start_step = sem("start_step")
        silu_done = sem("silu_done")
        mod_full = sem("mod_full")
        mod_out = sem("mod_out")
        weights_split = sem("weights_split")
        gates_stored = sem("gates_stored")
        piece_loaded = [sem("piece_loaded0"), sem("piece_loaded1")]
        piece_hi = sem("piece_hi")
        piece_lo = sem("piece_lo")

        x_early_loaded = event("x_early_loaded", 1, 16)
        x_loaded = event("x_loaded", 2, 16)
        gb_loaded = event("gb_loaded", 1, 16)
        max_rows_set = event("max_rows_set", 4, 16)
        kept = event("kept", 1)
        h_short = event("h_short", KD)
        stored = event("stored", 1, 16, ahead=1)
        ring_full = event("ring_full", len(JOB))
        early_full = event("early_full", len(EARLY_JOB))
        stats_ready = [event(f"stats_ready{n}", 1) for n in range(2)]
        var_ready = [event(f"var_ready{n}", 1) for n in range(2)]
        rstd_ready = [event(f"rstd_ready{n}", 1) for n in range(2)]
        normed = [event(f"normed{n}", 1) for n in range(2)]
        modulated = [event(f"modulated{n}", KD) for n in range(2)]
        h_split = [event(f"h_split{n}", KD) for n in range(2)]
        qk_var_ready = event("qk_var_ready", 2)
        qk_rstd_ready = event("qk_rstd_ready", 2)
        squares = event("squares", T)
        qk_weighted = event("qk_weighted", T)
        sin_done = event("sin_done", T)
        rotated = event("rotated", T)
        v_hi = event("v_hi", T)
        v_sub = event("v_sub", T)
        v_mid = event("v_mid", T)
        v_done = event("v_done", T)
        qk_hi = event("qk_hi", HALVES * T)
        qk_lo = event("qk_lo", HALVES * T)
        q_t_out = event("q_t_out", HALVES * T)
        k_t_out = event("k_t_out", HALVES * T)
        maxed = event("maxed", HALVES * T * 2 * G)
        max_t_out = event("max_t_out", HALVES)
        exped = event("exped", HALVES * UNITS * 2)
        p_hi_out = event("p_hi_out", HALVES * UNITS)
        p_lo_pool = event("p_lo_pool", HALVES * len(ON_POOL))
        p_lo_dve = event("p_lo_dve", HALVES * (UNITS - len(ON_POOL)))
        pv_read = event("pv_read", HALVES * UNITS)
        attn_out = event("attn_out", HALVES * UNITS)
        attn_t_hi = event("attn_t_hi", T)
        attn_t_lo = event("attn_t_lo", T)
        proj_read = event("proj_read", T)
        resid = event("resid", T)
        logits_t_out = event("logits_t_out", 1)
        logits_out = event("logits_out", 1)
        shifted_out = event("shifted_out", 1)
        exps_out = event("exps_out", 1)
        route_out = event("route_out", 1)
        route_t_out = event("route_t_out", 1)
        router_full = event("router_full", 3)
        ffn_full = event("ffn_full", 3 * NC)
        w_out = event("w_out", NC)
        y_done = event("y_done", NC, ahead=1)
        tanh_out = event("tanh_out", NC)
        a_read = event("a_read", NC, ahead=1)
        b_read = event("b_read", NC, ahead=1)
        weighed = event("weighed", NC, ahead=1)
        g_hi_out = event("g_hi_out", NC)
        g_lo_out = event("g_lo_out", NC, ahead=1)
        y_read = event("y_read", 2, ahead=1)
        final = event("final", 2)
        early_step = event("early_step", EARLY_STEPS)
        late_step = event("late_step", LATE_STEPS)
        route_step = event("route_step", ROUTE_STEPS)

        def p_lo_wait(eng, row, unit):
            half, n = divmod(unit, UNITS)
            if n in ON_POOL:
                eng.wait_ge(p_lo_pool.sem, p_lo_pool.at(row, half * len(ON_POOL) + ON_POOL.index(n)))
            else:
                on_dve = [m for m in range(UNITS) if m not in ON_POOL]
                eng.wait_ge(p_lo_dve.sem, p_lo_dve.at(row, half * len(on_dve) + on_dve.index(n)))

        def bank(job):
            return ring[SLOT[job] % RING]

        def bank_free(eng, row, job):
            n = SLOT[job]
            while True:
                n -= RING
                if n < 0:
                    row, n = row.before(), last_on(RING, SLOT[job] % RING, len(JOBS))
                if not row.exists() and not row.after().exists():
                    return
                kind, *at = JOBS[n]
                if (row.after() if kind in EARLY else row).exists():
                    break
            next_row = row.after()
            if kind == "early ln":
                eng.wait_ge(modulated[0].sem, modulated[0].at(next_row, at[0]))
            if kind == "ln":
                eng.wait_ge(modulated[1].sem, modulated[1].at(row, at[0]))
            if kind == "qk":
                eng.wait_ge(qk_weighted.sem, qk_weighted.at(next_row, at[0]))
            if kind == "v":
                eng.wait_ge(v_sub.sem, v_sub.at(next_row, at[0]))
            if kind == "qT":
                eng.wait_ge(q_t_out.sem, q_t_out.at(row, at[0] * T + at[1]))
            if kind == "kT":
                eng.wait_ge(k_t_out.sem, k_t_out.at(row, at[0] * T + at[1]))
            if kind == "max":
                eng.wait_ge(maxed.sem, maxed.at(row, (at[0] * T + at[1]) * 2 * G + at[2]))
            if kind == "mT":
                eng.wait_ge(max_t_out.sem, max_t_out.at(row, at[0]))
            if kind == "st":
                eng.wait_ge(exped.sem, exped.at(row, at[0] * 2 + at[1]))
            if kind == "pv":
                eng.wait_ge(pv_read.sem, pv_read.at(row, at[0]))
            if kind == "oT":
                eng.wait_ge(attn_t_lo.sem, attn_t_lo.at(row, at[0]))
            if kind == "op":
                eng.wait_ge(proj_read.sem, proj_read.at(row, at[0]))

        def queries(n):
            return 2 * P if n % T < T - 1 else P

        def heads(qk):
            return qk.rearrange("p (h d) -> p h d", d=HD // 2)

        def y_before(eng, f, m):
            if m >= 2:
                eng.wait_ge(y_done.sem, y_done.at(f, m - 2))
            else:
                eng.wait_ge(y_done.sem, y_done.at(f.before(), last_on(2, m, NC)))

        def low_probs(eng, row, unit, done):
            nq = queries(unit)
            eng.wait_ge(p_hi_out.sem, p_hi_out.at(row, unit))
            eng.tensor_tensor(p_lo[:, unit % 3, :, 0:nq], probs[:, unit % 2, :, 0:nq], p_hi[:, unit % 3, :, 0:nq],
                              ALU.subtract).then_inc(done.sem, 1)

        def one_row(row):
            b = row.index()
            return slice(b, b + 1) if isinstance(b, int) else bass.ds(b, 1)

        def run(place, point):
            for n in places_at(point):
                place(n)

        block = ctx.enter_context(nc.Block())

        @block.sync
        def _(sp):
            sp.dma_start(ct[:, :, :], c_t).then_inc(c_loaded, 16)
            sp.dma_start(x_early[:, :, :], x[0]).then_inc(x_early_loaded.sem, 16)
            for k in range(KD):
                sp.dma_start(raw_mod[k], w_mod[k]).then_inc(mod_loaded, 16)
            sp.dma_start(raw_qkv, w_qkv_t).then_inc(w_loaded, 16)
            sp.dma_start(raw_o, w_o_t).then_inc(w_loaded, 16)
            sp.dma_start(wg_raw[:, :, :], w_g_t).then_inc(w_loaded, 16)
            sp.dma_start(cos[:, :, :], rope[0]).then_inc(consts_loaded, 16)
            sp.dma_start(sin[:, :, :], rope[1]).then_inc(consts_loaded, 16)
            sp.dma_start(norm_w[:, 0:D], q_norm.broadcast_to((P, D))).then_inc(consts_loaded, 16)
            sp.dma_start(norm_w[:, D:2 * D], k_norm.broadcast_to((P, D))).then_inc(consts_loaded, 16)
            sp.wait_ge(mod_out, 2)
            sp.dma_start(gates[:, :], gate_rows[0]).then_inc(gates_stored, 16)
            sp.wait_ge(gates_stored, 16)

            def store(prev):
                sp.wait_ge(final.sem, final.at(prev, 1))
                sp.nop(nofuse=True)
                sp.dma_start(out[prev.index()], x1[:, :, :]).then_inc(stored.sem, 16)

            def attention(row):
                if row.after().exists():
                    sp.wait_ge(normed[0].sem, normed[0].at(row, 0))
                    sp.nop(nofuse=True)
                    sp.dma_start(x_early[:, :, :], x[row.after().index()]).then_inc(x_early_loaded.sem, 16)
                if row.before().exists():
                    sp.wait_ge(kept.sem, kept.at(row.before(), 0))
                    sp.nop(nofuse=True)
                sp.dma_start(x_sb[:, :, :], x[row.index()]).then_inc(x_loaded.sem, 16)
                sp.dma_start(ga[:, :], gates[one_row(row), 0:D].broadcast_to((P, D))).then_inc(x_loaded.sem, 16)
                for half in range(HALVES):
                    sp.wait_ge(max_t_out.sem, max_t_out.at(row, half))
                    for a in range(2):
                        sp.dma_start(q_t[half][64 * a + 3 * HD:64 * a + 3 * HD + 1, :, :].bitcast(F32),
                                     neg_max_t[PAIRS * a:PAIRS * a + PAIRS, :].bitcast(F32))\
                            .then_inc(max_rows_set.sem, 16)
                if row.before().exists():
                    store(row.before())
                    sp.wait_ge(y_read.sem, y_read.at(row.before(), 1))
                    sp.nop(nofuse=True)
                sp.dma_start(gb[:, :], gates[one_row(row), D:2 * D].broadcast_to((P, D))).then_inc(gb_loaded.sem, 16)

            attention(Row(0))
            stored.grant(sp)
            with sp.Fori(0, B - 2) as r:
                attention(Row(r, 1))
            attention(Row(B - 1))
            store(Row(B - 1))
            sp.wait_ge(stored.sem, stored.at(Row(B - 1), 0))

        @block.gpsimd
        def _(pool):
            steps = 0

            def step(instruction):
                nonlocal steps
                steps += 1
                instruction.then_inc(pool_step, 1)

            def layer_norm(row, which):
                pool.wait_ge(stats_ready[which].sem, stats_ready[which].at(row, 0))
                pool.nop(nofuse=True)
                pool.tensor_scalar(variance[:, :], moments[:, :, 1], LN_EPS, None, ALU.add).then_inc(var_ready[which].sem, 1)
                pool.wait_ge(var_ready[which].sem, var_ready[which].at(row, 0))
                pool.tensor_tensor(rstd[:, :], variance[:, :], minus_half[:, :, 0], ALU.pow)\
                    .then_inc(rstd_ready[which].sem, 1)

            step(pool.memset(minus_half[:, :, :], -0.5))
            step(pool.memset(ident[:, :], 0.0))
            pool.wait_ge(pool_step, steps)
            step(pool.affine_select(out=ident[:, :], in_=ident[:, :], compare_op=ALU.not_equal, fill=1.0,
                                    base=0, pattern=[[-1, P]], channel_multiplier=1))
            pool.wait_ge(pool_step, steps)
            pool.sem_inc(ident_ready, 1)
            layer_norm(Row(0), 0)
            step(pool.memset(band[:, :], 0.0))
            step(pool.memset(band_t[:, :, :], 0.0))
            step(pool.memset(earlier[:, :, :], 1.0))
            step(pool.memset(expert_rows[:, :, :].bitcast(F32), 0.0))
            pool.wait_ge(pool_step, steps)
            step(pool.affine_select(out=band[:, 0:P], in_=band[:, 0:P], compare_op=ALU.is_gt, fill=-BIG,
                                    base=0, pattern=[[1, P]], channel_multiplier=-1))
            step(pool.affine_select(out=band[:, P:2 * P], in_=band[:, P:2 * P], compare_op=ALU.is_ge, fill=-BIG,
                                    base=0, pattern=[[-1, P]], channel_multiplier=1))
            step(pool.affine_select(out=earlier[:, :, :], in_=earlier[:, :, :], compare_op=ALU.is_gt, fill=0.0,
                                    base=0, pattern=[[1, E], [-1, E]], channel_multiplier=0))
            step(pool.affine_select(out=band_t[:, :, 0:P], in_=band_t[:, :, 0:P], compare_op=ALU.is_ge, fill=-BIG,
                                    base=0, pattern=[[0, 2], [1, P]], channel_multiplier=-1))
            step(pool.affine_select(out=band_t[:, :, P:2 * P], in_=band_t[:, :, P:2 * P], compare_op=ALU.is_gt, fill=-BIG,
                                    base=0, pattern=[[0, 2], [-1, P]], channel_multiplier=1))
            pool.wait_ge(pool_step, steps)
            step(pool.tensor_copy(ident_bf[:, :], ident[:, :]))
            for part in range(2):
                step(pool.affine_select(out=expert_rows[:, :, :], in_=expert_rows[:, :, :].bitcast(F32),
                                        compare_op=ALU.not_equal, fill=0.5, base=-E * part,
                                        pattern=[[-1, E], [0, HID]], channel_multiplier=1))
                pool.wait_ge(pool_step, steps)
            pool.sem_inc(constants, 1)

            def early_tile(row, t):
                pool.wait_ge(qk_weighted.sem, qk_weighted.at(row, t))
                if t >= 2:
                    pool.wait_ge(rotated.sem, rotated.at(row, t - 2))
                pool.tensor_tensor(
                    heads(by_sin[:, t % 2, :]), heads(weighted[:, t % 2, :]),
                    sin[:, t, :].unsqueeze(1).broadcast_to((P, 4 * NH, HD // 2)), ALU.mult).then_inc(sin_done.sem, 1)
                pool.wait_ge(v_mid.sem, v_mid.at(row, t))
                pool.tensor_tensor(v_parts[:, t, :, 2 * HD:3 * HD], v_rest[:, t % 2, :, :],
                                   v_parts[:, t, :, HD:2 * HD], ALU.subtract).then_inc(v_done.sem, 1)
                if t % 2:
                    two = slice(t - 1, t + 1)
                    pool.wait_ge(squares.sem, squares.at(row, t))
                    pool.nop(nofuse=True)
                    pool.tensor_scalar(meansq[:, two, :], sumsq[:, two, :], 1.0 / D, RMS_EPS, ALU.mult, ALU.add)\
                        .then_inc(qk_var_ready.sem, 1)
                    pool.wait_ge(qk_var_ready.sem, qk_var_ready.at(row, t // 2))
                    pool.tensor_tensor(qk_rstd[:, two, :], meansq[:, two, :], minus_half[:, two, :], ALU.pow)\
                        .then_inc(qk_rstd_ready.sem, 1)

            def attention(row, place):
                next_row = row.after()
                for t in range(T):
                    for n in range(2):
                        run(place, ("tile", t, n))
                run(place, ("gap",))
                for u in range(END):
                    if u < NU and u % UNITS in ON_POOL:
                        low_probs(pool, row, u, p_lo_pool)
                    run(place, ("unit", u))
                    if u == STATS_AT and next_row.exists():
                        layer_norm(next_row, 0)
                    t = u - NU - 3
                    if 0 <= t < T and next_row.exists():
                        early_tile(next_row, t)
                    if u == OUT_AT + T + 1:
                        layer_norm(row, 1)
                for n in range(2):
                    run(place, ("end", n))
                shorten(row)

            def shorten(row):
                for k in range(KD):
                    pool.wait_ge(h_split[1].sem, h_split[1].at(row, k))
                    pool.nop(nofuse=True)
                    pool.tensor_copy(h2_bf[:, k, :], h2[:, 0, k, :].bitcast(F32)).then_inc(h_short.sem, 1)

            def keep(f):
                pool.wait_ge(resid.sem, resid.at(f, T - 1))
                pool.wait_ge(stored.sem, stored.at(f.before(), 0))
                pool.nop(nofuse=True)
                pool.tensor_copy(x1[:, :, :], x_sb[:, :, :]).then_inc(kept.sem, 1)

            def output(f):
                for b in range(2):
                    pool.wait_ge(y_read.sem, y_read.at(f, b))
                    pool.tensor_tensor(x1[:, 2 * b:2 * b + 2, :], x1[:, 2 * b:2 * b + 2, :], gated_y[b], ALU.add)\
                        .then_inc(final.sem, 1)

            def split_piece(place):
                n, odd = divmod(place, 2)
                if odd or n >= PIECES:
                    return
                pool.wait_ge(piece_hi, n + 1)
                a, z = n * PIECE, (n + 1) * PIECE
                low = w12_lo[:, a:z] if z <= WCOLS else w3_lo[:, a - WCOLS:z - WCOLS]
                pool.tensor_tensor(low, raw_ffn[:, n % 2, :], w_hi[:, a:z].bitcast(F32),
                                   ALU.subtract).then_inc(piece_lo, 1)

            def experts(f, place, pairs=pairs):
                c, odd = divmod(place - 1, 2)
                if c < NC and not odd:
                    pool.wait_ge(w_out.sem, w_out.at(f, c))
                    pool.wait_ge(b_read.sem, b_read.at(f, c))
                    pool.tensor_tensor(gated[:, c % 2, :], gated[:, c % 2, :], w_spread[:, c % 2, :], ALU.mult)\
                        .then_inc(weighed.sem, 1)
                c -= 1
                if 0 <= c < NC and not odd:
                    pool.wait_ge(g_hi_out.sem, g_hi_out.at(f, c))
                    y_before(pool, f, c)
                    pool.tensor_tensor(g_lo[:, c % 2, :], gated[:, c % 2, :], g_hi[:, c % 2, :].bitcast(F32),
                                       ALU.subtract).then_inc(g_lo_out.sem, 1)

            for t in range(T):
                early_tile(Row(0), t)
            attention(Row(0), split_piece)
            g_lo_out.grant(pool)
            weighed.grant(pool)
            with pool.Fori(0, B - 2) as r:
                f = Row(r, 0)
                keep(f)
                attention(Row(r, 1), lambda place: experts(f, place))
                output(f)
            f = Row(B - 2)
            keep(f)
            attention(Row(B - 1), lambda place: experts(f, place))
            output(f)
            f = Row(B - 1)
            keep(f)
            for place in range(PLACES):
                experts(f, place)
            output(f)

        @block.scalar
        def _(act):
            act.wait_ge(c_loaded, 16)
            act.activation(ct_tmp[:, :, :], ct[:, :, :], ACT.Exp, scale=-1.0).then_inc(silu_exp, 1)

            def load_piece(n):
                act.dma_start(raw_ffn[:, n % 2, :], w_ffn[:, n * PIECE:(n + 1) * PIECE])\
                    .then_inc(piece_loaded[n % 2], 16)

            act.wait_ge(mod_full, 1)
            for n in range(2):
                load_piece(n)

            def modulate(row, which):
                for k in range(KD):
                    job = ("ln", k) if which else ("early ln", k)
                    if which:
                        act.wait_ge(ring_full.sem, ring_full.at(row, JOB[job]))
                    else:
                        act.wait_ge(early_full.sem, early_full.at(row, EARLY_JOB[job]))
                    b = one_row(row)
                    act.activation((h1, h2)[which][:, 0, k, :], bank(job)[:, :], ACT.Identity,
                                   scale=cmod[:, 2 * which, k, b], bias=cmod[:, 2 * which + 1, k, b])
                    if k >= 1:
                        act.wait_ge(h_split[which].sem, h_split[which].at(row, k - 1))
                        act.nop(nofuse=True)
                    act.activation(h_f32[:, :], bank(job)[:, :], ACT.Identity,
                                   scale=cmod[:, 2 * which, k, b], bias=cmod[:, 2 * which + 1, k, b])\
                        .then_inc(modulated[which].sem, 1)

            def early_tile(row, t):
                act.wait_ge(early_full.sem, early_full.at(row, EARLY_JOB[("qk", t)]))
                if t >= 1:
                    act.wait_ge(squares.sem, squares.at(row, t - 1))
                for s in range(2):
                    ins = act.activation(square[:, s, :], bank(("qk", t))[:, s * D:(s + 1) * D], ACT.Square,
                                         accum_out=sumsq[:, t, s:s + 1])
                ins.then_inc(squares.sem, 1)
                act.wait_ge(early_full.sem, early_full.at(row, EARLY_JOB[("v", t)]))
                act.activation(v_parts[:, t, :, 0:HD],
                               bank(("v", t))[:, 0:D].rearrange("p (h d) -> p h d", d=HD), ACT.Copy)\
                    .then_inc(v_hi.sem, 1)

            def v_middle(row, t):
                act.wait_ge(v_sub.sem, v_sub.at(row, t))
                act.activation(v_parts[:, t, :, HD:2 * HD], v_rest[:, t % 2, :, :], ACT.Copy).then_inc(v_mid.sem, 1)

            def max_out(row, half):
                act.wait_ge(ring_full.sem, ring_full.at(row, JOB[("mT", half)]))
                act.activation(neg_max_t, bank(("mT", half))[0:HH, :], ACT.Copy, scale=-1.0).then_inc(max_t_out.sem, 1)

            def attention(row, place, routing):
                next_row = row.after()
                high_qk(row, 0, 0)
                routing(0)
                high_qk(row, 0, 1)
                for t in range(T):
                    run(place, ("tile", t, 0))
                    transposed_out(row, 0, t)
                    high_qk(row, *divmod(t + 2, T))
                    if t <= 1:
                        routing(1 + t)
                    run(place, ("tile", t, 1))
                transposed_out(row, 1, 0)
                max_out(row, 0)
                high_qk(row, 1, 2)
                transposed_out(row, 1, 1)
                high_qk(row, 1, 3)
                run(place, ("gap",))
                for u in range(END):
                    if u < NU:
                        exp_unit(row, u)
                        high_probs(row, u)
                    if u in TURN_AT:
                        transposed_out(row, 1, TURN_AT[u])
                    if u == MAX_ROWS_AT:
                        max_out(row, 1)
                    run(place, ("unit", u))
                    if 0 <= u - OUT_AT < T:
                        t = u - OUT_AT
                        act.wait_ge(ring_full.sem, ring_full.at(row, JOB[("oT", t)]))
                        act.activation(attn_t[:, t % 2, 0, :, :],
                                       bank(("oT", t))[:, 0:D].rearrange("p (k c) -> p k c", k=KD), ACT.Copy)\
                            .then_inc(attn_t_hi.sem, 1)
                    if next_row.exists():
                        if u == NU:
                            modulate(next_row, 0)
                        if 0 <= u - NU - 3 < T:
                            early_tile(next_row, u - NU - 3)
                        if 0 <= u - NU - 4 < T:
                            v_middle(next_row, u - NU - 4)
                if next_row.exists():
                    v_middle(next_row, T - 1)
                run(place, ("end", 0))
                modulate(row, 1)
                run(place, ("end", 1))

            def router(f, stage):
                if stage == 0:
                    act.wait_ge(router_full.sem, router_full.at(f, 0))
                    act.activation(logits_t, ps_a[0:E, :], ACT.Copy).then_inc(logits_t_out.sem, 1)
                if stage == 1:
                    act.wait_ge(shifted_out.sem, shifted_out.at(f, 0))
                    act.activation(exps[:, :, :], shifted[:, :, :], ACT.Exp).then_inc(exps_out.sem, 1)
                if stage == 2:
                    act.wait_ge(router_full.sem, router_full.at(f, 2))
                    act.activation(route_t[:, :], ps_a[0:2 * E, :], ACT.Copy).then_inc(route_t_out.sem, 1)

            def high_qk(row, half, t):
                slot = (half * T + t) % 2
                if half == 0 and t % 2 == 0:
                    act.wait_ge(qk_rstd_ready.sem, qk_rstd_ready.at(row, t // 2))
                act.wait_ge(rotated.sem, rotated.at(row, t))
                if half * T + t >= 2:
                    act.wait_ge(ring_full.sem, ring_full.at(row, JOB[("kT", *divmod(half * T + t - 2, T))]))
                for s, dst in ((0, q_parts[:, slot, :, 0:2 * HD].rearrange("p h (r d) -> p h r d", r=2)),
                               (1, k_parts[:, slot, :, :].rearrange("p h (r d) -> p h r d", d=HD)[:, :, 0:3:2, :])):
                    src = rot[:, 2 * s + half, t, :].rearrange("p (h d) -> p h d", d=HD)
                    ins = act.activation(dst, src.unsqueeze(2).broadcast_to((P, HH, 2, HD)), ACT.Copy,
                                         scale=qk_rstd[:, t, s:s + 1])
                ins.then_inc(qk_hi.sem, 1)

            def transposed_out(row, half, t):
                at = slice(t * P, (t + 1) * P)
                for job, dst, done in (("qT", q_t[half][:, :, at], q_t_out), ("kT", k_t[half][:, :, at], k_t_out)):
                    act.wait_ge(ring_full.sem, ring_full.at(row, JOB[(job, half, t)]))
                    act.activation(dst, bank((job, half, t))[:, :].rearrange("p (a c) -> p a c", a=PAIRS), ACT.Copy)\
                        .then_inc(done.sem, 1)

            def exp_unit(row, unit):
                nq = queries(unit)
                for a in range(2):
                    act.wait_ge(ring_full.sem, ring_full.at(row, JOB[("st", unit, a)]))
                    if a == 0:
                        if unit >= 2:
                            p_lo_wait(act, row, unit - 2)
                        elif row.before().exists():
                            p_lo_wait(act, row.before(), NU - 2 + unit)
                    act.activation(probs[:, unit % 2, 2 * a:2 * a + 2, 0:nq],
                                   bank(("st", unit, a))[:, :].rearrange("p (r c) -> p r c", r=2)[:, :, 0:nq],
                                   ACT.Exp).then_inc(exped.sem, 1)

            def high_probs(row, unit):
                nq = queries(unit)
                act.wait_ge(exped.sem, exped.at(row, 2 * unit + 1))
                if unit >= 2:
                    act.wait_ge(ring_full.sem, ring_full.at(row, JOB[("pv", unit - 2)]))
                act.activation(p_hi[:, unit % 3, :, 0:nq], probs[:, unit % 2, :, 0:nq], ACT.Copy)\
                    .then_inc(p_hi_out.sem, 1)

            def split_piece(place):
                n, odd = divmod(place, 2)
                if odd or n >= PIECES:
                    return
                act.wait_ge(piece_loaded[n % 2], 16 * (n // 2 + 1))
                act.activation(w_hi[:, n * PIECE:(n + 1) * PIECE], raw_ffn[:, n % 2, :],
                               ACT.Copy).then_inc(piece_hi, 1)
                if 1 <= n < PIECES - 1:
                    act.wait_ge(piece_lo, n)
                    load_piece(n + 1)

            def experts(f, place, pairs=pairs):
                c, odd = divmod(place, 2)
                if odd:
                    return
                if c < NC:
                    act.wait_ge(ffn_full.sem, ffn_full.at(f, 3 * c + (c == 0)))
                    if c >= 2:
                        act.wait_ge(weighed.sem, weighed.at(f, c - 2))
                    else:
                        act.wait_ge(weighed.sem, weighed.at(f.before(), last_on(2, c, NC)))
                    act.activation(w_spread[:, c % 2, :], pairs[c % 2][0][:, :], ACT.Copy).then_inc(w_out.sem, 1)
                if 1 <= c <= NC:
                    m = c - 1
                    act.wait_ge(weighed.sem, weighed.at(f, m))
                    y_before(act, f, m)
                    act.activation(g_hi[:, m % 2, :], gated[:, m % 2, :], ACT.Copy).then_inc(g_hi_out.sem, 1)
                if c < NC:
                    act.wait_ge(ffn_full.sem, ffn_full.at(f, 3 * c + 2))
                    if c >= 2:
                        act.wait_ge(g_lo_out.sem, g_lo_out.at(f, c - 2))
                    else:
                        act.wait_ge(g_lo_out.sem, g_lo_out.at(f.before(), last_on(2, c, NC)))
                    act.activation(gated[:, c % 2, :], pairs[c % 2][0][:, :], ACT.Tanh, scale=0.5).then_inc(tanh_out.sem, 1)

            modulate(Row(0), 0)
            for t in range(T):
                early_tile(Row(0), t)
                v_middle(Row(0), t)
            attention(Row(0), split_piece, lambda stage: None)
            with act.Fori(0, B - 2) as r:
                f = Row(r, 0)
                attention(Row(r, 1), lambda place: experts(f, place), lambda stage: router(f, stage))
            f = Row(B - 2)
            attention(Row(B - 1), lambda place: experts(f, place), lambda stage: router(f, stage))
            for stage in range(3):
                router(Row(B - 1), stage)
            for place in range(PLACES):
                experts(Row(B - 1), place, spare_pairs)

        @block.vector
        def _(dve):
            steps = 0

            def start(instruction):
                nonlocal steps
                steps += 1
                instruction.then_inc(start_step, 1)
                dve.wait_ge(start_step, steps)

            def counted(event, row, count):
                done = 0

                def step(instruction):
                    nonlocal done
                    assert done < count
                    instruction.then_inc(event.sem, 1)
                    dve.wait_ge(event.sem, event.at(row, done))
                    done += 1
                return step

            def ln_stats(row, which, src, step):
                for t in range(T):
                    ins = dve.bn_stats(stats[:, t, :], src[:, t, :])
                step(ins)
                dve.nop(nofuse=True)
                for t in range(T):
                    ins = dve.bn_aggr(moments[:, t, :], stats[:, t, :])
                ins.then_inc(stats_ready[which].sem, 1)

            def ln_normalise(row, which, src):
                dve.wait_ge(stats_ready[which].sem, stats_ready[which].at(row, 0))
                dve.wait_ge(rstd_ready[which].sem, rstd_ready[which].at(row, 0))
                for t in range(T):
                    ins = dve.tensor_scalar(xn[:, t, :], src[:, t, :], moments[:, t, 0:1], rstd[:, t:t + 1],
                                            ALU.subtract, ALU.mult)
                ins.then_inc(normed[which].sem, 1)

            dve.wait_ge(silu_exp, 1)
            start(dve.tensor_scalar(ct_tmp[:, :, :], ct_tmp[:, :, :], 1.0, None, ALU.add))
            start(dve.reciprocal(ct_tmp[:, :, :], ct_tmp[:, :, :]))
            dve.tensor_tensor(ct[:, :, :], ct[:, :, :], ct_tmp[:, :, :], ALU.mult).then_inc(silu_done, 1)
            early = counted(early_step, Row(0), EARLY_STEPS)
            dve.wait_ge(x_early_loaded.sem, x_early_loaded.at(Row(0), 0))
            ln_stats(Row(0), 0, x_early, early)
            for parts in (q_parts, k_parts):
                dve.memset(parts[:, :, :, 3 * HD:64].bitcast(F32), 0.0)
            dve.memset(v_parts[:, :, :, 3 * HD:V3], 1.0)
            dve.wait_ge(consts_loaded, 64)
            start(dve.tensor_scalar(norm_w[:, 0:D], norm_w[:, 0:D], HD ** -0.5, None, ALU.mult))
            start(dve.memset(k_parts[:, :, :, 3 * HD:3 * HD + 1].bitcast(F32), 1.0))
            dve.wait_ge(w_loaded, 48)
            for raw, w in ((raw_qkv, wqkv), (raw_o, wo), (wg_raw, wg)):
                start(dve.tensor_copy(w[:, 0, :, :], raw[:, :, :]))
                ins = dve.tensor_tensor(w[:, 1, :, :], raw[:, :, :], w[:, 0, :, :].bitcast(F32), ALU.subtract)
            ins.then_inc(weights_split, 1)
            ln_normalise(Row(0), 0, x_early)
            dve.wait_ge(mod_full, 1)
            start(dve.tensor_copy(cmod[:, :, :, :], ring[0][:, 0:4 * KD * B].rearrange("p (m k b) -> p m k b", m=4, k=KD)))
            for m in (0, 2):
                ins = dve.tensor_scalar(cmod[:, m, :, :], cmod[:, m, :, :], 1.0, None, ALU.add)
            ins.then_inc(mod_out, 1)
            g = ring[1][0:B, :]
            dve.tensor_scalar(gate_rows[1], g, 0.0, None, ALU.is_ge)
            dve.tensor_scalar(gate_rows[2], g, 0.25, None, ALU.max)
            start(dve.tensor_scalar(gate_rows[0], g, -0.25, None, ALU.min))
            start(dve.tensor_tensor(gate_rows[2], gate_rows[2], gate_rows[0], ALU.subtract))
            start(dve.tensor_tensor(gate_rows[1], gate_rows[1], gate_rows[2], ALU.mult))
            dve.tensor_tensor(gate_rows[0], gate_rows[0], gate_rows[1], ALU.add).then_inc(mod_out, 1)

            def ln_split(row, which):
                h = (h1, h2)[which]
                for k in range(KD):
                    dve.wait_ge(modulated[which].sem, modulated[which].at(row, k))
                    dve.tensor_tensor(h[:, 1, k, :], h_f32[:, :], h[:, 0, k, :].bitcast(F32), ALU.subtract)\
                        .then_inc(h_split[which].sem, 1)

            def early_tile(row, t, step):
                w2 = weighted[:, t % 2, :]
                dve.wait_ge(squares.sem, squares.at(row, t))
                if t >= 2:
                    dve.wait_ge(sin_done.sem, sin_done.at(row, t - 2))
                dve.tensor_tensor(w2, bank(("qk", t))[:, :], norm_w[:, :], ALU.mult).then_inc(qk_weighted.sem, 1)
                dve.wait_ge(v_hi.sem, v_hi.at(row, t))
                if t >= 2:
                    dve.wait_ge(v_done.sem, v_done.at(row, t - 2))
                dve.tensor_tensor(v_rest[:, t % 2, :, :], bank(("v", t))[:, 0:D].rearrange("p (h d) -> p h d", d=HD),
                                  v_parts[:, t, :, 0:HD], ALU.subtract).then_inc(v_sub.sem, 1)
                dve.wait_ge(qk_weighted.sem, qk_weighted.at(row, t))
                step(dve.tensor_tensor(rot[:, :, t, :].rearrange("p b (h d) -> p b h d", d=HD // 2),
                                       w2.rearrange("p (b h d) -> p b h d", d=HD // 2, b=4),
                                       cos[:, t, :].unsqueeze(1).unsqueeze(1).broadcast_to((P, 4, NH, HD // 2)), ALU.mult))

            def early_turn(row, t):
                dve.wait_ge(sin_done.sem, sin_done.at(row, t))
                a, z = (rot[:, :, t, :].rearrange("p b (h s d) -> p b h s d", s=2, d=HD // 2)[:, :, :, s, :]
                        for s in range(2))
                sa, sz = (by_sin[:, t % 2, :].rearrange("p (b h s d) -> p b h s d", b=4, s=2, d=HD // 2)[:, :, :, s, :]
                          for s in range(2))
                dve.tensor_tensor(a, a, sz, ALU.subtract)
                dve.tensor_tensor(z, z, sa, ALU.add).then_inc(rotated.sem, 1)

            def residual(row, t):
                if t == 0:
                    dve.wait_ge(x_loaded.sem, x_loaded.at(row, 1))
                dve.wait_ge(ring_full.sem, ring_full.at(row, JOB[("op", t)]))
                dve.tensor_tensor(gated_proj[:, t % 2, :], bank(("op", t))[:, 0:D], ga[:, :], ALU.mult)\
                    .then_inc(proj_read.sem, 1)
                dve.wait_ge(proj_read.sem, proj_read.at(row, t))
                dve.tensor_tensor(x_sb[:, t, :], gated_proj[:, t % 2, :], x_sb[:, t, :], ALU.add)\
                    .then_inc(resid.sem, 1)

            def attention(row, place, routing, finish):
                next_row = row.after()
                early, late = counted(early_step, next_row, EARLY_STEPS), counted(late_step, row, LATE_STEPS)
                low_qk(row, 0, 0)
                low_qk(row, 0, 1)
                for t in range(T):
                    run(place, ("tile", t, 0))
                    if t >= 1:
                        maxima(row, 0, t - 1)
                    if t == 0:
                        routing()
                    low_qk(row, *divmod(t + 2, T))
                    run(place, ("tile", t, 1))
                maxima(row, 0, T - 1)
                low_qk(row, 1, 2)
                maxima(row, 1, 0)
                low_qk(row, 1, 3)
                run(place, ("gap",))
                for u in range(END):
                    if PV_LAG <= u < NU + PV_LAG:
                        attend(row, u - PV_LAG)
                    if u in MAX_AT:
                        maxima(row, 1, MAX_AT[u])
                    run(place, ("unit", u))
                    if next_row.exists():
                        if u == STATS_AT:
                            dve.wait_ge(x_early_loaded.sem, x_early_loaded.at(next_row, 0))
                            ln_stats(next_row, 0, x_early, early)
                        if u == NORM_AT:
                            ln_normalise(next_row, 0, x_early)
                    if u < NU and u % UNITS not in ON_POOL:
                        low_probs(dve, row, u, p_lo_dve)
                    if 0 <= u - OUT_AT - 2 < T:
                        residual(row, u - OUT_AT - 2)
                    if u - OUT_AT - 2 == T - 1:
                        dve.wait_ge(resid.sem, resid.at(row, T - 1))
                        ln_stats(row, 1, x_sb, late)
                    if 0 <= u - OUT_AT < T:
                        t = u - OUT_AT
                        dve.wait_ge(attn_t_hi.sem, attn_t_hi.at(row, t))
                        dve.tensor_tensor(attn_t[:, t % 2, 1, :, :],
                                          bank(("oT", t))[:, 0:D].rearrange("p (k c) -> p k c", k=KD),
                                          attn_t[:, t % 2, 0, :, :].bitcast(F32), ALU.subtract).then_inc(attn_t_lo.sem, 1)
                    if next_row.exists() and 0 <= u - NU - 3 < T:
                        early_tile(next_row, u - NU - 3, early)
                    if u == NU and next_row.exists():
                        ln_split(next_row, 0)
                    if next_row.exists() and 0 <= u - NU - 4 < T:
                        early_turn(next_row, u - NU - 4)
                ln_normalise(row, 1, x_sb)
                if next_row.exists():
                    early_turn(next_row, T - 1)
                run(place, ("end", 0))
                ln_split(row, 1)
                run(place, ("end", 1))
                finish()

            def low_qk(row, half, t):
                slot = (half * T + t) % 2
                dve.wait_ge(qk_hi.sem, qk_hi.at(row, half * T + t))
                for s, parts, at in ((0, q_parts, 2), (1, k_parts, 1)):
                    src = rot[:, 2 * s + half, t, :].rearrange("p (h d) -> p h d", d=HD)
                    ins = dve.scalar_tensor_tensor(
                        out=parts[:, slot, :, at * HD:(at + 1) * HD], in0=src, scalar=qk_rstd[:, t, s:s + 1],
                        in1=parts[:, slot, :, 0:HD].bitcast(F32), op0=ALU.mult, op1=ALU.subtract)
                ins.then_inc(qk_lo.sem, 1)

            def maxima(row, half, t):
                nk = 2 * P if t else P
                for u in range(2 * G):
                    g, a = divmod(u, 2)
                    dve.wait_ge(ring_full.sem, ring_full.at(row, JOB[("max", half, t, u)]))
                    dve.nop(nofuse=True)
                    for r in range(2):
                        m = PAIRS * a + 2 * g + r
                        scores = bank(("max", half, t, u))[:, 2 * P * r:2 * P * r + nk]
                        ins = dve.tensor_tensor_reduce(scores, scores, band[:, 2 * P - nk:2 * P], 1.0, -3e38, ALU.add,
                                                       ALU.max, row_max[:, half, t, m:m + 1])
                    ins.then_inc(maxed.sem, 1)

            def attend(row, unit):
                t, slot = unit % T, unit % 2
                dve.wait_ge(ring_full.sem, ring_full.at(row, JOB[("pv", unit)]))
                sums = bank(("pv", unit))[:, 0:4 * V3].rearrange("p (h c) -> p h c", c=V3)
                dve.reciprocal(pv_rden[:, slot, :], sums[:, :, V3 - 1])
                dve.tensor_reduce(pv_sum[:, slot, :, :], sums[:, :, 0:3 * HD].rearrange("p h (s d) -> p h d s", s=3),
                                  AX_X, ALU.add).then_inc(pv_read.sem, 1)
                dve.wait_ge(pv_read.sem, pv_read.at(row, unit))
                h = unit // T * 4
                dve.tensor_tensor(attn[:, t, h:h + 4, :], pv_sum[:, slot, :, :],
                                  pv_rden[:, slot, :].unsqueeze(2).broadcast_to((P, 4, HD)), ALU.mult).then_inc(attn_out.sem, 1)

            def router(f):
                row, step = f, counted(route_step, f, ROUTE_STEPS)
                dve.wait_ge(router_full.sem, router_full.at(row, 1))
                dve.tensor_copy(logits[:, :, :], ps_a[:, 0:T * E].rearrange("p (t e) -> p t e", e=E))\
                    .then_inc(logits_out.sem, 1)
                dve.wait_ge(logits_out.sem, logits_out.at(row, 0))
                step(dve.tensor_reduce(top1[:, :], logits[:, :, :], AX_X, ALU.max))
                dve.tensor_tensor(shifted[:, :, :], logits[:, :, :], top1[:, :].unsqueeze(2).broadcast_to((P, T, E)),
                                  ALU.subtract).then_inc(shifted_out.sem, 1)
                other = logits[:, :, :].unsqueeze(2).broadcast_to((P, T, E, E))
                own = logits[:, :, :].unsqueeze(3).broadcast_to((P, T, E, E))
                dve.tensor_tensor(beats[:, :, :, :], other, own, ALU.is_gt)
                step(dve.tensor_tensor(ties[:, :, :, :], other, own, ALU.is_equal))
                step(dve.tensor_tensor(ties[:, :, :, :], ties[:, :, :, :],
                                       earlier[:, :, :].unsqueeze(1).broadcast_to((P, T, E, E)), ALU.mult))
                step(dve.tensor_tensor(beats[:, :, :, :], beats[:, :, :, :], ties[:, :, :, :], ALU.add))
                step(dve.tensor_reduce(rank[:, :, :], beats[:, :, :, :], AX_X, ALU.add))
                step(dve.tensor_scalar(rank[:, :, :], rank[:, :, :], 1.5, None, ALU.is_lt))
                dve.wait_ge(exps_out.sem, exps_out.at(row, 0))
                step(dve.tensor_tensor(route[:, :, :], exps[:, :, :], rank[:, :, :], ALU.mult))
                step(dve.tensor_reduce(route_sum[:, :], route[:, :, :], AX_X, ALU.add))
                step(dve.reciprocal(route_sum[:, :], route_sum[:, :]))
                step(dve.tensor_tensor(route[:, :, :], route[:, :, :],
                                       route_sum[:, :].unsqueeze(2).broadcast_to((P, T, E)), ALU.mult))
                step(dve.tensor_copy(route_parts[:, :, 0, :], route[:, :, :]))
                dve.tensor_tensor(route_parts[:, :, 1, :], route[:, :, :], route_parts[:, :, 0, :].bitcast(F32),
                                  ALU.subtract).then_inc(route_out.sem, 1)

            def experts(f, place, pairs=pairs):
                c, odd = divmod(place, 2)
                if not odd or c >= NC:
                    return
                g = gated[:, c % 2, :]
                dve.wait_ge(tanh_out.sem, tanh_out.at(f, c))
                dve.scalar_tensor_tensor(out=g, in0=g, scalar=1.0, in1=pairs[c % 2][0][:, :], op0=ALU.add, op1=ALU.mult)\
                    .then_inc(a_read.sem, 1)
                dve.wait_ge(a_read.sem, a_read.at(f, c))
                dve.wait_ge(ffn_full.sem, ffn_full.at(f, 3 * c + (c > 0)))
                dve.tensor_tensor(g, g, pairs[c % 2][1][:, :], ALU.mult).then_inc(b_read.sem, 1)

            def finish(f):
                dve.wait_ge(y_done.sem, y_done.at(f, NC - 1))
                dve.wait_ge(gb_loaded.sem, gb_loaded.at(f, 0))
                for b in range(2):
                    dve.tensor_tensor(gated_y[b], ps_y[b][:, :].rearrange("p (t c) -> p t c", t=2),
                                      gb[:, :].unsqueeze(1).broadcast_to((P, 2, D)), ALU.mult).then_inc(y_read.sem, 1)

            ln_split(Row(0), 0)
            for t in range(T):
                early_tile(Row(0), t, early)
                if t >= 1:
                    early_turn(Row(0), t - 1)
            early_turn(Row(0), T - 1)
            dve.wait_ge(constants, 1)
            attention(Row(0), lambda place: None, lambda: None, lambda: None)
            for read in (a_read, b_read, y_read):
                read.grant(dve)
            with dve.Fori(0, B - 2) as r:
                f = Row(r, 0)
                attention(Row(r, 1), lambda place: experts(f, place), lambda: router(f), lambda: finish(f))
            f = Row(B - 2)
            attention(Row(B - 1), lambda place: experts(f, place), lambda: router(f), lambda: finish(f))
            router(Row(B - 1))
            for place in range(PLACES):
                experts(Row(B - 1), place, spare_pairs)
            finish(Row(B - 1))

        @block.tensor
        def _(pe):
            pe.wait_ge(mod_loaded, 16 * KD)
            pe.wait_ge(silu_done, 1)
            for m, chunk in enumerate((1, 0, 4, 3)):
                for k in range(KD):
                    at = (m * KD + k) * B
                    for j in range(KD):
                        c = chunk * D + k * P
                        pe.matmul(ring[0][:, at:at + B], raw_mod[j][:, c:c + P], ct[:, j, :],
                                  start=(j == 0), stop=(j == KD - 1))
            for m, chunk in enumerate((2, 5)):
                for j in range(KD):
                    ins = pe.matmul(ring[1][0:B, m * D:(m + 1) * D], ct[:, j, :],
                                    raw_mod[j][:, chunk * D:(chunk + 1) * D], start=(j == 0), stop=(j == KD - 1))
            ins.then_inc(mod_full, 1)
            pe.wait_ge(ident_ready, 1)
            pe.wait_ge(weights_split, 1)
            pe.wait_ge(mod_out, 2)

            SPLIT = ((0, 0), (0, 1), (1, 0))

            def products(dst, stationary, moving, signal=None):
                for k in range(KD):
                    for n, (s, m) in enumerate(SPLIT):
                        ins = pe.matmul(dst, stationary(s, k), moving(m, k), start=(k == 0 and n == 0),
                                        stop=(k == KD - 1 and n == len(SPLIT) - 1))
                return ins

            def layer_norm_transposes(row, which):
                pe.wait_ge(normed[which].sem, normed[which].at(row, 0))
                now = row if which else row.before()
                for k in range(KD):
                    job = ("ln", k) if which else ("early ln", k)
                    bank_free(pe, now, job)
                    for t in range(T):
                        ins = pe.transpose(bank(job)[:, t * P:(t + 1) * P], xn[:, t, k * P:(k + 1) * P], ident[:, :])
                    ins.then_inc((ring_full if which else early_full).sem, 1)

            def project(row, t):
                if t == 0:
                    pe.wait_ge(h_split[0].sem, h_split[0].at(row, KD - 1))
                tokens = slice(t * P, (t + 1) * P)
                for job, a, z in ((("qk", t), 0, 2 * D), (("v", t), 2 * D, 3 * D)):
                    bank_free(pe, row.before(), job)
                    products(bank(job)[:, 0:z - a], lambda s, k: h1[:, s, k, tokens],
                             lambda m, k: wqkv[:, m, k, a:z]).then_inc(early_full.sem, 1)

            def turn_maxima(row, half):
                bank_free(pe, row, ("mT", half))
                pe.wait_ge(maxed.sem, maxed.at(row, (half * T + T) * 2 * G - 1))
                for t in range(T):
                    ins = pe.transpose(bank(("mT", half))[0:HH, t * P:(t + 1) * P], row_max[:, half, t, :], ident[:, :])
                ins.then_inc(ring_full.sem, 1)

            def attention(row, place, routing):
                next_row = row.after()
                routing(0)
                for t in range(T):
                    transpose_qk(row, 0, t)
                    if t == 0:
                        routing(1)
                    run(place, ("tile", t, 0))
                    if t >= 1:
                        query_scores(row, 0, t - 1)
                    run(place, ("tile", t, 1))
                query_scores(row, 0, T - 1)
                transpose_qk(row, 1, 0)
                turn_maxima(row, 0)
                transpose_qk(row, 1, 1)
                query_scores(row, 1, 0)
                run(place, ("gap",))
                for u in range(END):
                    if u < NU:
                        if u % UNITS == 0:
                            pe.wait_ge(max_rows_set.sem, max_rows_set.at(row, 2 * (u // UNITS) + 1))
                        for a in range(2):
                            key_scores(row, u, a)
                    if PV_LAG <= u < NU + PV_LAG:
                        probs_times_v(row, u - PV_LAG)
                    if u in MAX_AT:
                        query_scores(row, 1, MAX_AT[u])
                    if u in TURN_AT:
                        transpose_qk(row, 1, TURN_AT[u])
                    run(place, ("unit", u))
                    if u == MAX_ROWS_AT:
                        turn_maxima(row, 1)
                    if 0 <= u - OUT_AT - 2 < T:
                        job, slot = ("op", u - OUT_AT - 2), u % 2
                        pe.wait_ge(attn_t_lo.sem, attn_t_lo.at(row, u - OUT_AT - 2))
                        bank_free(pe, row, job)
                        products(bank(job)[:, 0:D], lambda s, k: attn_t[:, slot, s, k, :],
                                 lambda m, k: wo[:, m, k, :]).then_inc(ring_full.sem, 1)
                    if 0 <= u - OUT_AT < T:
                        t = u - OUT_AT
                        job = ("oT", t)
                        pe.wait_ge(attn_out.sem, attn_out.at(row, NU - T + t))
                        bank_free(pe, row, job)
                        for k in range(KD):
                            ins = pe.transpose(bank(job)[:, k * P:(k + 1) * P],
                                               attn[:, t, k * HH:(k + 1) * HH, :].rearrange("p h d -> p (h d)"), ident[:, :])
                        ins.then_inc(ring_full.sem, 1)
                    if next_row.exists():
                        if u == NU:
                            layer_norm_transposes(next_row, 0)
                        if 0 <= u - NU - 3 < T:
                            project(next_row, u - NU - 3)
                run(place, ("end", 0))
                layer_norm_transposes(row, 1)
                run(place, ("end", 1))

            def router(f, stage):
                if stage == 0:
                    pe.wait_ge(h_split[1].sem, h_split[1].at(f, KD - 1))
                    pe.wait_ge(a_read.sem, a_read.at(f.before(), NC - 1))
                    products(ps_a[0:E, :], lambda s, k: wg[:, s, k, :], lambda m, k: h2[:, m, k, :])\
                        .then_inc(router_full.sem, 1)
                if stage == 1:
                    pe.wait_ge(logits_t_out.sem, logits_t_out.at(f, 0))
                    pe.nop(nofuse=True)
                    for t in range(T):
                        ins = pe.transpose(ps_a[:, t * E:(t + 1) * E], logits_t[:, t * P:(t + 1) * P], ident[0:E, 0:E])
                    ins.then_inc(router_full.sem, 1)
                if stage == 2:
                    pe.wait_ge(route_out.sem, route_out.at(f, 0))
                    for t in range(T):
                        ins = pe.transpose(ps_a[0:2 * E, t * P:(t + 1) * P],
                                           route_parts[:, t, :, :].rearrange("p s e -> p (s e)").bitcast(F32), ident[:, :])
                    ins.then_inc(router_full.sem, 1)

            def transpose_qk(row, half, t):
                slot = (half * T + t) % 2
                pe.wait_ge(qk_lo.sem, qk_lo.at(row, half * T + t))
                for job, parts in (("qT", q_parts), ("kT", k_parts)):
                    bank_free(pe, row, (job, half, t))
                    for p in range(PAIRS):
                        ins = pe.transpose(bank((job, half, t))[:, p * P:(p + 1) * P],
                                           parts[:, slot, 2 * p:2 * p + 2, :].rearrange("p h c -> p (h c)").bitcast(F32),
                                           ident[:, :])
                    ins.then_inc(ring_full.sem, 1)

            def query_scores(row, half, t):
                pe.wait_ge(k_t_out.sem, k_t_out.at(row, half * T + t))
                first = max(t - 1, 0)
                nk = (t + 1 - first) * P
                for u in range(2 * G):
                    g, a = divmod(u, 2)
                    job, rows = ("max", half, t, u), slice(64 * a, 64 * a + 64)
                    bank_free(pe, row, job)
                    for r in range(2):
                        ins = pe.matmul(bank(job)[:, 2 * P * r:2 * P * r + nk], q_t[half][rows, 2 * g + r, t * P:(t + 1) * P],
                                        k_t[half][rows, 2 * g + r, first * P:(t + 1) * P], start=True, stop=True)
                    ins.then_inc(ring_full.sem, 1)

            def key_scores(row, unit, a):
                half, n = divmod(unit, UNITS)
                (g, j), nq, rows = divmod(n, T), queries(n), slice(64 * a, 64 * a + 64)
                job = ("st", unit, a)
                bank_free(pe, row, job)
                pe.matmul(bank(job)[:, :].rearrange("p (r c) -> p r c", r=2)[:, :, 0:nq], ident_bf[:, :],
                          band_t[:, :, 0:nq], start=True, stop=False)
                for r in range(2):
                    ins = pe.matmul(bank(job)[:, 2 * P * r:2 * P * r + nq], k_t[half][rows, 2 * g + r, j * P:(j + 1) * P],
                                    q_t[half][rows, 2 * g + r, j * P:j * P + nq], start=False, stop=(r == 1))
                ins.then_inc(ring_full.sem, 1)

            def probs_times_v(row, unit):
                job, t = ("pv", unit), unit % T
                if unit == 0:
                    pe.wait_ge(v_done.sem, v_done.at(row, T - 1))
                p_lo_wait(pe, row, unit)
                bank_free(pe, row, job)
                for h in range(4):
                    r, a = divmod(h, 2)
                    todo = [(p, u, at) for u, at in ([(unit - 1, P)] if t else []) + [(unit, 0)] for p in (p_hi, p_lo)]
                    for i, (p, u, at) in enumerate(todo):
                        tile = t - (at > 0)
                        ins = pe.matmul(bank(job)[:, h * V3:(h + 1) * V3], p[:, u % 3, 2 * a + r, at:at + P],
                                        v_parts[:, tile, unit // T * 4 + h, :],
                                        start=(i == 0), stop=(i == len(todo) - 1))
                ins.then_inc(ring_full.sem, 1)

            def hidden(f, c, pairs):
                bank_a, bank_b = pairs[c % 2]
                same = c - (1 if pairs[0] == pairs[1] else 2)
                for n, dst in (((1, bank_b), (2, bank_a), (0, bank_a)) if c == 0 else
                               ((2, bank_a), (1, bank_b), (0, bank_a))):
                    if n == 2:
                        if c == 0:
                            router(f, 2)
                            pe.wait_ge(route_t_out.sem, route_t_out.at(f, 0))
                        elif same >= 0:
                            pe.wait_ge(a_read.sem, a_read.at(f, same))
                        pe.matmul(bank_a[:, :], few_rows[0:2 * E, c * P:(c + 1) * P], route_t[:, :],
                                  start=True, stop=True).then_inc(ffn_full.sem, 1)
                        continue
                    if n == 0:
                        pe.wait_ge(w_out.sem, w_out.at(f, c))
                    elif same >= 0:
                        pe.wait_ge(b_read.sem, b_read.at(f, same))
                    else:
                        pe.wait_ge(b_read.sem, b_read.at(f.before(), NC - 1))
                        if c == 0:
                            pe.wait_ge(h_short.sem, h_short.at(f, KD - 1))
                    for k in range(KD):
                        at = k * 2 * FH + n * FH + c * P
                        first, last = k == 0, k == KD - 1
                        pe.matmul(dst[:, :], w_hi[:, at:at + P], h2[:, 0, k, :], start=first, stop=False)
                        pe.matmul(dst[:, :], w_hi[:, at:at + P], h2[:, 1, k, :], start=False, stop=False)
                        ins = pe.matmul(dst[:, :], w12_lo[:, at:at + P], h2_bf[:, k, :], start=False, stop=last)
                    ins.then_inc(ffn_full.sem, 1)

            def add_to_y(f, c):
                pe.wait_ge(g_lo_out.sem, g_lo_out.at(f, c))
                if c == 0:
                    pe.wait_ge(y_read.sem, y_read.at(f.before(), 1))
                w3_hi = w_hi[:, WCOLS + c * D:WCOLS + (c + 1) * D]
                for t in range(T):
                    tokens = slice(t * P, (t + 1) * P)
                    for n, (g, w) in enumerate(((g_hi, w3_hi), (g_hi, w3_lo[:, c * D:(c + 1) * D]), (g_lo, w3_hi))):
                        ins = pe.matmul(ps_y[t // 2][:, t % 2 * D:(t % 2 + 1) * D], g[:, c % 2, tokens], w,
                                        start=(c == 0 and n == 0 and t % 2 == 0), stop=(c == NC - 1 and n == 2),
                                        skip_group_check=True)
                ins.then_inc(y_done.sem, 1)

            def experts(f, place, pairs=pairs):
                if place % 2 == 0 and place // 2 < NC:
                    hidden(f, place // 2, pairs)
                if place % 2 and place >= 5:
                    add_to_y(f, (place - 5) // 2)

            layer_norm_transposes(Row(0), 0)
            for t in range(T):
                project(Row(0), t)
            pe.wait_ge(constants, 1)
            attention(Row(0), lambda place: None, lambda stage: None)
            y_done.grant(pe)
            pe.wait_ge(piece_hi, PIECES)
            pe.wait_ge(piece_lo, PIECES)
            with pe.Fori(0, B - 2) as r:
                f = Row(r, 0)
                attention(Row(r, 1), lambda place: experts(f, place), lambda stage: router(f, stage))
            f = Row(B - 2)
            attention(Row(B - 1), lambda place: experts(f, place), lambda stage: router(f, stage))
            for stage in range(2):
                router(Row(B - 1), stage)
            for place in range(PLACES):
                experts(Row(B - 1), place, spare_pairs)


def kernel(L0_attn_hidden_states, L0_attn_w_qkv, L0_attn_q_norm_w, L0_attn_k_norm_w, L0_attn_w_o,
           L0_ffn_Wg, L0_ffn_W1, L0_ffn_W2, L0_ffn_W3, L0_c, L0_wmod):
    import concourse.bacc as bacc
    from concourse.bass_utils import run_bass_kernel_spmd

    def by_contraction(w):
        return np.ascontiguousarray(np.transpose(np.asarray(w).reshape(w.shape[0], -1, P), (2, 1, 0)))

    w12 = by_contraction(np.concatenate([np.asarray(L0_ffn_W1).reshape(FH, D), np.asarray(L0_ffn_W2).reshape(FH, D)]))
    w3 = by_contraction(np.transpose(np.asarray(L0_ffn_W3), (1, 0, 2)).reshape(D, FH))
    angles = np.arange(S, dtype=np.float32)[:, None] * (
        1.0 / 10000.0 ** (np.arange(0, HD, 2, dtype=np.float32) / np.float32(HD))).astype(np.float32)[None, :]
    rope = np.stack([np.cos(angles), np.sin(angles)]).astype(np.float32)
    arrays = {
        "x": np.ascontiguousarray(np.asarray(L0_attn_hidden_states).reshape(B, T, P, D).transpose(0, 2, 1, 3)),
        "w_qkv_t": by_contraction(L0_attn_w_qkv),
        "q_norm": np.asarray(L0_attn_q_norm_w).reshape(1, D),
        "k_norm": np.asarray(L0_attn_k_norm_w).reshape(1, D),
        "w_o_t": by_contraction(L0_attn_w_o),
        "w_g_t": by_contraction(L0_ffn_Wg),
        "w_ffn": np.concatenate([w12.reshape(P, WCOLS), w3.reshape(P, W3COLS)], axis=1),
        "c_t": by_contraction(L0_c),
        "w_mod": np.ascontiguousarray(np.asarray(L0_wmod).reshape(KD, P, 6 * D)),
        "rope": np.ascontiguousarray(rope.reshape(2, T, P, HD // 2).transpose(0, 2, 1, 3)),
    }
    nc = bacc.Bacc("TRN2", target_bir_lowering=False, num_devices=1,
                   dynamic_dma_scratch_size=1024)
    args = {n: nc.dram_tensor("in_" + n, a.shape, mybir.dt.from_np(a.dtype), kind="ExternalInput").ap()
            for n, a in arrays.items()}
    gates = nc.dram_tensor("gates", (B, 2 * D), F32).ap()
    out = nc.dram_tensor("out", (B, P, T, D), F32, kind="ExternalOutput").ap()
    build(nc, **args, gates=gates, out=out)
    r = run_bass_kernel_spmd(nc, [{"in_" + n: a for n, a in arrays.items()}], core_ids=[0])
    got = r.results[0]["out"]
    return got.transpose(0, 2, 1, 3).reshape(B, S, D)
```
